# Optimizing a Trainium2 kernel written in Bass

```python
import numpy as np
import jax
import jax.numpy as jnp

def _softmax(x, axis=-1):
    return jax.nn.softmax(x, axis=axis)

def _gelu(x):
    return jax.nn.gelu(x, approximate=True)

def _silu(x):
    return jax.nn.silu(x)

def _sigmoid(x):
    return jax.nn.sigmoid(x)

def _layernorm(x, axis=-1, eps=1e-05):
    m = jnp.mean(x, axis=axis, keepdims=True)
    v = jnp.var(x, axis=axis, keepdims=True)
    return (x - m) / jnp.sqrt(v + eps)

def _scatter_add(tgt, idx, src, axis=0):
    return tgt.at[idx].add(src)

def _segment_sum(src, seg, n):
    return jax.ops.segment_sum(src, seg, n)
kernel_name = 'mk_sandwich_d2_jaxref_r8_b2daca'

def setup_inputs(seed: int=0):
    np.random.seed(seed)
    _w = jnp.asarray

    def _L0_attn_setup():
        import jax, jax.numpy as jnp
        import numpy as np
        EPS = 1e-15
        HEAD_DIM = 32
        PAD_VAL = 1.0
        key = jax.random.key(seed)
        k1, k2, k3, k4 = jax.random.split(key, 4)
        B, N, C = (2, 512, 256)
        s = 1.0 / np.sqrt(C).astype(np.float32)
        x = jax.random.normal(k1, (B, N, C), jnp.float32)
        w_qkv = jax.random.normal(k2, (3 * C, C), jnp.float32) * s
        w_proj = jax.random.normal(k3, (C, C), jnp.float32) * s
        b_proj = jax.random.normal(k4, (C,), jnp.float32) * 0.01
        return {'x': x, 'w_qkv': w_qkv, 'w_proj': w_proj, 'b_proj': b_proj}
    _L0_attn_in = _L0_attn_setup()

    def _L0_ffn_setup():
        import jax, jax.numpy as jnp
        import numpy as np
        B, S, D, H = (4, 256, 256, 1024)

        def fwht(x):
            orig_shape = x.shape
            n = orig_shape[-1]
            x = x.reshape(-1, n)
            h = 1
            while h < n:
                xb = x.reshape(-1, n // (2 * h), 2, h)
                a = xb[:, :, 0, :]
                b = xb[:, :, 1, :]
                x = jnp.stack([a + b, a - b], axis=2).reshape(-1, n)
                h *= 2
            scale = jnp.asarray(1.0 / np.sqrt(n), dtype=x.dtype)
            return (x * scale).reshape(orig_shape)
        key = jax.random.key(seed)
        kx, k1, k2, k3 = jax.random.split(key, 4)
        x = jax.random.normal(kx, (B, S, D), dtype=jnp.float32)
        W1 = jax.random.normal(k1, (H, D), dtype=jnp.float32) * (1.0 / np.sqrt(D))
        W2 = jax.random.normal(k2, (D, H), dtype=jnp.float32) * (1.0 / np.sqrt(H))
        W3 = jax.random.normal(k3, (H, D), dtype=jnp.float32) * (1.0 / np.sqrt(D))
        return {'x': x, 'W1': W1, 'W2': W2, 'W3': W3}
    _L0_ffn_in = _L0_ffn_setup()

    def _L1_attn_setup():
        import math
        import jax, jax.numpy as jnp
        import numpy as np
        H, G = (16, 4)

        def alibi_bias(S, n_heads, dtype):
            n = 2 ** int(math.floor(math.log2(n_heads)))
            m0 = 2.0 ** (-8.0 / n)
            slopes = m0 ** np.arange(1, n + 1)
            if n < n_heads:
                m1 = 2.0 ** (-4.0 / n)
                slopes = np.concatenate([slopes, m1 ** np.arange(1, 1 + 2 * (n_heads - n), 2)])
            i = jnp.arange(S)[:, None]
            j = jnp.arange(S)[None, :]
            dist = jnp.sqrt(jnp.maximum(i - j, 0).astype(dtype))
            bias = -jnp.asarray(slopes, dtype)[:, None, None] * dist[None]
            return jnp.where((j <= i)[None], bias, jnp.asarray(-jnp.inf, dtype))
        key = jax.random.key(seed)
        ks = jax.random.split(key, 5)
        B, S, Hd = (2, 256, 256)
        D = Hd // H
        return {'x': jax.random.normal(ks[0], (B, S, Hd), jnp.float32), 'Wq': jax.random.normal(ks[1], (Hd, Hd), jnp.float32) * 0.02, 'Wk': jax.random.normal(ks[2], (G * D, Hd), jnp.float32) * 0.02, 'Wv': jax.random.normal(ks[3], (G * D, Hd), jnp.float32) * 0.02, 'Wo': jax.random.normal(ks[4], (Hd, Hd), jnp.float32) * 0.02}
    _L1_attn_in = _L1_attn_setup()

    def _L1_ffn_setup():
        import jax, jax.numpy as jnp
        import numpy as np
        B, S, H = (4, 256, 256)
        INTER = 512
        E = 8
        TOPK = 2
        SHARED_I = INTER * 2

        def moe_forward(hidden_states, router_w, w1, w2, w_gate, w_up, w_down):
            b, s, h = hidden_states.shape
            x = hidden_states.reshape(-1, h)
            T = x.shape[0]
            logits = x @ router_w
            top_logits, top_indices = jax.lax.top_k(logits, TOPK)
            scores = jax.nn.softmax(top_logits, axis=-1)
            flat_idx = top_indices.reshape(-1)
            sorted_pos = jnp.argsort(flat_idx, stable=True)
            permuted = x[sorted_pos // TOPK]
            expert_ids = flat_idx[sorted_pos]
            out = jnp.zeros((T * TOPK, h), x.dtype)
            for e in range(E):
                mask = (expert_ids == e)[:, None]
                f1 = permuted * mask @ w1[e]
                g, u = jnp.split(f1, 2, axis=-1)
                act = jax.nn.silu(g) * u
                out = out + jnp.where(mask, act @ w2[e], 0.0)
            unperm = jnp.zeros_like(out).at[sorted_pos].set(out)
            combined = (unperm.reshape(T, TOPK, h) * scores[..., None]).sum(axis=1)
            shared = jax.nn.silu(x @ w_gate) * (x @ w_up) @ w_down
            return (combined + shared).reshape(b, s, h)
        key = jax.random.key(seed)
        ks = jax.random.split(key, 7)
        s = 0.02
        return {'hidden_states': jax.random.normal(ks[0], (B, S, H), jnp.float32), 'router_w': jax.random.normal(ks[1], (H, E), jnp.float32) * s, 'w1': jax.random.normal(ks[2], (E, H, 2 * INTER), jnp.float32) * s, 'w2': jax.random.normal(ks[3], (E, INTER, H), jnp.float32) * s, 'w_gate': jax.random.normal(ks[4], (H, SHARED_I), jnp.float32) * s, 'w_up': jax.random.normal(ks[5], (H, SHARED_I), jnp.float32) * s, 'w_down': jax.random.normal(ks[6], (SHARED_I, H), jnp.float32) * s}
    _L1_ffn_in = _L1_ffn_setup()
    _d = {'L0_attn_x': _L0_attn_in['x'], 'L0_attn_w_qkv': _L0_attn_in['w_qkv'], 'L0_attn_w_proj': _L0_attn_in['w_proj'], 'L0_attn_b_proj': _L0_attn_in['b_proj'], 'L0_ffn_W1': _L0_ffn_in['W1'], 'L0_ffn_W2': _L0_ffn_in['W2'], 'L0_ffn_W3': _L0_ffn_in['W3'], 'L1_attn_Wq': _L1_attn_in['Wq'], 'L1_attn_Wk': _L1_attn_in['Wk'], 'L1_attn_Wv': _L1_attn_in['Wv'], 'L1_attn_Wo': _L1_attn_in['Wo'], 'L1_ffn_router_w': _L1_ffn_in['router_w'], 'L1_ffn_w1': _L1_ffn_in['w1'], 'L1_ffn_w2': _L1_ffn_in['w2'], 'L1_ffn_w_gate': _L1_ffn_in['w_gate'], 'L1_ffn_w_up': _L1_ffn_in['w_up'], 'L1_ffn_w_down': _L1_ffn_in['w_down']}
    _x0 = _d['L0_attn_x']
    _d['L0_attn_x'] = jax.random.normal(jax.random.fold_in(jax.random.key(seed), 1), (4, 512, 256), dtype=_x0.dtype)
    del _x0
    return _d

def reference(L0_attn_x, L0_attn_w_qkv, L0_attn_w_proj, L0_attn_b_proj, L0_ffn_W1, L0_ffn_W2, L0_ffn_W3, L1_attn_Wq, L1_attn_Wk, L1_attn_Wv, L1_attn_Wo, L1_ffn_router_w, L1_ffn_w1, L1_ffn_w2, L1_ffn_w_gate, L1_ffn_w_up, L1_ffn_w_down):

    def _L0_attn_ref(x, w_qkv, w_proj, b_proj):
        import jax, jax.numpy as jnp
        import numpy as np
        EPS = 1e-15
        HEAD_DIM = 32
        PAD_VAL = 1.0
        B, N, C = x.shape
        d = HEAD_DIM
        h = C // d
        qkv = (x @ w_qkv.T).reshape(B, N, 3, C)
        q, k, v = (qkv[:, :, 0], qkv[:, :, 1], qkv[:, :, 2])

        def to_heads(t):
            return t.reshape(B, N, h, d).transpose(0, 2, 3, 1)
        q = jax.nn.relu(to_heads(q))
        k = jax.nn.relu(to_heads(k))
        v = to_heads(v)
        v_pad = jnp.pad(v, ((0, 0), (0, 0), (0, 1), (0, 0)), constant_values=PAD_VAL)
        vk = jnp.einsum('bhen,bhdn->bhed', v_pad, k)
        out = jnp.einsum('bhed,bhdn->bhen', vk, q)
        out = out[:, :, :-1] / (out[:, :, -1:] + EPS)
        out = out.reshape(B, C, N).transpose(0, 2, 1)
        return out @ w_proj.T + b_proj

    def _L0_ffn_ref(x, W1, W2, W3):
        import jax, jax.numpy as jnp
        import numpy as np
        B, S, D, H = (4, 256, 256, 1024)

        def fwht(x):
            orig_shape = x.shape
            n = orig_shape[-1]
            x = x.reshape(-1, n)
            h = 1
            while h < n:
                xb = x.reshape(-1, n // (2 * h), 2, h)
                a = xb[:, :, 0, :]
                b = xb[:, :, 1, :]
                x = jnp.stack([a + b, a - b], axis=2).reshape(-1, n)
                h *= 2
            scale = jnp.asarray(1.0 / np.sqrt(n), dtype=x.dtype)
            return (x * scale).reshape(orig_shape)
        up_gate = jnp.einsum('bsd,hd->bsh', x, W1)
        up_lin = jnp.einsum('bsd,hd->bsh', x, W3)
        hidden = jax.nn.silu(up_gate) * up_lin
        hidden = fwht(hidden)
        out = jnp.einsum('bsh,dh->bsd', hidden, W2)
        return out

    def _L1_attn_ref(x, Wq, Wk, Wv, Wo):
        import math
        import jax, jax.numpy as jnp
        import numpy as np
        H, G = (16, 4)

        def alibi_bias(S, n_heads, dtype):
            n = 2 ** int(math.floor(math.log2(n_heads)))
            m0 = 2.0 ** (-8.0 / n)
            slopes = m0 ** np.arange(1, n + 1)
            if n < n_heads:
                m1 = 2.0 ** (-4.0 / n)
                slopes = np.concatenate([slopes, m1 ** np.arange(1, 1 + 2 * (n_heads - n), 2)])
            i = jnp.arange(S)[:, None]
            j = jnp.arange(S)[None, :]
            dist = jnp.sqrt(jnp.maximum(i - j, 0).astype(dtype))
            bias = -jnp.asarray(slopes, dtype)[:, None, None] * dist[None]
            return jnp.where((j <= i)[None], bias, jnp.asarray(-jnp.inf, dtype))
        B, S, Hd = x.shape
        D = Hd // H
        rep = H // G
        q = (x @ Wq.T).reshape(B, S, G, rep, D)
        k = (x @ Wk.T).reshape(B, S, G, D)
        v = (x @ Wv.T).reshape(B, S, G, D)
        scale = 1.0 / math.sqrt(D)
        bias = alibi_bias(S, H, x.dtype).reshape(G, rep, S, S)
        scores = jnp.einsum('bqgrd,bkgd->bgrqk', q, k) * scale + bias
        attn = jax.nn.softmax(scores, axis=-1)
        o = jnp.einsum('bgrqk,bkgd->bqgrd', attn, v).reshape(B, S, Hd)
        return o @ Wo.T

    def _L1_ffn_ref(hidden_states, router_w, w1, w2, w_gate, w_up, w_down):
        import jax, jax.numpy as jnp
        import numpy as np
        B, S, H = (4, 256, 256)
        INTER = 512
        E = 8
        TOPK = 2
        SHARED_I = INTER * 2

        def moe_forward(hidden_states, router_w, w1, w2, w_gate, w_up, w_down):
            b, s, h = hidden_states.shape
            x = hidden_states.reshape(-1, h)
            T = x.shape[0]
            logits = x @ router_w
            top_logits, top_indices = jax.lax.top_k(logits, TOPK)
            scores = jax.nn.softmax(top_logits, axis=-1)
            flat_idx = top_indices.reshape(-1)
            sorted_pos = jnp.argsort(flat_idx, stable=True)
            permuted = x[sorted_pos // TOPK]
            expert_ids = flat_idx[sorted_pos]
            out = jnp.zeros((T * TOPK, h), x.dtype)
            for e in range(E):
                mask = (expert_ids == e)[:, None]
                f1 = permuted * mask @ w1[e]
                g, u = jnp.split(f1, 2, axis=-1)
                act = jax.nn.silu(g) * u
                out = out + jnp.where(mask, act @ w2[e], 0.0)
            unperm = jnp.zeros_like(out).at[sorted_pos].set(out)
            combined = (unperm.reshape(T, TOPK, h) * scores[..., None]).sum(axis=1)
            shared = jax.nn.silu(x @ w_gate) * (x @ w_up) @ w_down
            return (combined + shared).reshape(b, s, h)
        return moe_forward(hidden_states, router_w, w1, w2, w_gate, w_up, w_down)
    x = L0_attn_x
    x = x + _layernorm(_L0_attn_ref(_layernorm(x, axis=-1), L0_attn_w_qkv, L0_attn_w_proj, L0_attn_b_proj), axis=-1)
    x = x + _layernorm(_L0_ffn_ref(_layernorm(x, axis=-1), L0_ffn_W1, L0_ffn_W2, L0_ffn_W3), axis=-1)
    x = x + _layernorm(_L1_attn_ref(_layernorm(x, axis=-1), L1_attn_Wq, L1_attn_Wk, L1_attn_Wv, L1_attn_Wo), axis=-1)
    x = x + _layernorm(_L1_ffn_ref(_layernorm(x, axis=-1), L1_ffn_router_w, L1_ffn_w1, L1_ffn_w2, L1_ffn_w_gate, L1_ffn_w_up, L1_ffn_w_down), axis=-1)
    return x

_drawn_inputs = setup_inputs


def setup_inputs(seed=0):
    import zlib

    import numpy as np

    out = dict(_drawn_inputs(seed))
    spreads = {}
    factors = {}
    for name, (base, spread) in spreads.items():
        noise = np.random.default_rng([zlib.crc32(name.encode()), seed]).standard_normal(out[name].shape)
        drawn = base * np.exp(spread * noise) if base else spread * noise
        out[name] = jnp.asarray(drawn.astype(out[name].dtype))
    for name, factor in factors.items():
        out[name] = (out[name] * factor).astype(out[name].dtype)
    return out
```

```python
from contextlib import ExitStack

import concourse.bass as bass
from concourse import mybir

F32 = mybir.dt.float32
F32R = mybir.dt.float32r
BF16 = mybir.dt.bfloat16
I32 = mybir.dt.int32
ALU = mybir.AluOpType
ACT = mybir.ActivationFunctionType
AX = mybir.AxisListType.X
ds = bass.ds

P = 128
B, S, D = 4, 512, 256
NT = S // P
TILES = B * NT
DC = D // P
FF = 1024
FC = FF // P
LH, LD = 8, 32
H, G, HD = 16, 4, 16
REP = H // G
VW = 32
KROWS = 6 * HD
E, INTER = 8, 512
MT = 40
ROW = 260
NEG = -1.0e30
EPS_LN = 1e-5
EPS_ATT = 1e-15
SLOPES = [2.0 ** (-0.5 * (h + 1)) for h in range(H)]


class Edge:

    def __init__(self, sem, per, by=1, ahead=None):
        self.sem, self.per, self.by, self.ahead = sem, per, by, per if ahead is None else ahead

    def open(self, engine):
        engine.sem_inc(self.sem, self.ahead * self.by)

    def wait(self, engine, i, k=0):
        engine.wait_ge(self.sem, (i * self.per + self.ahead + k + 1) * self.by)

    def wait_prev(self, engine, i, k=0):
        engine.wait_ge(self.sem, (i * self.per + self.ahead - self.per + k + 1) * self.by)


def both_streams():
    plan = """c29 b0 a0 c30 b1 a1 c31 b2 a2 b3 a3 a4 a5 b4 a6 a7 a8 a9 b5 a10 b6 a11 b7
              a12 b8 a13 b9 b10 a14 b11 b12 a15 b13 b14 b15 a16 b16 a17 a18 b17 a19 b18 b19 a20 b20 a21 b21 b22 b23 a22
              b24 b25 b26 b27 b28"""
    plan = [(step[0], int(step[1:])) for step in plan.split()]
    return [[step for step in plan if step[0] in streams] for streams in ("ab", "abc", "bc")]


def build(nc, t, out):
    ctx = ExitStack()
    with ctx:
        def sem(name):
            return ctx.enter_context(nc.semaphore(name))

        def edge(name, per, by=1, ahead=None):
            return Edge(sem(name), per, by, ahead)

        def sb(name, shape, dt, where=ctx):
            return where.enter_context(nc.sbuf_tensor(name, shape, dt))

        pa = ctx.enter_context(nc.psum_tensor("pa", [P, 4, 512], F32))
        pb = ctx.enter_context(nc.psum_tensor("pb", [P, 4, 512], F32))

        const = sb("const", [P, 1156], F32)
        ident = const[:, 0:128]
        had = const[:, 128:256]
        blk = const[:, 256:384]
        upper = const[:, 384:512]
        dist = const[:, 512:1024]
        hm4 = const[:, 1024:1028]
        noncausal = const[:, 1028:1156]
        identb = sb("identb", [P, P], BF16)
        maskb = sb("maskb", [P, P], BF16)
        mhalf = sb("mhalf", [P, NT], F32)
        X = sb("X", [P, TILES, D], F32)

        ab = ExitStack()
        bias = sb("bias", [P, D], F32, ab)
        w_qkv = sb("w_qkv", [P, 2, DC, 3 * D], F32R, ab)
        w_mix = sb("w_mix", [P, 2, 1792], F32R, ab)
        w_up = sb("w_up", [P, 2, 2, DC, FF], F32R, ab)
        w_dn = sb("w_dn", [P, 2, FC, D], F32R, ab)
        def wmix(s, at, n):
            return w_mix[:, s, at:at + DC * n].rearrange("p (c n) -> p c n", c=DC)
        w_proj = [wmix(s, 0, D) for s in range(2)]
        w_q = [wmix(s, 512, D) for s in range(2)]
        w_kv = [wmix(s, 1024, P) for s in range(2)]
        w_o = [wmix(s, 1280, D) for s in range(2)]
        xT = sb("xT", [P, 2, DC, S], F32R, ab)
        hT = sb("hT", [P, 2, 2, S], F32R, ab)
        xn = sb("xn", [P, NT, D], F32, ab)
        qT = sb("qT", [P, DC, S], F32, ab)
        ksb = sb("ksb", [P, NT, D], F32, ab)
        vsb = sb("vsb", [P, NT, DC, P + 1], F32, ab)
        vk = sb("vk", [P, DC, P + 4], F32, ab)
        th = sb("th", [P, 2, S // 2], F32, ab)
        hf = sb("hf", [P, 2, S], F32, ab)
        xnb = sb("xnb", [P, NT, D], F32, ab)
        xTb = sb("xTb", [P, 2, DC, S], F32R, ab)
        rq = sb("rq", [P, S], F32, ab)
        o0 = xn
        small = sb("small", [P, 132], F32, ab)
        stats = small[:, 0:24].rearrange("p (t s) -> p t s", t=NT)
        mv = small[:, 24:32].rearrange("p (t s) -> p t s", t=NT)
        var = small[:, 32:36]
        rstd = sb("rstd", [P, NT], F32, ab)
        rden = small[:, 36:52]
        den = small[:, 52:56]
        statst = small[:, 96:120].rearrange("p (t s) -> p t s", t=NT)
        mvt = small[:, 120:128].rearrange("p (t s) -> p t s", t=NT)
        vart = small[:, 128:132]
        rstdt = sb("rstdt", [P, NT], F32, ab)
        statsb = small[:, 56:80].rearrange("p (t s) -> p t s", t=NT)
        mvb = small[:, 80:88].rearrange("p (t s) -> p t s", t=NT)
        varb = small[:, 88:92]
        rstdb = sb("rstdb", [P, NT], F32, ab)

        raw = ExitStack()
        rawA = sb("rawA", [P, 2048], F32, raw)
        rawB = sb("rawB", [P, 2048], F32, raw)
        rawC = sb("rawC", [P, 2048], F32, raw)
        raw.close()
        Q6 = sb("Q6", [P, H, S], BF16, ab)
        K6 = sb("K6", [P, G, S], BF16, ab)
        V1 = sb("V1", [P, NT, G, VW], F32, ab)
        pq = sb("pq", [P, 3, DC, S], BF16, ab)
        pk = sb("pk", [P, 3, S], BF16, ab)
        kvs = sb("kvs", [P, S], F32, ab)
        sbi = sb("sbi", [P, 2, S], F32, ab)
        pr = sb("pr", [P, 3, S], F32, ab)
        mxn = sb("mxn", [P, P], F32, ab)
        pm = sb("pm", [NT * H, 3, P], BF16, ab)
        pmr = rq[0:NT * H, 0:P]
        OT = sb("OT", [P, 2, S], F32, ab)
        zt = OT[:].rearrange("p g (k d) -> p (g k) d", d=D)
        rco = sb("rco", [P, NT * REP], F32, ab)
        ab.close()

        cd = ExitStack()
        table = sb("table", [P, 72], F32, cd)
        tok2 = table[:, 0:TILES]
        ehigh = table[:, 16:24]
        tile_no = table[:, 24:64]
        pad_row = sb("pad_row", [P, 2, ROW], F32, cd)
        XN = sb("XN", [P, TILES, ROW], F32, cd)
        SH = sb("SH", [P, TILES, D], F32, cd)
        xnc = sb("xnc", [P, NT, D], F32, cd)
        rt = sb("rt", [P, 2, DC, P], F32R, cd)
        rraw = sb("rraw", [P, DC, P], F32, cd)
        s_th = sb("s_th", [P, 2, S], F32, cd)
        s_hf = sb("s_hf", [P, 2, S], F32, cd)
        lgT = sb("lgT", [P, S], F32, cd)
        ones = sb("ones", [P, P], F32, cd)
        L = sb("L", [P, TILES, E], F32, cd)
        R = [sb(f"R{n}", [P, TILES, E], F32, cd) for n in range(14)]
        r16 = [sb(f"r16_{n}", [P, TILES], F32, cd) for n in range(11)]
        r8 = [sb(f"r8_{n}", [P, E], F32, cd) for n in range(8)]
        i8 = [sb(f"i8_{n}", [P, E], I32, cd) for n in range(2)]
        idx = sb("idx", [P, 2, TILES], I32, cd)
        teI = sb("teI", [P, MT], I32, cd)
        teF = [sb(f"teF{n}", [P, MT], F32, cd) for n in range(2)]
        teC = sb("teC", [P, MT, E], F32, cd)
        c_small = sb("c_small", [P, 36], F32, cd)
        c_stats = c_small[:, 0:24].rearrange("p (t s) -> p t s", t=NT)
        c_mv = c_small[:, 24:32].rearrange("p (t s) -> p t s", t=NT)
        c_var = c_small[:, 32:36]
        c_rstd = sb("c_rstd", [P, NT], F32, cd)
        mo1 = ExitStack()
        XT = sb("XT", [P, 2, B, DC, S], F32R, mo1)
        s_up = sb("s_up", [P, 2, 2, DC, FF], F32R, mo1)
        s_dn = sb("s_dn", [P, 2, FC, D], F32R, mo1)
        s_stage = ExitStack()
        s_raw = sb("s_raw", [P, 2, 2048], F32, s_stage)
        s_stage.close()
        s_hT = sb("s_hT", [P, 2, FC, S], F32R, mo1)
        mo1.close()
        mo2 = ExitStack()
        ew1 = sb("ew1", [P, E, DC, 2 * INTER], F32, mo2)
        ew2 = sb("ew2", [P, E, INTER // P, D], F32, mo2)
        xt = sb("xt", [P, 2, ROW], F32, mo2)
        xtT = sb("xtT", [P, 2, DC, P], F32, mo2)
        e_s = sb("e_s", [P, 2, INTER], F32, mo2)
        e_h = sb("e_h", [P, 2, INTER], F32, mo2)
        e_hT = sb("e_hT", [P, 2, INTER // P, P], F32, mo2)
        e_y = sb("e_y", [P, 2, D], F32, mo2)
        e_number = sb("e_number", [P, 2], F32, mo2)
        e_row = sb("e_row", [P, 2], I32, mo2)
        mo2.close()
        mo3 = ExitStack()
        yb = sb("yb", [P, 2, NT, 2, D], F32, mo3)
        zc = sb("zc", [P, 2, NT, D], F32, mo3)
        mo3.close()
        cd.close()

        qd = nc.dram_tensor("q_pieces", (3, D, S), BF16, kind="Internal").ap()
        kd = nc.dram_tensor("k_pieces", (3, G * HD, S), BF16, kind="Internal").ap()
        xs = nc.dram_tensor("x_slots", (MT * P, ROW), F32, kind="Internal").ap()
        ys = nc.dram_tensor("y_rows", (2 * (TILES + 2) * P, D), F32, kind="Internal").ap()

        c_in = sem("const_loaded")
        b_in = sem("bias_loaded")
        x_in = sem("x_loaded")
        raw_in = [sem(f"raw_loaded{n}") for n in range(5)]
        split_hi = sem("weight_hi_written")
        split_lo = sem("weight_lo_written")
        setup = sem("setup_by_vector")
        bfly = sem("butterflies_done")
        hadd = sem("hadamard_product_done")
        hadh = sem("hadamard_hi_written")
        setup_pool = sem("setup_by_gpsimd")

        var_a, rstd_a = edge("variance_a", 4), edge("rstd_a", 4)
        xn_a, ps_a = edge("normed_a", 2), edge("psum_a_full", 26)
        xh_a, xl_a = edge("xT_hi_a", 3), edge("xT_lo_a", 3)
        q_a, kv_a, vk_a, o_a, y_a = edge("q_written", 1), edge("kv_written", 2), edge("vk_written", 1), edge("o_written", 2), edge("proj_added", 1)
        th_a, h_a, hh_a, hl_a, dn_a, z_a = edge("tanh_written", 16), edge("h_written", 16), edge("h_hi_written", 8), edge("h_lo_written", 8), edge("h_used", 8), edge("ffn_copied", 1)

        var_b, rstd_b = edge("variance_b", 1), edge("rstd_b", 1)
        var_t, rstd_t = edge("variance_t", 1), edge("rstd_t", 1)
        xn_b, psg_b = edge("normed_b", 1), edge("psum_b_full", 7)
        xh_b, xl_b = edge("xT_hi_b", 2), edge("xT_lo_b", 2)
        qh_b, kh_b, pc_b = edge("q_hi_written", 1), edge("k_hi_written", 1), edge("pieces_written", 2)
        v_b = edge("v_written", 1)
        bo_b = edge("pieces_in_dram", 2, 16)
        q6_b, k6_b = edge("q_packed", 6, 16), edge("k_packed", 6, 16)
        psm_b, mx_b = edge("max_scores_full", 44), edge("max_taken", 44)
        pm_b, m6_b = edge("max_pieces_written", 1), edge("max_packed", 3, 16)
        pss_b, bank_b = edge("scores_full", 44), edge("score_bank_read", 48)
        ex_b, pv_b, pso_b = edge("exp_written", 44), edge("probs_used", 44), edge("heads_summed", 4)
        ot_b, pst_b, on_b = edge("OT_written", 4), edge("OT_transposed", 4), edge("attention_written", 1)
        z_b = edge("attention_added", 1)
        var_c, rstd_c, xn_c = edge("variance_c", 1), edge("rstd_c", 1), edge("normed_c", 1)
        t_c, xh_c, xl_c = edge("xnc_transposed", 1), edge("XT_hi", 1), edge("XT_lo", 1)
        lg_c, lgc_c, lgt_c, L_c = edge("logits_full", 1), edge("logits_copied", 1), edge("logits_transposed", 1), edge("logits_written", 1)
        xc_c = edge("routed_row_copied", 1)
        t_in, pad_set, pad_out, r_in, rt_hi, rt_lo = (sem(n) for n in ("table_loaded", "pad_row_set", "pads_written", "router_loaded", "router_hi", "router_lo"))
        s_in = [sem(f"shared_weight_loaded{n}") for n in range(3)]
        s_hi, s_lo = sem("shared_hi_written"), sem("shared_lo_written")
        chosen, exped, counted, slots = (sem(n) for n in ("experts_chosen", "gap_exponentiated", "counts_full", "slots_written"))
        ps_s, th_s, h_s, hh_s, hl_s, z_s = (edge("psum_s_full", 10), edge("silu_written", 8), edge("s_h_written", 8), edge("s_h_hi_written", 8),
                                            edge("s_h_lo_written", 8), edge("shared_written", 2))
        shared_done = [sem(f"shared_done_{n}") for n in ("pe", "act", "dve", "pool")]
        ew_in = [sem("expert_w1_loaded"), sem("expert_w2_loaded")]
        xt_in = [edge(f"slot_rows_loaded{x}", 1, 16) for x in range(2)]
        tx_d, xT_d, w1_d, s_d, h_d = edge("slot_rows_transposed", 2), edge("xtT_written", 2), edge("expert_up_full", 4), edge("expert_silu_written", 2), edge("expert_h_written", 2)
        th_d, hT_d, w2_d, y_d, row_d = edge("expert_h_transposed", 2), edge("expert_hT_written", 2), edge("expert_down_full", 2), edge("expert_y_written", 2), edge("row_numbers_written", 2)
        number_d, turns = edge("number_written", 2), sem("scatters_begun")
        ysc = [edge(f"rows_scattered{x}", 1, 16, ahead=TILES) for x in range(2)]
        yb_in = [edge(f"y_rows_loaded{x}", 1, 16) for x in range(2)]
        var_e, rstd_e, out_e = edge("variance_e", 2), edge("rstd_e", 2), edge("result_ready", 2)
        y_used = edge("y_rows_used", 2)
        ab_done = [sem(f"layers_done_{n}") for n in ("pe", "act", "dve", "pool", "sp")]

        RAW = [(rawA, 1536), (rawB, 1792), (rawC, 2048), (rawA, 2048), (rawB, 2048)]
        HI_LO = [
            [w_qkv[:, s].rearrange("p c n -> p (c n)") for s in range(2)],
            [w_mix[:, s] for s in range(2)],
            [w_up[:, s, 0].rearrange("p c n -> p (c n)") for s in range(2)],
            [w_up[:, s, 1].rearrange("p c n -> p (c n)") for s in range(2)],
            [w_dn[:, s].rearrange("p c n -> p (c n)") for s in range(2)],
        ]

        def tile_of(i, k):
            return ds(i * NT + k, 1)

        PASSES = [(0, 0), (0, 1), (1, 0)]

        def norm_stats(dve, i, src, st, m, v, e_var):
            for k in range(NT):
                dve.bn_stats(st[:, k, :], src(k))
            dve.drain()
            for k in range(NT):
                dve.bn_aggr(m[:, k, :], st[:, k, :])
            dve.drain()
            dve.tensor_scalar(v, m[:, :, 1], EPS_LN, None, ALU.add).then_inc(e_var.sem, 1)

        def norm_apply(dve, k, dst, src, m, r):
            return dve.tensor_scalar(dst, src, m[:, k, 0:1], r[:, k:k + 1], ALU.subtract, ALU.mult)

        def rsqrt(pool, i, k, v, r, e_var, e_rstd):
            e_var.wait(pool, i, k)
            pool.tensor_tensor(r, v, mhalf[:, :], ALU.pow).then_inc(e_rstd.sem, 1)

        def split3(pe, dst, lhs, rhs, first=True, last=True):
            for n, (a, b) in enumerate(PASSES):
                mm = pe.matmul(dst, lhs[a], rhs[b], start=first and n == 0, stop=last and n == 2,
                               skip_group_check=True)
            return mm

        def in_order(order, **streams):
            ahead = {name: next(stream) for name, stream in streams.items()}
            for name, step in order:
                while ahead[name] is not None and ahead[name] <= step:
                    ahead[name] = next(streams[name], None)

        A_STEPS, B_STEPS = 23, 32
        ALONE_A = [("a", n) for n in range(A_STEPS)]
        ALONE_B = [("b", n) for n in range(B_STEPS)]
        FIRST, TOGETHER, LAST = both_streams()
        TAIL = [("c", n) for n in range(29, B_STEPS)]

        def pe_A(pe, i):
            def xs_(c):
                return [xT[:, s, c, :] for s in range(2)]

            def transposes(src, n):
                for c in range(DC):
                    for k in range(NT):
                        mm = pe.transpose(pa[:, 2 * (n % 2) + c, k * P:(k + 1) * P], src[:, k, c * P:(c + 1) * P], ident)
                mm.then_inc(ps_a.sem, 1)

            yield 1
            xn_a.wait(pe, i, 0)
            transposes(xn, 0)
            yield 3
            xh_a.wait(pe, i, 0)
            xl_a.wait(pe, i, 0)
            z_a.wait_prev(pe, i)
            for m in range(DC):
                for c in range(DC):
                    mm = split3(pe, pa[:, 2 + m, :], [w_qkv[:, s, c, m * P:(m + 1) * P] for s in range(2)], xs_(c), c == 0, c == 1)
            mm.then_inc(ps_a.sem, 1)
            for half in range(2):
                yield 4 + half
                if half == 1:
                    q_a.wait(pe, i)
                for kk in range(2):
                    k = 2 * half + kk
                    for c in range(DC):
                        mm = split3(pe, pa[:, 2 * half + kk, :], [xT[:, s, c, k * P:(k + 1) * P] for s in range(2)],
                                    [w_qkv[:, s, c, D:3 * D] for s in range(2)], c == 0, c == 1)
                mm.then_inc(ps_a.sem, 1)
            yield 6
            kv_a.wait(pe, i, 1)
            for c in range(DC):
                for k in range(NT):
                    mm = pe.matmul(pa[:, c, 0:P + 1], ksb[:, k, c * P:(c + 1) * P], vsb[:, k, c, :], start=k == 0, stop=k == NT - 1)
            mm.then_inc(ps_a.sem, 1)
            yield 7
            vk_a.wait(pe, i)
            for half in range(2):
                for kk in range(2):
                    k = 2 * half + kk
                    for c in range(DC):
                        mm = pe.matmul(pa[:, 2 * (1 - half) + kk, c * (P + 4):(c + 1) * (P + 4)], qT[:, c, k * P:(k + 1) * P], vk[:, c, :],
                                       start=True, stop=True, skip_group_check=True)
                mm.then_inc(ps_a.sem, 1)
            yield 8
            o_a.wait(pe, i, 1)
            transposes(o0, 1)
            yield 9
            xh_a.wait(pe, i, 1)
            xl_a.wait(pe, i, 1)
            for k in range(NT):
                for c in range(DC):
                    mm = split3(pe, pa[:, k // 2, (k % 2) * D:(k % 2 + 1) * D], [xT[:, s, c, k * P:(k + 1) * P] for s in range(2)],
                                [w_proj[s][:, c, :] for s in range(2)], c == 0, c == 1)
            mm.then_inc(ps_a.sem, 1)
            yield 11
            xn_a.wait(pe, i, 1)
            transposes(xn, 1)
            def down(j):
                hl_a.wait(pe, i, j)
                for k in range(NT):
                    mm = split3(pe, pa[:, 2 + k // 2, (k % 2) * D:(k % 2 + 1) * D], [hT[:, s, j % 2, k * P:(k + 1) * P] for s in range(2)],
                                [w_dn[:, s, j, :] for s in range(2)], j == 0 and k % 2 == 0, j == FC - 1)
                mm.then_inc(dn_a.sem, 1)
                return mm

            for j in range(FC):
                yield 12 + j
                if j == 0:
                    xh_a.wait(pe, i, 2)
                    xl_a.wait(pe, i, 2)
                for half in range(2):
                    if j >= 1:
                        h_a.wait(pe, i, 2 * (j - 1) + half)
                    for u in range(2):
                        for c in range(DC):
                            mm = split3(pe, pa[:, half, u * D:(u + 1) * D], [w_up[:, s, u, c, j * P:(j + 1) * P] for s in range(2)],
                                        [xT[:, s, c, half * D:(half + 1) * D] for s in range(2)], c == 0, c == 1)
                    mm.then_inc(ps_a.sem, 1)
                if j >= 1:
                    down(j - 1)
            yield 20
            down(FC - 1)

        def act_A(act, i):
            def hi(k, n, slot):
                ps_a.wait(act, i, n)
                act.activation(xT[:, 0], pa[:, 2 * slot:2 * slot + 2, :], ACT.Copy).then_inc(xh_a.sem, 1)

            yield 1
            hi(0, 0, 0)
            yield 3
            ps_a.wait(act, i, 1)
            act.activation(qT[:], pa[:, 2:4, :], ACT.Relu).then_inc(q_a.sem, 1)
            for half in range(2):
                yield 4 + half
                ps_a.wait(act, i, 2 + half)
                src = pa[:, 2 * half:2 * half + 2, :]
                act.activation(ksb[:, 2 * half:2 * half + 2, :], src[:, :, 0:D], ACT.Relu)
                for kk in range(2):
                    v = act.activation(vsb[:, 2 * half + kk, :, 0:P], src[:, kk, D:2 * D].rearrange("p (c n) -> p c n", c=DC), ACT.Copy)
                act.drain().then_inc(kv_a.sem, 1)
            yield 8
            hi(1, 7, 1)
            yield 11
            hi(2, 9, 1)

            def h_hi(j):
                h_a.wait(act, i, 2 * j + 1)
                if j >= 2:
                    dn_a.wait(act, i, j - 2)
                act.activation(hT[:, 0, j % 2], hf[:, j % 2], ACT.Copy).then_inc(hh_a.sem, 1)

            for j in range(FC):
                yield 12 + j
                if j >= 1:
                    h_hi(j - 1)
                for half in range(2):
                    ps_a.wait(act, i, 10 + 2 * j + half)
                    act.activation(th[:, half], pa[:, half, 0:D], ACT.Tanh, scale=0.5).then_inc(th_a.sem, 1)
            yield 20
            h_hi(FC - 1)

        def dve_A(dve, i):
            def xtile(k):
                return X[:, tile_of(i, k), :].rearrange("p a d -> p (a d)")

            def lo(k, slot):
                xh_a.wait(dve, i, k)
                dve.tensor_tensor(xT[:, 1], pa[:, 2 * slot:2 * slot + 2, :], xT[:, 0].bitcast(F32), ALU.subtract).then_inc(xl_a.sem, 1)

            yield 0
            norm_stats(dve, i, xtile, stats, mv, var, var_a)
            yield 1
            rstd_a.wait(dve, i, 0)
            for k in range(NT):
                norm_apply(dve, k, xn[:, k], xtile(k), mv, rstd)
            dve.drain().then_inc(xn_a.sem, 1)
            yield 2
            lo(0, 0)
            yield 6
            ps_a.wait(dve, i, 4)
            for c in range(DC):
                dve.tensor_tensor(vk[:, c, 0:P], pa[:, c, 0:P], blk, ALU.mult)
                dve.tensor_copy(den[:, c:c + 1], pa[:, c, P:P + 1])
            dve.drain()
            for c in range(DC):
                dve.tensor_scalar(vk[:, c, P:P + 4], hm4, den[:, c:c + 1], None, ALU.mult)
            dve.drain().then_inc(vk_a.sem, 1)
            for half in range(2):
                if half == 0:
                    yield 7
                ps_a.wait(dve, i, 5 + half)
                src = pa[:, 2 * (1 - half):2 * (1 - half) + 2, :]
                for kk in range(2):
                    o_src = src[:, kk, 0:DC * (P + 4)].rearrange("p (c n) -> p c n", c=DC)
                    r = rden[:, 8 * kk:8 * kk + 8]
                    dve.tensor_scalar(r.rearrange("p (c h) -> p c h", c=DC), o_src[:, :, P:P + 4], EPS_ATT, None, ALU.add)
                dve.drain()
                dve.reciprocal(rden, rden)
                dve.drain()
                for kk in range(2):
                    for c in range(DC):
                        o_src = src[:, kk, c * (P + 4):c * (P + 4) + P].rearrange("p (h e) -> p h e", e=LD)
                        r = rden[:, 8 * kk + 4 * c:8 * kk + 4 * c + 4]
                        dve.tensor_tensor(o0[:, 2 * half + kk, c * P:(c + 1) * P].rearrange("p (h e) -> p h e", e=LD), o_src,
                                          r.unsqueeze(2).to_broadcast([P, 4, LD]), ALU.mult)
                dve.drain().then_inc(o_a.sem, 1)
            yield 8
            lo(1, 1)
            yield 9
            ps_a.wait(dve, i, 8)
            dve.tensor_tensor(xn[:], pa[:, 0:2, :].rearrange("p b (k d) -> p (b k) d", d=D),
                              bias[:].unsqueeze(1).to_broadcast([P, NT, D]), ALU.add).then_inc(y_a.sem, 1)
            dve.drain()
            norm_stats(dve, i, lambda k: xn[:, k], stats, mv, var, var_a)
            yield 10
            rstd_a.wait(dve, i, 1)
            for k in range(NT):
                norm_apply(dve, k, xn[:, k], xn[:, k], mv, rstd)
            dve.drain()
            xb = X[:, ds(i * NT, NT), :]
            dve.tensor_tensor(xb, xb, xn[:], ALU.add)
            dve.drain()
            norm_stats(dve, i, xtile, stats, mv, var, var_a)
            yield 11
            rstd_a.wait(dve, i, 2)
            for k in range(NT):
                norm_apply(dve, k, xn[:, k], xtile(k), mv, rstd)
            dve.drain().then_inc(xn_a.sem, 1)
            lo(2, 1)
            for j in range(FC):
                yield 12 + j
                for half in range(2):
                    th_a.wait(dve, i, 2 * j + half)
                    dve.scalar_tensor_tensor(out=th[:, half], in0=th[:, half], scalar=1.0, in1=pa[:, half, 0:D], op0=ALU.add, op1=ALU.mult)
                    dve.drain()
                    if j >= 2 and half == 0:
                        hl_a.wait(dve, i, j - 2)
                    dve.scalar_tensor_tensor(out=hf[:, j % 2, half * D:(half + 1) * D], in0=th[:, half], scalar=0.5, in1=pa[:, half, D:2 * D],
                                             op0=ALU.mult, op1=ALU.mult).then_inc(h_a.sem, 1)
            yield 21
            dn_a.wait(dve, i, FC - 1)

            def product(k):
                return pa[:, 2 + k // 2, (k % 2) * D:(k % 2 + 1) * D]

            norm_stats(dve, i, product, stats, mv, var, var_a)
            yield 22
            rstd_a.wait(dve, i, 3)
            for k in range(NT):
                norm_apply(dve, k, xn[:, k], product(k), mv, rstd)
            dve.drain().then_inc(z_a.sem, 1)
            dve.tensor_tensor(xb, xb, xn[:], ALU.add)
            dve.drain()

        def pool_A(pool, i):
            for k, at in enumerate((0, 9, 10)):
                yield at
                rsqrt(pool, i, k, var, rstd[:], var_a, rstd_a)
            for j in range(FC):
                yield 13 + j
                hh_a.wait(pool, i, j)
                pool.tensor_tensor(hT[:, 1, j % 2], hf[:, j % 2], hT[:, 0, j % 2].bitcast(F32), ALU.subtract).then_inc(hl_a.sem, 1)
            yield 21
            rsqrt(pool, i, 3, var, rstd[:], var_a, rstd_a)

        def units_of(g):
            for kb in range(NT):
                hh = {0: 1, 1: 1, 2: 2, 3: 4}[kb]
                for h0 in range(0, REP, hh):
                    yield kb, h0, hh
        SEQ = []
        for g in range(G):
            for u, (kb, h0, hh) in enumerate(units_of(g)):
                SEQ.append(("S", g, kb, h0, hh))
                if u == 5 and g > 0:
                    SEQ.append(("T", g - 1))
        SEQ.append(("T", G - 1))
        MAXU = [(g, qb, h0, {0: 4, 1: 2, 2: 1, 3: 1}[qb]) for g in range(G) for qb in range(NT)
                for h0 in range(0, REP, {0: 4, 1: 2, 2: 1, 3: 1}[qb])]

        def pe_B(pe, i):
            yield 1
            xn_b.wait(pe, i)
            for c in range(DC):
                for k in range(NT):
                    mm = pe.transpose(pb[:, c, k * P:(k + 1) * P], xnb[:, k, c * P:(c + 1) * P], ident)
            mm.then_inc(psg_b.sem, 1)
            yield 3
            z_b.wait_prev(pe, i)
            xh_b.wait(pe, i, 0)
            xl_b.wait(pe, i, 0)
            for m in range(DC):
                for c in range(DC):
                    mm = split3(pe, pb[:, 2 + m, :], [w_q[s][:, c, m * P:(m + 1) * P] for s in range(2)],
                                [xTb[:, s, c, :] for s in range(2)], c == 0, c == 1)
            mm.then_inc(psg_b.sem, 1)
            for c in range(DC):
                mm = split3(pe, pb[:, 0, :], [w_kv[s][:, c, :] for s in range(2)], [xTb[:, s, c, :] for s in range(2)], c == 0, c == 1)
            mm.then_inc(psg_b.sem, 1)
            yield 4
            kh_b.wait(pe, i)
            for k in range(NT):
                mm = pe.transpose(pb[:, 1, k * P:(k + 1) * P], kvs[:, k * P:(k + 1) * P], ident)
            mm.then_inc(psg_b.sem, 1)
            yield 5
            q6_b.wait(pe, i, 5)
            k6_b.wait(pe, i, 5)
            v_b.wait(pe, i)
            pc_b.wait(pe, i, 1)
            for n, (g, qb, h0, hh) in enumerate(MAXU):
                if n % 4 == 0:
                    yield 5 + n // 4
                if n >= 2:
                    mx_b.wait(pe, i, n - 2)
                w = (qb + 1) * P
                for x in range(hh):
                    h = g * REP + h0 + x
                    pe.matmul(pb[:, n % 2, x * w:(x + 1) * w], Q6[0:KROWS, h, qb * P:(qb + 1) * P], K6[0:KROWS, g, 0:w],
                              start=True, stop=False, skip_group_check=True)
                    mm = pe.matmul(pb[:, n % 2, x * w + qb * P:(x + 1) * w], identb[:], maskb[:], start=False, stop=True, skip_group_check=True)
                mm.then_inc(psm_b.sem, 1)
            yield 16
            mx_b.wait(pe, i, len(MAXU) - 1)
            pe.transpose(pb[:, 2, 0:P], mxn[:], ident).then_inc(psg_b.sem, 1)
            yield 17
            m6_b.wait(pe, i, 2)

            def front(n):
                u = SEQ[n]
                if n >= 2:
                    bank_b.wait(pe, i, n - 2)
                if u[0] == "S":
                    _, g, kb, h0, hh = u
                    w = S - kb * P
                    pe.matmul(pb[:, n % 2, 0:hh * w], K6[0:KROWS + 3, g, kb * P:(kb + 1) * P],
                              Q6[0:KROWS + 3, g * REP + h0:g * REP + h0 + hh, kb * P:S], start=True, stop=True).then_inc(pss_b.sem, 1)
                else:
                    g = u[1]
                    ot_b.wait(pe, i, g)
                    for k in range(NT):
                        mm = pe.transpose(pb[:, n % 2, k * P:(k + 1) * P], OT[:, g % 2, k * P:(k + 1) * P], ident)
                    mm.then_inc(pst_b.sem, 1)

            s_at = 0
            front(0)
            front(1)
            for n, u in enumerate(SEQ[:-1]):
                if n % 4 == 0:
                    yield 17 + n // 4
                if n + 2 < len(SEQ) - 1:
                    front(n + 2)
                if u[0] == "S":
                    _, g, kb, h0, hh = u
                    w = S - kb * P
                    ex_b.wait(pe, i, s_at)
                    if kb == 0 and h0 == 0 and g >= 2:
                        ot_b.wait(pe, i, g - 2)
                    for x in range(hh):
                        hq = h0 + x
                        mm = pe.matmul(pb[hq * VW:(hq + 1) * VW, 2 + g % 2, kb * P:S], V1[:, kb, g, :], pr[:, s_at % 3, x * w:(x + 1) * w],
                                       start=kb == 0, stop=kb == NT - 1, skip_group_check=True)
                    s_at += 1
                    mm.then_inc(pv_b.sem, 1)
                    if kb == NT - 1:
                        pe.drain().then_inc(pso_b.sem, 1)
            front(len(SEQ) - 1)

        def pe_B_tail(pe, i):
            yield 29
            on_b.wait(pe, i)
            for c in range(DC):
                for k in range(NT):
                    mm = pe.transpose(pb[:, c, k * P:(k + 1) * P], xnb[:, k, c * P:(c + 1) * P], ident)
            mm.then_inc(psg_b.sem, 1)
            yield 30
            xh_b.wait(pe, i, 1)
            xl_b.wait(pe, i, 1)
            ot_b.wait(pe, i, G - 1)
            for k in range(NT):
                for c in range(DC):
                    mm = split3(pe, pb[:, 2 + k // 2, (k % 2) * D:(k % 2 + 1) * D], [xTb[:, s, c, k * P:(k + 1) * P] for s in range(2)],
                                [w_o[s][:, c, :] for s in range(2)], c == 0, c == 1)
            mm.then_inc(psg_b.sem, 1)

        def act_B(act, i):
            yield 1
            psg_b.wait(act, i, 0)
            act.activation(xTb[:, 0], pb[:, 0:2, :], ACT.Copy).then_inc(xh_b.sem, 1)
            yield 3
            psg_b.wait(act, i, 1)
            act.activation(pq[:, 0], pb[:, 2:4, :], ACT.Copy, scale=HD ** -0.5).then_inc(qh_b.sem, 1)
            psg_b.wait(act, i, 2)
            act.activation(pk[:, 0], pb[:, 0, :], ACT.Copy)
            act.activation(kvs[:], pb[:, 0, :], ACT.Copy)
            act.drain().then_inc(kh_b.sem, 1)
            s_at = 0
            for n, u in enumerate(SEQ):
                if n % 4 == 0:
                    yield 17 + n // 4
                if u[0] != "S":
                    continue
                _, g, kb, h0, hh = u
                w = S - kb * P
                bank_b.wait(act, i, n)
                if s_at >= 3:
                    pv_b.wait(act, i, s_at - 3)
                act.activation(pr[:, s_at % 3, 0:hh * w], sbi[:, s_at % 2, 0:hh * w], ACT.Exp).then_inc(ex_b.sem, 1)
                s_at += 1
                if kb == 0 and h0 == 1 and g > 0:
                    copy_OT(act, i, g - 1)
            copy_OT(act, i, G - 1)

        def act_B_tail(act, i):
            yield 29
            psg_b.wait(act, i, 5)
            act.activation(xTb[:, 0], pb[:, 0:2, :], ACT.Copy).then_inc(xh_b.sem, 1)

        def copy_OT(act, i, g):
            pso_b.wait(act, i, g)
            act.activation(OT[:, g % 2], pb[:, 2 + g % 2, :], ACT.Copy).then_inc(ot_b.sem, 1)

        def dve_B(dve, i):
            def xtile(k):
                return X[:, tile_of(i, k), :].rearrange("p a d -> p (a d)")

            yield 0
            norm_stats(dve, i, xtile, statsb, mvb, varb, var_b)
            yield 1
            rstd_b.wait(dve, i, 0)
            for k in range(NT):
                norm_apply(dve, k, xnb[:, k], xtile(k), mvb, rstdb)
            dve.drain().then_inc(xn_b.sem, 1)
            yield 2
            xh_b.wait(dve, i, 0)
            dve.tensor_tensor(xTb[:, 1], pb[:, 0:2, :], xTb[:, 0].bitcast(F32), ALU.subtract).then_inc(xl_b.sem, 1)
            yield 3
            qh_b.wait(dve, i)
            for c in range(DC):
                dve.scalar_tensor_tensor(out=rq[:], in0=pb[:, 2 + c, :], scalar=HD ** -0.5, in1=pq[:, 0, c], op0=ALU.mult, op1=ALU.subtract)
                dve.drain()
                dve.tensor_copy(pq[:, 1, c], rq[:])
                dve.drain()
                dve.tensor_tensor(pq[:, 2, c], rq[:], pq[:, 1, c], ALU.subtract)
                dve.drain()
            dve.drain().then_inc(pc_b.sem, 1)
            kh_b.wait(dve, i)
            dve.tensor_tensor(rq[:], pb[:, 0, :], pk[:, 0], ALU.subtract)
            dve.drain()
            dve.tensor_copy(pk[:, 1], rq[:])
            dve.drain()
            dve.tensor_tensor(pk[:, 2], rq[:], pk[:, 1], ALU.subtract).then_inc(pc_b.sem, 1)
            yield 4
            psg_b.wait(dve, i, 3)
            dve.tensor_copy(V1[:, :, :, 0:HD], pb[:, 1, :].rearrange("p (k z g d) -> p k z g d", k=NT, z=2, g=G)[:, :, 1]).then_inc(v_b.sem, 1)
            for n, (g, qb, h0, hh) in enumerate(MAXU):
                if n % 4 == 0:
                    yield 5 + n // 4
                psm_b.wait(dve, i, n)
                h = g * REP + h0
                dve.tensor_reduce(mxn[:, 0:NT * H].rearrange("p (h k) -> p k h", k=NT)[:, qb, h:h + hh], pb[:, n % 2, 0:hh * (qb + 1) * P].rearrange("p (h w) -> p h w", h=hh), AX, ALU.max,
                                  negate=True).then_inc(mx_b.sem, 1)
            yield 16
            psg_b.wait(dve, i, 4)
            mT = pb[0:NT * H, 2, 0:P]
            dve.tensor_copy(pm[:, 0], mT)
            dve.drain()
            dve.tensor_tensor(pmr, mT, pm[:, 0], ALU.subtract)
            dve.drain()
            dve.tensor_copy(pm[:, 1], pmr)
            dve.drain()
            dve.tensor_tensor(pm[:, 2], pmr, pm[:, 1], ALU.subtract).then_inc(pm_b.sem, 1)
            s_at = 0
            for n, u in enumerate(SEQ):
                if n % 4 == 0:
                    yield 17 + n // 4
                if u[0] == "S":
                    _, g, kb, h0, hh = u
                    w = S - kb * P
                    pss_b.wait(dve, i, s_at)
                    if s_at >= 2:
                        ex_b.wait(dve, i, s_at - 2)
                    for x in range(hh):
                        ins = dve.scalar_tensor_tensor(out=sbi[:, s_at % 2, x * w:(x + 1) * w], in0=dist[:, 0:w], scalar=-SLOPES[g * REP + h0 + x],
                                                       in1=pb[:, n % 2, x * w:(x + 1) * w], op0=ALU.mult, op1=ALU.add)
                    ins.then_inc(bank_b.sem, 1)
                    s_at += 1
                else:
                    g = u[1]
                    pst_b.wait(dve, i, g)
                    src = pb[:, n % 2, :].rearrange("p (k h e) -> p k h e", k=NT, h=REP)
                    dve.reciprocal(rco[:].rearrange("p (k h) -> p k h", k=NT), src[:, :, :, HD])
                    dve.drain()
                    ins = dve.tensor_tensor(xnb[:, :, g * REP * HD:(g + 1) * REP * HD].rearrange("p k (h e) -> p k h e", e=HD), src[:, :, :, 0:HD],
                                            rco[:].rearrange("p (k h) -> p k h", k=NT).unsqueeze(3).to_broadcast([P, NT, REP, HD]), ALU.mult)
                    ins.then_inc(bank_b.sem, 1)
            dve.drain().then_inc(on_b.sem, 1)

        def dve_B_tail(dve, i):
            yield 29
            xh_b.wait(dve, i, 1)
            dve.tensor_tensor(xTb[:, 1], pb[:, 0:2, :], xTb[:, 0].bitcast(F32), ALU.subtract).then_inc(xl_b.sem, 1)
            yield 30
            psg_b.wait(dve, i, 6)

            def product(k):
                return pb[:, 2 + k // 2, (k % 2) * D:(k % 2 + 1) * D]

            norm_stats(dve, i, product, statst, mvt, vart, var_t)
            yield 31
            rstd_t.wait(dve, i)
            for k in range(NT):
                norm_apply(dve, k, zt[:, k], product(k), mvt, rstdt)
            dve.drain().then_inc(z_b.sem, 1)
            xb = X[:, ds(i * NT, NT), :]
            dve.tensor_tensor(xb, xb, zt, ALU.add)
            dve.drain()

        def pool_B(pool, i):
            yield 0
            rsqrt(pool, i, 0, varb, rstdb[:], var_b, rstd_b)

        def pool_B_tail(pool, i):
            yield 30
            rsqrt(pool, i, 0, vart, rstdt[:], var_t, rstd_t)

        QP, KP = [0, 0, 1, 1, 0, 2], [0, 1, 0, 1, 2, 0]

        def sp_B(sp, i):
            yield 3
            pc_b.wait(sp, i, 0)
            sp.dma_start(qd.rearrange("z (c p) n -> p z c n", p=P), pq[:]).then_inc(bo_b.sem, 16)
            bo_b.wait(sp, i, 0)
            for r in range(6):
                sp.dma_start(Q6[r * HD:(r + 1) * HD], qd[QP[r]].rearrange("(h d) n -> d h n", d=HD)).then_inc(q6_b.sem, 16)
            pc_b.wait(sp, i, 1)
            sp.dma_start(kd.rearrange("z p n -> p z n"), pk[0:G * HD]).then_inc(bo_b.sem, 16)
            bo_b.wait(sp, i, 1)
            for r in range(6):
                sp.dma_start(K6[r * HD:(r + 1) * HD], kd[KP[r]].rearrange("(g d) n -> d g n", d=HD)).then_inc(k6_b.sem, 16)
            yield 16
            pm_b.wait(sp, i)
            for r in range(3):
                sp.dma_start(Q6[KROWS + r:KROWS + r + 1].rearrange("p h (k q) -> p (h k) q", k=NT), pm[:, r, :]).then_inc(m6_b.sem, 16)

        def xnorm(i, k):
            return X[:, tile_of(i, k), :].rearrange("p a d -> p (a d)")

        def XTs(i, s, c):
            return XT[:, s, ds(i, 1), c, :].rearrange("p a n -> p (a n)")

        def pe_router(pe, i):
            xn_c.wait(pe, i)
            xl_c.wait_prev(pe, i)
            for c in range(DC):
                for k in range(NT):
                    mm = pe.transpose(pa[:, c, k * P:(k + 1) * P], xnc[:, k, c * P:(c + 1) * P], ident)
            mm.then_inc(t_c.sem, 1)
            xh_c.wait(pe, i)
            xl_c.wait(pe, i)
            lgc_c.wait_prev(pe, i)
            for c in range(DC):
                mm = split3(pe, pb[:, 0, :], [rt[:, s, c, :] for s in range(2)], [XTs(i, s, c) for s in range(2)], c == 0, c == 1)
            mm.then_inc(lg_c.sem, 1)
            lgc_c.wait(pe, i)
            L_c.wait_prev(pe, i)
            for k in range(NT):
                mm = pe.transpose(pb[:, 1, k * P:(k + 1) * P], lgT[:, k * P:(k + 1) * P], ident)
            mm.then_inc(lgt_c.sem, 1)

        def act_router(act, i):
            xn_c.wait(act, i)
            act.activation(XN[:, ds(i * NT, NT), 0:D], xnc[:], ACT.Copy).then_inc(xc_c.sem, 1)
            t_c.wait(act, i)
            act.activation(XT[:, 0, ds(i, 1)].rearrange("p a c n -> p (a c n)"), pa[:, 0:2, :].rearrange("p c n -> p (c n)"), ACT.Copy).then_inc(xh_c.sem, 1)
            lg_c.wait(act, i)
            act.activation(lgT[:], pb[:, 0, :], ACT.Copy).then_inc(lgc_c.sem, 1)

        def dve_router(dve, i):
            norm_stats(dve, i, lambda k: xnorm(i, k), c_stats, c_mv, c_var, var_c)
            rstd_c.wait(dve, i)
            xc_c.wait_prev(dve, i)
            t_c.wait_prev(dve, i)
            for k in range(NT):
                norm_apply(dve, k, xnc[:, k], xnorm(i, k), c_mv, c_rstd)
            dve.drain().then_inc(xn_c.sem, 1)
            xh_c.wait(dve, i)
            dve.tensor_tensor(XT[:, 1, ds(i, 1)].rearrange("p a c n -> p (a c n)"), pa[:, 0:2, :].rearrange("p c n -> p (c n)"),
                              XT[:, 0, ds(i, 1)].rearrange("p a c n -> p (a c n)").bitcast(F32), ALU.subtract).then_inc(xl_c.sem, 1)
            lgt_c.wait(dve, i)
            dve.tensor_copy(L[:, ds(i * NT, NT), :], pb[:, 1, :].rearrange("p (k e) -> p k e", k=NT)[:, :, 0:E]).then_inc(L_c.sem, 1)

        def over_experts(a):
            return a.unsqueeze(2).to_broadcast([P, TILES, E])

        def over_tiles(a):
            return a.unsqueeze(1).to_broadcast([P, TILES, E])

        def dve_route(dve):
            def choose(logits, best, equal, key, kbest, mask):
                dve.tensor_reduce(best[:], logits[:], AX, ALU.max)
                dve.drain()
                dve.tensor_tensor(equal[:], logits[:], over_experts(best[:]), ALU.is_equal)
                dve.drain()
                dve.tensor_tensor(key[:], equal[:], over_tiles(ehigh), ALU.mult)
                dve.drain()
                dve.tensor_reduce(kbest[:], key[:], AX, ALU.max)
                dve.drain()
                dve.tensor_tensor(mask[:], key[:], over_experts(kbest[:]), ALU.is_equal)
                dve.drain()

            M1, M2, both = R[2], R[6], R[7]
            choose(L, r16[0], R[0], R[1], r16[1], M1)
            dve.scalar_tensor_tensor(out=R[3][:], in0=M1[:], scalar=-3.0e38, in1=L[:], op0=ALU.mult, op1=ALU.add)
            dve.drain()
            choose(R[3], r16[2], R[4], R[5], r16[3], M2)
            dve.tensor_tensor(r16[4][:], r16[2][:], r16[0][:], ALU.subtract)
            dve.tensor_tensor(both[:], M1[:], M2[:], ALU.add)
            dve.tensor_scalar(XN[:, :, D + 1], r16[1][:], -1.0, float(E), ALU.mult, ALU.add)
            dve.tensor_copy(XN[:, :, D], tok2)
            dve.drain().then_inc(chosen, 1)
            dve.wait_ge(counted, 1)
            total, inc = R[8], R[10]
            dve.tensor_copy(total[:], pb[:, 3, 0:TILES * E].rearrange("p (t e) -> p t e", e=E))
            dve.drain()
            src = total
            for n, dst in enumerate((R[9], R[10], R[11], R[10])):
                w = 1 << n
                dve.tensor_tensor(dst[:, w:], src[:, w:], src[:, :TILES - w], ALU.add)
                dve.tensor_copy(dst[:, 0:w], src[:, 0:w])
                dve.drain()
                src = dst
            dve.tensor_scalar(r8[0][:], inc[:, TILES - 1, :], float(P - 1), None, ALU.add)
            dve.drain()
            dve.tensor_copy(i8[0][:], r8[0][:])
            dve.drain()
            dve.tensor_scalar(i8[1][:], i8[0][:], 7, None, ALU.logical_shift_right)
            dve.drain()
            dve.tensor_copy(r8[1][:], i8[1][:])
            dve.drain()
            src = r8[1]
            for n, dst in enumerate((r8[2], r8[3], r8[4])):
                w = 1 << n
                dve.tensor_tensor(dst[:, w:], src[:, w:], src[:, :E - w], ALU.add)
                dve.tensor_copy(dst[:, 0:w], src[:, 0:w])
                dve.drain()
                src = dst
            end = r8[4]
            dve.tensor_tensor(r8[5][:], end[:], r8[1][:], ALU.subtract)
            dve.tensor_tensor(R[12][:], inc[:], total[:], ALU.subtract)
            dve.tensor_tensor(teC[:], tile_no.unsqueeze(2).to_broadcast([P, MT, E]), end[:].unsqueeze(1).to_broadcast([P, MT, E]), ALU.is_ge)
            dve.drain()
            dve.tensor_reduce(teF[0][:], teC[:], AX, ALU.add)
            dve.tensor_scalar(r8[6][:], r8[5][:], float(P), None, ALU.mult)
            dve.tensor_tensor(R[13][:], R[12][:], pb[:, 2, 0:TILES * E].rearrange("p (t e) -> p t e", e=E), ALU.add)
            dve.drain()
            dve.tensor_scalar(teF[1][:], teF[0][:], float(E - 1), None, ALU.min)
            dve.tensor_tensor(R[11][:], R[13][:], over_tiles(r8[6][:]), ALU.add)
            dve.drain()
            dve.tensor_copy(teI[:], teF[1][:])
            for k, m in enumerate((M1, M2)):
                dve.tensor_tensor(R[k][:], R[11][:], m[:], ALU.mult)
            dve.drain()
            for k in range(2):
                dve.tensor_reduce(r16[4 * k][:] if k == 0 else r16[3][:], R[k][:], AX, ALU.add)
            dve.drain()
            dve.tensor_copy(idx[:, 0, :], r16[0][:])
            dve.tensor_copy(idx[:, 1, :], r16[3][:])
            dve.drain().then_inc(slots, 1)
            dve.wait_ge(exped, 1)
            dve.tensor_scalar(r16[6][:], r16[5][:], 1.0, None, ALU.add)
            dve.drain()
            dve.reciprocal(r16[7][:], r16[6][:])
            dve.drain()
            dve.tensor_tensor(r16[8][:], r16[5][:], r16[7][:], ALU.mult)
            dve.drain()

        def pe_shared(pe, i):
            for j in range(FC):
                if j >= 2:
                    h_s.wait(pe, i, j - 2)
                else:
                    z_s.wait_prev(pe, i, j)
                for u in range(2):
                    for c in range(DC):
                        mm = split3(pe, pa[:, 2 * (j % 2) + u, :], [s_up[:, s, u, c, j * P:(j + 1) * P] for s in range(2)],
                                    [XTs(i, s, c) for s in range(2)], c == 0, c == 1)
                mm.then_inc(ps_s.sem, 1)
            hl_s.wait(pe, i, FC - 1)
            for half in range(2):
                for kk in range(2):
                    k = 2 * half + kk
                    for j in range(FC):
                        mm = split3(pe, pa[:, 2 * half, kk * D:(kk + 1) * D], [s_hT[:, s, j, k * P:(k + 1) * P] for s in range(2)],
                                    [s_dn[:, s, j, :] for s in range(2)], j == 0, j == FC - 1)
                mm.then_inc(ps_s.sem, 1)

        def act_shared(act, i):
            for j in range(FC):
                ps_s.wait(act, i, j)
                act.activation(s_th[:, j % 2], pa[:, 2 * (j % 2), :], ACT.Silu).then_inc(th_s.sem, 1)
                if j >= 1:
                    h_s.wait(act, i, j - 1)
                    act.activation(s_hT[:, 0, j - 1], s_hf[:, (j - 1) % 2], ACT.Copy).then_inc(hh_s.sem, 1)
            h_s.wait(act, i, FC - 1)
            act.activation(s_hT[:, 0, FC - 1], s_hf[:, (FC - 1) % 2], ACT.Copy).then_inc(hh_s.sem, 1)

        def dve_shared(dve, i):
            for j in range(FC):
                th_s.wait(dve, i, j)
                if j >= 2:
                    hl_s.wait(dve, i, j - 2)
                else:
                    hl_s.wait_prev(dve, i, FC - 2 + j)
                dve.tensor_tensor(s_hf[:, j % 2], s_th[:, j % 2], pa[:, 2 * (j % 2) + 1, :], ALU.mult).then_inc(h_s.sem, 1)
            for half in range(2):
                ps_s.wait(dve, i, FC + half)
                dve.tensor_copy(SH[:, ds(i * NT + 2 * half, 2), :], pa[:, 2 * half, :].rearrange("p (k d) -> p k d", d=D)).then_inc(z_s.sem, 1)

        def pool_shared(pool, i):
            for j in range(FC):
                hh_s.wait(pool, i, j)
                pool.tensor_tensor(s_hT[:, 1, j], s_hf[:, j % 2], s_hT[:, 0, j].bitcast(F32), ALU.subtract).then_inc(hl_s.sem, 1)

        def before(n, k=1):
            for _ in range(k):
                n = (n[0], 0) if n[1] else (n[0] - 1, 1)
            return n

        def after(n):
            return (n[0] + 1, 0) if n[1] else (n[0], 1)

        def expert_of(pe, n):
            return pe.value_load(teI[0:1, ds(2 * n[0] + n[1], 1)], min_val=0, max_val=E - 1)

        def pe_slot_rows(pe, n, bank_new=False):
            m, x = n
            xt_in[x].wait(pe, m)
            if not bank_new:
                y_d.wait(pe, m - 2, x)
            for c in range(DC):
                mm = pe.transpose(pb[:, x, c * P:(c + 1) * P], xt[:, x, c * P:(c + 1) * P], ident)
            mm.then_inc(tx_d.sem, 1)

        def pe_step(pe, n, up, down, rows=False):
            m, x = n
            m1, x1 = before(n)

            def w1(u):
                for c in range(DC):
                    mm = pe.matmul(pa[:, 2 * x + u, :], xtT[:, x, c, :], ew1[:, ds(te, 1), c, u * INTER:(u + 1) * INTER].rearrange("p a n -> p (a n)"),
                                   start=c == 0, stop=c == 1)
                mm.then_inc(w1_d.sem, 1)

            if up:
                te = expert_of(pe, n)
                xT_d.wait(pe, m, x)
                h_d.wait(pe, m - 1, x)
                w1(0)
            if down:
                te1 = expert_of(pe, (m1, x1))
                h_d.wait(pe, m1, x1)
                hT_d.wait(pe, m1 - 1, x1)
                for q in range(INTER // P):
                    mm = pe.transpose(pb[:, 2 + x1, q * P:(q + 1) * P], e_h[:, x1, q * P:(q + 1) * P], ident)
                mm.then_inc(th_d.sem, 1)
            if up:
                w1(1)
            if down:
                hT_d.wait(pe, m1, x1)
                if rows:
                    xT_d.wait(pe, *after(n))
                for q in range(INTER // P):
                    mm = pe.matmul(pb[:, x1, D:2 * D], e_hT[:, x1, q, :], ew2[:, ds(te1, 1), q, :].rearrange("p a n -> p (a n)"), start=q == 0, stop=q == INTER // P - 1)
                mm.then_inc(w2_d.sem, 1)

        def pe_experts(pe, n, first=False, last=False):
            if first:
                pe_slot_rows(pe, n, True)
            if not last:
                pe_slot_rows(pe, after(n), first)
            pe_step(pe, n, True, not first, not last)
            if last:
                pe_step(pe, after(n), False, True)

        def act_experts(act, n, first=False, last=False):
            def rows(n):
                m, x = n
                tx_d.wait(act, m, x)
                w1_d.wait(act, m - 1, 2 * x + 1)
                act.activation(xtT[:, x], pb[:, x, 0:D].rearrange("p (c n) -> p c n", c=DC), ACT.Copy).then_inc(xT_d.sem, 1)

            def result(n):
                m, x = n
                w2_d.wait(act, m, x)
                ysc[x].wait(act, m - 1)
                act.activation(e_y[:, x], pb[:, x, D:2 * D], ACT.Copy).then_inc(y_d.sem, 1)

            if first:
                rows(n)
            if not last:
                rows(after(n))
            m, x = n
            w1_d.wait(act, m, 2 * x)
            act.activation(e_s[:, x], pa[:, 2 * x, :], ACT.Silu).then_inc(s_d.sem, 1)
            if not first:
                result(before(n))
            if last:
                result(n)

        def dve_experts(dve, n, first=False, last=False):
            def number(n):
                m, x = n
                xt_in[x].wait(dve, m)
                dve.tensor_scalar(e_number[:, x:x + 1], xt[:, x, D + 1:D + 2], teF[1][:, ds(2 * m + x, 1)], xt[:, x, D:D + 1],
                                  ALU.not_equal, ALU.add).then_inc(number_d.sem, 1)

            def hidden_T(n):
                m, x = n
                th_d.wait(dve, m, x)
                dve.tensor_copy(e_hT[:, x], pb[:, 2 + x, :].rearrange("p (q n) -> p q n", n=P)).then_inc(hT_d.sem, 1)

            def row(n):
                m, x = n
                dve.drain()
                ysc[x].wait(dve, m - 1)
                dve.tensor_copy(e_row[:, x:x + 1], e_number[:, x:x + 1]).then_inc(row_d.sem, 1)
                dve.drain()

            m, x = n
            if first:
                number(n)
            else:
                row(before(n))
            if not last:
                number(after(n))
            if not first:
                hidden_T(before(n))
            w1_d.wait(dve, m, 2 * x + 1)
            s_d.wait(dve, m, x)
            dve.tensor_tensor(e_h[:, x], e_s[:, x], pa[:, 2 * x + 1, :], ALU.mult).then_inc(h_d.sem, 1)
            if last:
                row(n)
                hidden_T(n)

        def pool_experts(pool, n, first=False, last=False):
            def scatter(n):
                m, x = n
                row_d.wait(pool, m, x)
                y_d.wait(pool, m, x)
                pool.sem_inc(turns, 1)
                pool.indirect_dma_start(ys, bass.IndirectOffsetOnAxis(ap=e_row[:, x:x + 1], axis=0), e_y[:, x, :], None).then_inc(ysc[x].sem, 16)

            if not first:
                scatter(before(n))
            if last:
                scatter(n)

        def sp_experts(sp, n):
            m, x = n
            tx_d.wait(sp, m - 1, x)
            number_d.wait(sp, m - 1, x)
            sp.dma_start(xt[:, x, :], xs[ds((2 * m + x) * P, P), :]).then_inc(xt_in[x].sem, 16)

        def all_slot_tiles(engine, steps):
            steps(engine, (0, 0), first=True)
            with engine.Fori(0, MT // 2 - 1) as m:
                steps(engine, (m, 1))
                steps(engine, (m + 1, 0))
            steps(engine, (MT // 2 - 1, 1), last=True)

        def dve_result(dve, p):
            for x in range(2):
                yb_in[x].wait(dve, p)
                base = 2 * NT * p + x * NT
                def w(r, k):
                    return r[:, ds(base + k, 1)]
                for k in range(NT):
                    dve.scalar_tensor_tensor(out=zc[:, x, k], in0=yb[:, x, k, 0], scalar=w(r16[7], k), in1=SH[:, ds(base + k, 1), :].rearrange("p a d -> p (a d)"),
                                             op0=ALU.mult, op1=ALU.add)
                dve.drain()
                for k in range(NT):
                    dve.scalar_tensor_tensor(out=zc[:, x, k], in0=yb[:, x, k, 1], scalar=w(r16[8], k), in1=zc[:, x, k], op0=ALU.mult, op1=ALU.add)
                dve.drain().then_inc(y_used.sem, 1)
                norm_stats(dve, p, lambda k: zc[:, x, k], c_stats, c_mv, c_var, var_e)
                rstd_e.wait(dve, p, x)
                for k in range(NT):
                    norm_apply(dve, k, zc[:, x, k], zc[:, x, k], c_mv, c_rstd)
                dve.drain()
                xb = X[:, ds(base, NT), :]
                dve.tensor_tensor(xb, xb, zc[:, x], ALU.add).then_inc(out_e.sem, 1)
                dve.drain()

        def sp_result(sp, p):
            for x in range(2):
                y_used.wait_prev(sp, p, x)
                sp.dma_start(yb[:, x], ys[ds((2 * p + x) * 2 * S, 2 * S), :].rearrange("(t p k) d -> p t k d", p=P, k=2)).then_inc(yb_in[x].sem, 16)

        out_sem = sem("out_written")
        block = ctx.enter_context(nc.Block())

        SHARED = [[s_up[:, s, u].rearrange("p c n -> p (c n)") for s in range(2)] for u in range(2)] + \
                 [[s_dn[:, s].rearrange("p c n -> p (c n)") for s in range(2)]]

        def all_done(eng, me):
            eng.drain().then_inc(ab_done[me], 1)
            for n in range(5):
                if n != me:
                    eng.wait_ge(ab_done[n], 1)

        @block.sync
        def _(sp):
            sp.dma_start(const[:], t["const"]).then_inc(c_in, 16)
            for n, (r, w) in enumerate(RAW):
                if n == 3:
                    sp.wait_ge(split_lo, 1)
                if n == 4:
                    sp.wait_ge(split_lo, 2)
                sp.dma_start(r[:, 0:w], t[f"raw{n}"]).then_inc(raw_in[n], 16)
            for e in (bo_b, q6_b, k6_b, m6_b):
                e.open(sp)
            with sp.Fori(0, B) as i:
                in_order(ALONE_B, b=sp_B(sp, i))
            all_done(sp, 4)
            sp.dma_start(table[:], t["table"]).then_inc(t_in, 16)
            sp.wait_ge(pad_set, 1)
            for x in range(2):
                sp.dma_start(xs.rearrange("(t x p) r -> x p t r", x=2, p=P)[x], pad_row[:, x].unsqueeze(1).to_broadcast([P, MT // 2, ROW])).then_inc(pad_out, 16)
            sp.dma_start(rraw[:].rearrange("p c n -> p (c n)"), t["router"]).then_inc(r_in, 16)
            for n in range(3):
                if n == 2:
                    sp.wait_ge(s_lo, 1)
                sp.dma_start(s_raw[:, n % 2], t[f"shared{n}"]).then_inc(s_in[n], 16)
            for n in range(4):
                sp.wait_ge(shared_done[n], 1)
            sp.dma_start(ew1[:].rearrange("p e c n -> p (e c n)"), t["expert1"]).then_inc(ew_in[0], 16)
            sp.dma_start(ew2[:].rearrange("p e c n -> p (e c n)"), t["expert2"]).then_inc(ew_in[1], 16)
            for e in xt_in + yb_in:
                e.open(sp)
            for k in range(2):
                sp.wait_ge(ysc[k].sem, 16 * TILES)
            with sp.Fori(0, MT // 2) as m:
                for x in range(2):
                    sp_experts(sp, (m, x))
            for x in range(2):
                ysc[x].wait(sp, MT // 2 - 1)
            with sp.Fori(0, B // 2) as p:
                sp_result(sp, p)

        @block.scalar
        def _(act):
            act.dma_start(X[:], t["x"].rearrange("(t p) d -> p t d", p=P)).then_inc(x_in, 16)
            act.dma_start(bias[:], t["b_proj"].unsqueeze(0).to_broadcast([P, D])).then_inc(b_in, 16)
            for n in range(4):
                act.wait_ge(raw_in[n], 16)
                act.activation(HI_LO[n][0], RAW[n][0][:, 0:RAW[n][1]], ACT.Copy).then_inc(split_hi, 1)
            for q in range(2):
                act.wait_ge(hadd, q + 1)
                act.activation(w_dn[:, 0, 4 * q:4 * q + 4].rearrange("p a d -> p (a d)"), pa[:, 2 * q:2 * q + 2, :], ACT.Copy, scale=1 / 32).then_inc(hadh, 1)
            for e in (xh_a, q_a, kv_a, th_a, hh_a, xh_b, qh_b, kh_b, ex_b, ot_b):
                e.open(act)
            in_order(ALONE_A, a=act_A(act, 0))
            in_order(FIRST, a=act_A(act, 1), b=act_B(act, 0))
            with act.Fori(1, B - 1) as i:
                in_order(TOGETHER, c=act_B_tail(act, i - 1), a=act_A(act, i + 1), b=act_B(act, i))
            in_order(LAST, c=act_B_tail(act, B - 2), b=act_B(act, B - 1))
            in_order(TAIL, c=act_B_tail(act, B - 1))
            all_done(act, 1)
            act.wait_ge(r_in, 16)
            act.activation(rt[:, 0], rraw[:], ACT.Copy).then_inc(rt_hi, 1)
            for e in (xh_c, lgc_c, xc_c, th_s, hh_s, xT_d, s_d, y_d):
                e.open(act)
            with act.Fori(0, B) as i:
                act_router(act, i)
            act.wait_ge(chosen, 1)
            act.activation(r16[5][:], r16[4][:], ACT.Exp).then_inc(exped, 1)
            for n in range(3):
                act.wait_ge(s_in[n], 16)
                act.activation(SHARED[n][0], s_raw[:, n % 2], ACT.Copy).then_inc(s_hi, 1)
            with act.Fori(0, B) as i:
                act_shared(act, i)
            act.drain().then_inc(shared_done[1], 1)
            all_slot_tiles(act, act_experts)
            with act.Fori(0, B) as i:
                act.wait_ge(out_e.sem, i + 3)
                act.dma_start(out[ds(i * S, S), :].rearrange("(t p) d -> p t d", p=P), X[:, ds(i * NT, NT), :]).then_inc(out_sem, 16)
            act.wait_ge(out_sem, 16 * B)

        @block.vector
        def _(dve):
            dve.memset(mhalf[:], -0.5)
            dve.memset(vsb[:, :, :, P:P + 1], 1.0)
            dve.drain().then_inc(setup, 1)
            dve.wait_ge(c_in, 16)
            dve.tensor_copy(identb[:], ident)
            dve.tensor_copy(maskb[:], noncausal)
            dve.drain().then_inc(setup, 1)
            for n in range(4):
                dve.wait_ge(split_hi, n + 1)
                dve.tensor_tensor(HI_LO[n][1], RAW[n][0][:, 0:RAW[n][1]], HI_LO[n][0].bitcast(F32), ALU.subtract).then_inc(split_lo, 1)
            dve.wait_ge(raw_in[4], 16)
            dve.drain()
            src, dst = rawB, rawC
            for st in range(3):
                a = src[:].rearrange("p (x two y) -> p x two y", two=2, y=D << st)
                b = dst[:].rearrange("p (x two y) -> p x two y", two=2, y=D << st)
                dve.tensor_tensor(b[:, :, 0], a[:, :, 0], a[:, :, 1], ALU.add)
                dve.tensor_tensor(b[:, :, 1], a[:, :, 0], a[:, :, 1], ALU.subtract)
                dve.drain()
                src, dst = dst, src
            dve.drain().then_inc(bfly, 1)
            for q in range(2):
                dve.wait_ge(hadh, q + 1)
                dve.scalar_tensor_tensor(out=w_dn[:, 1, 4 * q:4 * q + 4].rearrange("p a d -> p (a d)"), in0=pa[:, 2 * q:2 * q + 2, :].rearrange("p a d -> p (a d)"),
                                         scalar=1 / 32, in1=w_dn[:, 0, 4 * q:4 * q + 4].rearrange("p a d -> p (a d)").bitcast(F32),
                                         op0=ALU.mult, op1=ALU.subtract).then_inc(split_lo, 1)
            dve.drain()
            dve.memset(K6[KROWS:P, :, :], 1.0)
            dve.memset(V1[:], 0.0)
            dve.memset(mxn[:], 0.0)
            dve.drain()
            dve.memset(V1[:, :, :, HD:HD + 1], 1.0)
            dve.drain()
            for e in (var_a, xn_a, xl_a, vk_a, o_a, y_a, h_a, z_a, var_b, var_t, xn_b, xl_b, pc_b, v_b, mx_b, pm_b, bank_b, on_b, z_b):
                e.open(dve)
            dve.wait_ge(x_in, 16)
            dve.wait_ge(b_in, 16)
            in_order(ALONE_A, a=dve_A(dve, 0))
            in_order(FIRST, a=dve_A(dve, 1), b=dve_B(dve, 0))
            with dve.Fori(1, B - 1) as i:
                in_order(TOGETHER, c=dve_B_tail(dve, i - 1), a=dve_A(dve, i + 1), b=dve_B(dve, i))
            in_order(LAST, c=dve_B_tail(dve, B - 2), b=dve_B(dve, B - 1))
            in_order(TAIL, c=dve_B_tail(dve, B - 1))
            all_done(dve, 2)
            dve.memset(ones[:], 1.0)
            dve.wait_ge(t_in, 16)
            dve.memset(pad_row[:], 0.0)
            dve.drain()
            dve.tensor_copy(pad_row[:, :, D], table[:, 64:66])
            dve.drain().then_inc(pad_set, 1)
            dve.memset(XN[:, :, D + 2:ROW], 0.0)
            dve.wait_ge(rt_hi, 1)
            dve.tensor_tensor(rt[:, 1], rraw[:], rt[:, 0].bitcast(F32), ALU.subtract).then_inc(rt_lo, 1)
            for e in (var_c, xn_c, xl_c, L_c, h_s, z_s, h_d, hT_d, row_d, number_d, var_e, out_e, y_used):
                e.open(dve)
            with dve.Fori(0, B) as i:
                dve_router(dve, i)
            dve.drain()
            dve_route(dve)
            for n in range(3):
                dve.wait_ge(s_hi, n + 1)
                dve.tensor_tensor(SHARED[n][1], s_raw[:, n % 2], SHARED[n][0].bitcast(F32), ALU.subtract).then_inc(s_lo, 1)
            with dve.Fori(0, B) as i:
                dve_shared(dve, i)
            dve.drain().then_inc(shared_done[2], 1)
            all_slot_tiles(dve, dve_experts)
            dve.drain()
            with dve.Fori(0, B // 2) as p:
                dve_result(dve, p)

        @block.gpsimd
        def _(pool):
            pool.wait_ge(setup, 1)
            for e in (rstd_a, hl_a, rstd_b, rstd_t):
                e.open(pool)
            in_order(ALONE_A, a=pool_A(pool, 0))
            in_order(FIRST, a=pool_A(pool, 1), b=pool_B(pool, 0))
            with pool.Fori(1, B - 1) as i:
                in_order(TOGETHER, c=pool_B_tail(pool, i - 1), a=pool_A(pool, i + 1), b=pool_B(pool, i))
            in_order(LAST, c=pool_B_tail(pool, B - 2), b=pool_B(pool, B - 1))
            in_order(TAIL, c=pool_B_tail(pool, B - 1))
            all_done(pool, 3)
            for e in [rstd_c, hl_s, rstd_e]:
                e.open(pool)
            with pool.Fori(0, B) as i:
                rsqrt(pool, i, 0, c_var, c_rstd[:], var_c, rstd_c)
            pool.wait_ge(pad_out, 32)
            pool.wait_ge(slots, 1)
            xc_c.wait(pool, B - 1)
            for n in range(TILES):
                for k in range(2):
                    pool.indirect_dma_start(xs, bass.IndirectOffsetOnAxis(ap=idx[:, k, n:n + 1], axis=0), XN[:, n, :], None).then_inc(ysc[k].sem, 16)
            with pool.Fori(0, B) as i:
                pool_shared(pool, i)
            pool.drain().then_inc(shared_done[3], 1)
            all_slot_tiles(pool, pool_experts)
            with pool.Fori(0, B // 2) as p:
                for x in range(2):
                    rsqrt(pool, p, x, c_var, c_rstd[:], var_e, rstd_e)

        @block.tensor
        def _(pe):
            pe.wait_ge(setup, 2)
            pe.wait_ge(c_in, 16)
            pe.wait_ge(bfly, 1)
            for q in range(4):
                mm = pe.matmul(pa[:, q, :], had, rawC[:, q * 512:(q + 1) * 512], start=True, stop=True)
                if q % 2:
                    mm.then_inc(hadd, 1)
            pe.wait_ge(split_lo, 6)
            for e in (ps_a, dn_a, psg_b, psm_b, pss_b, pv_b, pso_b, pst_b):
                e.open(pe)
            in_order(ALONE_A, a=pe_A(pe, 0))
            in_order(FIRST, a=pe_A(pe, 1), b=pe_B(pe, 0))
            with pe.Fori(1, B - 1) as i:
                in_order(TOGETHER, c=pe_B_tail(pe, i - 1), a=pe_A(pe, i + 1), b=pe_B(pe, i))
            in_order(LAST, c=pe_B_tail(pe, B - 2), b=pe_B(pe, B - 1))
            in_order(TAIL, c=pe_B_tail(pe, B - 1))
            all_done(pe, 0)
            for e in (t_c, lg_c, lgt_c, ps_s, tx_d, w1_d, th_d, w2_d):
                e.open(pe)
            pe.wait_ge(rt_lo, 1)
            with pe.Fori(0, B) as i:
                pe_router(pe, i)
            pe.wait_ge(chosen, 1)
            both = R[7][:].rearrange("p t e -> p (t e)")
            pe.matmul(pb[:, 2, 0:TILES * E], upper, both, start=True, stop=True)
            pe.matmul(pb[:, 3, 0:TILES * E], ones[:], both, start=True, stop=True).then_inc(counted, 1)
            pe.wait_ge(s_lo, 3)
            with pe.Fori(0, B) as i:
                pe_shared(pe, i)
            pe.drain().then_inc(shared_done[0], 1)
            pe.wait_ge(ew_in[0], 16)
            pe.wait_ge(ew_in[1], 16)
            pe.wait_ge(slots, 1)
            all_slot_tiles(pe, pe_experts)


def constants():
    import numpy as np
    c = np.zeros((P, 1156), np.float32)
    i = np.arange(P)
    c[:, 0:128] = np.eye(P)
    had = np.array([[1.0]])
    while had.shape[0] < P:
        had = np.block([[had, had], [had, -had]])
    c[:, 128:256] = had
    c[:, 256:384] = i[:, None] // LD == i[None, :] // LD
    c[:, 384:512] = i[:, None] < i[None, :]
    d = np.arange(512)[None, :] - i[:, None]
    c[:, 512:1024] = np.where(d >= 0, np.sqrt(np.maximum(d, 0).astype(np.float32)), 1e30)
    c[:, 1024:1028] = i[:, None] // LD == np.arange(4)[None, :]
    c[:, 1028:1156] = np.where(i[None, :] > i[:, None], NEG, 0)
    return c


def tables():
    import numpy as np
    c = np.zeros((P, 72), np.float32)
    i = np.arange(P)
    c[:, 0:TILES] = 2 * (np.arange(TILES)[None, :] * P + i[:, None])
    c[:, 16:24] = E - np.arange(E)
    c[:, 24:24 + MT] = np.arange(MT)
    c[:, 64:66] = 2 * (TILES + np.arange(2)[None, :]) * P + 2 * i[:, None]
    return c


def layout(inputs):
    import numpy as np

    def kt(w):
        w = np.asarray(w)
        k, n = w.shape
        return w.reshape(k // P, P, n).transpose(1, 0, 2).reshape(P, -1)

    g = {k: np.asarray(v) for k, v in inputs.items()}
    kv = np.concatenate([g["L1_attn_Wk"].T, g["L1_attn_Wv"].T], 1)
    return {
        "x": g["L0_attn_x"].reshape(B * S, D),
        "b_proj": g["L0_attn_b_proj"],
        "raw0": kt(g["L0_attn_w_qkv"].T),
        "raw1": np.concatenate([kt(g["L0_attn_w_proj"].T), kt(g["L1_attn_Wq"].T), kt(kv), kt(g["L1_attn_Wo"].T)], 1),
        "raw2": kt(g["L0_ffn_W1"].T),
        "raw3": kt(g["L0_ffn_W3"].T),
        "raw4": kt(g["L0_ffn_W2"].T),
        "const": constants(),
        "table": tables(),
        "router": kt(np.pad(g["L1_ffn_router_w"], ((0, 0), (0, P - E)))),
        "shared0": kt(g["L1_ffn_w_gate"]),
        "shared1": kt(g["L1_ffn_w_up"]),
        "shared2": kt(g["L1_ffn_w_down"]),
        "expert1": np.concatenate([kt(w) for w in g["L1_ffn_w1"]], 1),
        "expert2": np.concatenate([kt(w) for w in g["L1_ffn_w2"]], 1),
    }


def kernel(**inputs):
    import numpy as np
    import concourse.bacc as bacc
    from concourse.bass_utils import run_bass_kernel_spmd

    nc = bacc.Bacc("TRN2", target_bir_lowering=False, num_devices=1)
    arrays = {f"in_{k}": np.ascontiguousarray(v) for k, v in layout(inputs).items()}
    t = {k[3:]: nc.dram_tensor(k, v.shape, mybir.dt.from_np(v.dtype), kind="ExternalInput").ap() for k, v in arrays.items()}
    out = nc.dram_tensor("out", (B * S, D), F32, kind="ExternalOutput").ap()
    build(nc, t, out)
    r = run_bass_kernel_spmd(nc, [arrays], core_ids=[0])
    return r.results[0]["out"].reshape(B, S, D)
```

```python
from contextlib import ExitStack

import concourse.bass as bass
from concourse import mybir

F32 = mybir.dt.float32
F32R = mybir.dt.float32r
BF16 = mybir.dt.bfloat16
I32 = mybir.dt.int32
ALU = mybir.AluOpType
ACT = mybir.ActivationFunctionType
AX = mybir.AxisListType.X
ds = bass.ds

P = 128
B, S, D = 4, 512, 256
NT = S // P
TILES = B * NT
DC = D // P
FF = 1024
FC = FF // P
LH, LD = 8, 32
H, G, HD = 16, 4, 16
REP = H // G
VW = 32
KROWS = 6 * HD
E, INTER = 8, 512
MT = 40
ROW = 260
NEG = -1.0e30
EPS_LN = 1e-5
EPS_ATT = 1e-15
SLOPES = [2.0 ** (-0.5 * (h + 1)) for h in range(H)]


class Edge:

    def __init__(self, sem, per, by=1, ahead=None):
        self.sem, self.per, self.by, self.ahead = sem, per, by, per if ahead is None else ahead

    def open(self, engine):
        engine.sem_inc(self.sem, self.ahead * self.by)

    def wait(self, engine, i, k=0):
        engine.wait_ge(self.sem, (i * self.per + self.ahead + k + 1) * self.by)

    def wait_prev(self, engine, i, k=0):
        engine.wait_ge(self.sem, (i * self.per + self.ahead - self.per + k + 1) * self.by)


class Steps:

    def __init__(self, program):
        self.program, self.ahead = program, next(program)

    def through(self, step):
        while self.ahead is not None and self.ahead <= step:
            self.ahead = next(self.program, None)


def orders():
    both = """c29 b0 a0 c30 b1 a1 c31 b2 a2 b3 a3 a4 a5 b4 a6 a7 a8 a9 b5 a10 b6 a11 b7
              a12 b8 a13 b9 b10 a14 b11 b12 a15 b13 b14 b15 a16 b16 a17 a18 b17 a19 b18 b19 a20 b20 a21 b21 b22 b23 a22
              b24 b25 b26 b27 b28"""
    last = """c29 b0 s0 c30 b1 s1 c31 b2 s2 b3 w0 s3 s4 w1 w2 b4 s5 s6 s7 b5 s8 b6 s9 b7 s10 b8 s11 b9 s12 b10 s14
              t0 b11 t1 b12 t2 b13 t3 b14 t4 t5 b15 t6 b16 t7 t8 b17 t9 b18 t10 b19 t11 b20 t12 b21 t14
              u0 b22 u1 b23 u2 u3 b24 u4 u5 b25 u6 b26 u7 b27 u8 b28 u9"""
    tail = "c29 u10 c30 u11 c31 u12 u14 s0 s1 s2 s3 s4"
    ffn = "s5 r0 s6 r1 s7 r2 s8 r3 s9 r4 s10 r5 s11 r6 s12 r7 s14"

    def steps(plan, streams):
        return [(step[0], int(step[1:])) for step in plan.split() if step[0] in streams]

    return steps(both, "ab"), steps(both, "abc"), steps(last, "bcstuw"), steps(tail, "csu"), steps(ffn, "sr")


def build(nc, t, out):
    ctx = ExitStack()
    with ctx:
        def sem(name):
            return ctx.enter_context(nc.semaphore(name))

        def edge(name, per, by=1, ahead=None):
            return Edge(sem(name), per, by, ahead)

        def sb(name, shape, dt, where=ctx):
            return where.enter_context(nc.sbuf_tensor(name, shape, dt))

        pa = ctx.enter_context(nc.psum_tensor("pa", [P, 4, 512], F32))
        pb = ctx.enter_context(nc.psum_tensor("pb", [P, 4, 512], F32))

        const = sb("const", [P, 1156], F32)
        ident = const[:, 0:128]
        had = const[:, 128:256]
        blk = const[:, 256:384]
        upper = const[:, 384:512]
        dist = const[:, 512:1024]
        hm4 = const[:, 1024:1028]
        noncausal = const[:, 1028:1156]
        table = sb("table", [P, 72], F32)
        tok2 = table[:, 0:TILES]
        ehigh = table[:, 16:24]
        tile_no = table[:, 24:64]
        identb = sb("identb", [P, P], BF16)
        maskb = sb("maskb", [P, P], BF16)
        mhalf = sb("mhalf", [P, NT], F32)
        X = sb("X", [P, TILES, D], F32)
        in_place = ExitStack()
        rt_raw = sb("rt_raw", [P, 2, DC, P], F32, in_place)
        in_place.close()
        rt = sb("rt", [P, 2, DC, P], F32R)
        L = sb("L", [P, TILES, E], F32)

        in_place = ExitStack()
        up_raw = sb("up_raw", [P, 2, 2, DC, FF], F32, in_place)
        dn_raw = sb("dn_raw", [P, 2, FC, D], F32, in_place)
        in_place.close()
        ffn = ExitStack()
        w_up = sb("w_up", [P, 2, 2, DC, FF], F32R, ffn)
        w_dn = sb("w_dn", [P, 2, FC, D], F32R, ffn)
        xT = sb("xT", [P, 2, DC, S], F32R, ffn)
        hT = sb("hT", [P, 2, 2, S], F32R, ffn)
        hf = sb("hf", [P, 2, S], F32, ffn)
        th = sb("th", [P, 2, S // 2], F32, ffn)
        lgT = th[:].rearrange("p a b -> p (a b)")
        ffn.close()
        moe = ExitStack()
        ew2 = sb("ew2", [P, E, INTER // P, D], F32, moe)
        xt = sb("xt", [P, 2, ROW], F32, moe)
        xtT = sb("xtT", [P, 2, DC, P], F32, moe)
        e_s = sb("e_s", [P, 2, INTER], F32, moe)
        e_h = sb("e_h", [P, 2, INTER], F32, moe)
        e_hT = sb("e_hT", [P, 2, INTER // P, P], F32, moe)
        e_y = sb("e_y", [P, 2, D], F32, moe)
        e_number = sb("e_number", [P, 2], F32, moe)
        e_row = sb("e_row", [P, 2], I32, moe)
        moe.close()
        ffn_room = sb("ffn_room", [P, 17920], F32)
        small = sb("small", [P, 168], F32)

        def norm_buffers(at):
            return (small[:, at:at + 24].rearrange("p (t s) -> p t s", t=NT), small[:, at + 24:at + 32].rearrange("p (t s) -> p t s", t=NT),
                    small[:, at + 32:at + 36])
        stats, mv, var = norm_buffers(0)
        statsb, mvb, varb = norm_buffers(36)
        statst, mvt, vart = norm_buffers(72)
        c_stats, c_mv, c_var = norm_buffers(108)
        rden = small[:, 144:160]
        den = small[:, 160:164]
        rstd = sb("rstd", [P, NT], F32)
        rstdb = sb("rstdb", [P, NT], F32)
        rstdt = sb("rstdt", [P, NT], F32)
        c_rstd = sb("c_rstd", [P, NT], F32)

        mix = ExitStack()
        w_mix = sb("w_mix", [P, 2, 1792], F32R, mix)
        mix.close()
        ones = sb("ones", [P, P], F32)
        R = [sb(f"R{n}", [P, TILES, E], F32) for n in range(14)]
        r16 = [sb(f"r16_{n}", [P, TILES], F32) for n in range(11)]
        r8 = [sb(f"r8_{n}", [P, E], F32) for n in range(8)]
        i8 = [sb(f"i8_{n}", [P, E], I32) for n in range(2)]
        idx = sb("idx", [P, 2, TILES], I32)
        teI = sb("teI", [P, MT], I32)
        teF = [sb(f"teF{n}", [P, MT], F32) for n in range(2)]
        teC = sb("teC", [P, MT, E], F32)
        mix_rest = sb("mix_rest", [P, 936], F32)

        def wmix(s, at, n):
            return w_mix[:, s, at:at + DC * n].rearrange("p (c n) -> p c n", c=DC)
        w_proj = [wmix(s, 0, D) for s in range(2)]
        w_q = [wmix(s, 512, D) for s in range(2)]
        w_kv = [wmix(s, 1024, P) for s in range(2)]
        w_o = [wmix(s, 1280, D) for s in range(2)]

        lin = ExitStack()
        bias = sb("bias", [P, D], F32, lin)
        w_qkv = sb("w_qkv", [P, 2, DC, 3 * D], F32R, lin)
        xn = sb("xn", [P, NT, D], F32, lin)
        qT = sb("qT", [P, DC, S], F32, lin)
        ksb = sb("ksb", [P, NT, D], F32, lin)
        vsb = sb("vsb", [P, NT, DC, P + 1], F32, lin)
        vk = sb("vk", [P, DC, P + 4], F32, lin)
        o0 = xn
        lin.close()
        XN = sb("XN", [P, TILES, ROW], F32)
        SH = sb("SH", [P, TILES, D], F32)

        raw = ExitStack()
        rawA = sb("rawA", [P, 2048], F32, raw)
        rawB = sb("rawB", [P, 2048], F32, raw)
        rawC = sb("rawC", [P, 2048], F32, raw)
        raw.close()
        att = ExitStack()
        Q6 = sb("Q6", [P, H, S], BF16, att)
        K6 = sb("K6", [P, G, S], BF16, att)
        V1 = sb("V1", [P, NT, G, VW], F32, att)
        pq = sb("pq", [P, 3, DC, S], BF16, att)
        pk = sb("pk", [P, 3, S], BF16, att)
        kvs = sb("kvs", [P, S], F32, att)
        sbi = sb("sbi", [P, 2, S], F32, att)
        pr = sb("pr", [P, 3, S], F32, att)
        mxn = sb("mxn", [P, P], F32, att)
        pm = sb("pm", [NT * H, 3, P], BF16, att)
        xnb = sb("xnb", [P, NT, D], F32, att)
        xTb = sb("xTb", [P, 2, DC, S], F32R, att)
        rq = sb("rq", [P, S], F32, att)
        pmr = rq[0:NT * H, 0:P]
        OT = sb("OT", [P, 2, S], F32, att)
        zt = OT[:].rearrange("p g (k d) -> p (g k) d", d=D)
        pad_row = OT[:].rearrange("p g n -> p (g n)")[:, 0:2 * ROW].rearrange("p (x r) -> p x r", x=2)
        rco = sb("rco", [P, NT * REP], F32, att)
        att.close()
        end = ExitStack()
        yb = sb("yb", [P, 2, NT, 2, D], F32, end)
        zc = sb("zc", [P, 2, NT, D], F32, end)
        end.close()
        ew1 = sb("ew1", [P, E, DC, 2 * INTER], F32)

        qd = nc.dram_tensor("q_pieces", (3, D, S), BF16, kind="Internal").ap()
        kd = nc.dram_tensor("k_pieces", (3, G * HD, S), BF16, kind="Internal").ap()
        xs = nc.dram_tensor("x_slots", (MT * P, ROW), F32, kind="Internal").ap()
        ys = nc.dram_tensor("y_rows", (2 * (TILES + 2) * P, D), F32, kind="Internal").ap()

        c_in = sem("const_loaded")
        b_in = sem("bias_loaded")
        x_in = sem("x_loaded")
        raw_in = [sem(f"raw_loaded{n}") for n in range(5)]
        split_hi = sem("weight_hi_written")
        split_lo = sem("weight_lo_written")
        setup = sem("setup_by_vector")
        bfly = sem("butterflies_done")
        hadd = sem("hadamard_product_done")
        hadh = sem("hadamard_hi_written")

        var_a, rstd_a = edge("variance_a", 4), edge("rstd_a", 4)
        xn_a, ps_a = edge("normed_a", 2), edge("psum_a_full", 10)
        ps_f = edge("ffn_up_full", 16)
        xh_a, xl_a = edge("xT_hi_a", 3), edge("xT_lo_a", 3)
        q_a, kv_a, vk_a, o_a, y_a = edge("q_written", 1), edge("kv_written", 2), edge("vk_written", 1), edge("o_written", 2), edge("proj_added", 1)
        th_a, h_a, hh_a, hl_a, dn_a, z_a = edge("tanh_written", 16), edge("h_written", 16), edge("h_hi_written", 8), edge("h_lo_written", 8), edge("h_used", 8), edge("ffn_copied", 1)

        var_b, rstd_b = edge("variance_b", 1), edge("rstd_b", 1)
        var_t, rstd_t = edge("variance_t", 1), edge("rstd_t", 1)
        xn_b, psg_b = edge("normed_b", 1), edge("psum_b_full", 7)
        xh_b, xl_b = edge("xT_hi_b", 2), edge("xT_lo_b", 2)
        qh_b, kh_b, pc_b = edge("q_hi_written", 1), edge("k_hi_written", 1), edge("pieces_written", 2)
        v_b = edge("v_written", 1)
        bo_b = edge("pieces_in_dram", 2, 16)
        q6_b, k6_b = edge("q_packed", 6, 16), edge("k_packed", 6, 16)
        psm_b, mx_b = edge("max_scores_full", 44), edge("max_taken", 44)
        pm_b, m6_b = edge("max_pieces_written", 1), edge("max_packed", 3, 16)
        pss_b, bank_b = edge("scores_full", 44), edge("score_bank_read", 48)
        ex_b, pv_b, pso_b = edge("exp_written", 44), edge("probs_used", 44), edge("heads_summed", 4)
        ot_b, pst_b, on_b = edge("OT_written", 4), edge("OT_transposed", 4), edge("attention_written", 1)
        z_b = edge("attention_added", 1)
        var_c, rstd_c, xn_c = edge("variance_c", 1), edge("rstd_c", 1), edge("normed_c", 1)
        t_c, xh_c, xl_c = edge("xnc_transposed", 1), edge("XT_hi", 1), edge("XT_lo", 1)
        lg_c, lgc_c, lgt_c, L_c = edge("logits_full", 1), edge("logits_copied", 1), edge("logits_transposed", 1), edge("logits_written", 1)
        t_in, pad_set, pad_out, r_in, rt_hi, rt_lo = (sem(n) for n in ("table_loaded", "pad_row_set", "pads_written", "router_loaded", "router_hi", "router_lo"))
        s_in = [sem(f"shared_weight_loaded{n}") for n in range(3)]
        s_hi, s_lo = sem("shared_hi_written"), sem("shared_lo_written")
        chosen, exped, counted, slots = (sem(n) for n in ("experts_chosen", "gap_exponentiated", "counts_full", "slots_written"))
        z_s = edge("shared_output_written", 1)
        b_done = [sem(f"stream_b_done_{n}") for n in ("pe", "act", "dve", "pool")]
        s_done = [sem(f"stream_s_done_{n}") for n in ("pe", "act", "dve", "pool")]
        ew_in = [sem("expert_w1_loaded"), sem("expert_w2_loaded")]
        xt_in = [edge(f"slot_rows_loaded{x}", 1, 16) for x in range(2)]
        tx_d, xT_d, w1_d, s_d, h_d = edge("slot_rows_transposed", 2), edge("xtT_written", 2), edge("expert_up_full", 4), edge("expert_silu_written", 2), edge("expert_h_written", 2)
        th_d, hT_d, w2_d, y_d, row_d = edge("expert_h_transposed", 2), edge("expert_hT_written", 2), edge("expert_down_full", 2), edge("expert_y_written", 2), edge("row_numbers_written", 2)
        number_d, turns = edge("number_written", 2), sem("scatters_begun")
        ysc = [edge(f"rows_scattered{x}", 1, 16, ahead=TILES) for x in range(2)]
        yb_in = [edge(f"y_rows_loaded{x}", 1, 16) for x in range(2)]
        var_e, rstd_e, out_e = edge("variance_e", 2), edge("rstd_e", 2), edge("result_ready", 2)
        y_used = edge("y_rows_used", 2)

        RAW = [(rawA, 1536), (rawB, 1792), (rawC, 2048), (rawA, 2048), (rawB, 2048)]
        HI_LO = [
            [w_qkv[:, s].rearrange("p c n -> p (c n)") for s in range(2)],
            [w_mix[:, s] for s in range(2)],
            [w_up[:, s, 0].rearrange("p c n -> p (c n)") for s in range(2)],
            [w_up[:, s, 1].rearrange("p c n -> p (c n)") for s in range(2)],
            [w_dn[:, s].rearrange("p c n -> p (c n)") for s in range(2)],
        ]

        def tile_of(i, k):
            return ds(i * NT + k, 1)

        PASSES = [(0, 0), (0, 1), (1, 0)]

        def norm_stats(dve, i, src, st, m, v, e_var):
            for k in range(NT):
                dve.bn_stats(st[:, k, :], src(k))
            dve.drain()
            for k in range(NT):
                dve.bn_aggr(m[:, k, :], st[:, k, :])
            dve.drain()
            dve.tensor_scalar(v, m[:, :, 1], EPS_LN, None, ALU.add).then_inc(e_var.sem, 1)

        def norm_apply(dve, k, dst, src, m, r):
            return dve.tensor_scalar(dst, src, m[:, k, 0:1], r[:, k:k + 1], ALU.subtract, ALU.mult)

        def rsqrt(pool, i, k, v, r, e_var, e_rstd):
            e_var.wait(pool, i, k)
            pool.tensor_tensor(r, v, mhalf[:, :], ALU.pow).then_inc(e_rstd.sem, 1)

        def split3(pe, dst, lhs, rhs, first=True, last=True):
            for n, (a, b) in enumerate(PASSES):
                mm = pe.matmul(dst, lhs[a], rhs[b], start=first and n == 0, stop=last and n == 2,
                               skip_group_check=True)
            return mm

        def in_order(order, **streams):
            streams = {name: stream if isinstance(stream, Steps) else Steps(stream) for name, stream in streams.items()}
            for name, step in order:
                if name in streams:
                    streams[name].through(step)

        ALONE_A, ALONE_B = [("a", n) for n in range(23)], [("b", n) for n in range(32)]
        FIRST, TOGETHER, LAST, TAIL, S_FFN = orders()

        def pe_ffn(pe, f, at):
            def down(j):
                hl_a.wait(pe, f, j)
                for k in range(NT):
                    mm = split3(pe, pa[:, 2 + k // 2, (k % 2) * D:(k % 2 + 1) * D], [hT[:, s, j % 2, k * P:(k + 1) * P] for s in range(2)],
                                [w_dn[:, s, j, :] for s in range(2)], j == 0 and k % 2 == 0, j == FC - 1)
                mm.then_inc(dn_a.sem, 1)
                return mm

            for j in range(FC):
                if j >= 1:
                    yield at + j
                for half in range(2):
                    if j >= 1:
                        h_a.wait(pe, f, 2 * (j - 1) + half)
                    for u in range(2):
                        for c in range(DC):
                            mm = split3(pe, pa[:, half, u * D:(u + 1) * D], [w_up[:, s, u, c, j * P:(j + 1) * P] for s in range(2)],
                                        [xT[:, s, c, half * D:(half + 1) * D] for s in range(2)], c == 0, c == 1)
                    mm.then_inc(ps_f.sem, 1)
                if j >= 1:
                    down(j - 1)
            yield at + FC
            down(FC - 1)

        def act_ffn(act, f, at):
            def h_hi(j):
                h_a.wait(act, f, 2 * j + 1)
                if j >= 2:
                    dn_a.wait(act, f, j - 2)
                act.activation(hT[:, 0, j % 2], hf[:, j % 2], ACT.Copy).then_inc(hh_a.sem, 1)

            for j in range(FC):
                if j >= 1:
                    yield at + j
                if j >= 1:
                    h_hi(j - 1)
                for half in range(2):
                    ps_f.wait(act, f, 2 * j + half)
                    act.activation(th[:, half], pa[:, half, 0:D], ACT.Tanh, scale=0.5).then_inc(th_a.sem, 1)
            yield at + FC
            h_hi(FC - 1)

        def dve_ffn(dve, f, at):
            for j in range(FC):
                if j >= 1:
                    yield at + j
                for half in range(2):
                    th_a.wait(dve, f, 2 * j + half)
                    dve.scalar_tensor_tensor(out=th[:, half], in0=th[:, half], scalar=1.0, in1=pa[:, half, 0:D], op0=ALU.add, op1=ALU.mult)
                    dve.drain()
                    if j >= 2 and half == 0:
                        hl_a.wait(dve, f, j - 2)
                    dve.scalar_tensor_tensor(out=hf[:, j % 2, half * D:(half + 1) * D], in0=th[:, half], scalar=0.5, in1=pa[:, half, D:2 * D],
                                             op0=ALU.mult, op1=ALU.mult).then_inc(h_a.sem, 1)

        def pool_ffn(pool, f, at):
            for j in range(FC):
                yield at + 1 + j
                hh_a.wait(pool, f, j)
                pool.tensor_tensor(hT[:, 1, j % 2], hf[:, j % 2], hT[:, 0, j % 2].bitcast(F32), ALU.subtract).then_inc(hl_a.sem, 1)

        def pe_A(pe, i):
            def xs_(c):
                return [xT[:, s, c, :] for s in range(2)]

            def transposes(src, n):
                for c in range(DC):
                    for k in range(NT):
                        mm = pe.transpose(pa[:, 2 * (n % 2) + c, k * P:(k + 1) * P], src[:, k, c * P:(c + 1) * P], ident)
                mm.then_inc(ps_a.sem, 1)

            yield 1
            xn_a.wait(pe, i, 0)
            transposes(xn, 0)
            yield 3
            xh_a.wait(pe, i, 0)
            xl_a.wait(pe, i, 0)
            z_a.wait_prev(pe, i)
            for m in range(DC):
                for c in range(DC):
                    mm = split3(pe, pa[:, 2 + m, :], [w_qkv[:, s, c, m * P:(m + 1) * P] for s in range(2)], xs_(c), c == 0, c == 1)
            mm.then_inc(ps_a.sem, 1)
            for half in range(2):
                yield 4 + half
                if half == 1:
                    q_a.wait(pe, i)
                for kk in range(2):
                    k = 2 * half + kk
                    for c in range(DC):
                        mm = split3(pe, pa[:, 2 * half + kk, :], [xT[:, s, c, k * P:(k + 1) * P] for s in range(2)],
                                    [w_qkv[:, s, c, D:3 * D] for s in range(2)], c == 0, c == 1)
                mm.then_inc(ps_a.sem, 1)
            yield 6
            kv_a.wait(pe, i, 1)
            for c in range(DC):
                for k in range(NT):
                    mm = pe.matmul(pa[:, c, 0:P + 1], ksb[:, k, c * P:(c + 1) * P], vsb[:, k, c, :], start=k == 0, stop=k == NT - 1)
            mm.then_inc(ps_a.sem, 1)
            yield 7
            vk_a.wait(pe, i)
            for half in range(2):
                for kk in range(2):
                    k = 2 * half + kk
                    for c in range(DC):
                        mm = pe.matmul(pa[:, 2 * (1 - half) + kk, c * (P + 4):(c + 1) * (P + 4)], qT[:, c, k * P:(k + 1) * P], vk[:, c, :],
                                       start=True, stop=True, skip_group_check=True)
                mm.then_inc(ps_a.sem, 1)
            yield 8
            o_a.wait(pe, i, 1)
            transposes(o0, 1)
            yield 9
            xh_a.wait(pe, i, 1)
            xl_a.wait(pe, i, 1)
            for k in range(NT):
                for c in range(DC):
                    mm = split3(pe, pa[:, k // 2, (k % 2) * D:(k % 2 + 1) * D], [xT[:, s, c, k * P:(k + 1) * P] for s in range(2)],
                                [w_proj[s][:, c, :] for s in range(2)], c == 0, c == 1)
            mm.then_inc(ps_a.sem, 1)
            yield 11
            xn_a.wait(pe, i, 1)
            transposes(xn, 1)
            yield 12
            xh_a.wait(pe, i, 2)
            xl_a.wait(pe, i, 2)
            yield from pe_ffn(pe, i, 12)

        def act_A(act, i):
            def hi(k, n, slot):
                ps_a.wait(act, i, n)
                act.activation(xT[:, 0], pa[:, 2 * slot:2 * slot + 2, :], ACT.Copy).then_inc(xh_a.sem, 1)

            yield 1
            hi(0, 0, 0)
            yield 3
            ps_a.wait(act, i, 1)
            act.activation(qT[:], pa[:, 2:4, :], ACT.Relu).then_inc(q_a.sem, 1)
            for half in range(2):
                yield 4 + half
                ps_a.wait(act, i, 2 + half)
                src = pa[:, 2 * half:2 * half + 2, :]
                act.activation(ksb[:, 2 * half:2 * half + 2, :], src[:, :, 0:D], ACT.Relu)
                for kk in range(2):
                    v = act.activation(vsb[:, 2 * half + kk, :, 0:P], src[:, kk, D:2 * D].rearrange("p (c n) -> p c n", c=DC), ACT.Copy)
                act.drain().then_inc(kv_a.sem, 1)
            yield 8
            hi(1, 7, 1)
            yield 11
            hi(2, 9, 1)

            yield 12
            yield from act_ffn(act, i, 12)

        def dve_A(dve, i):
            def xtile(k):
                return X[:, tile_of(i, k), :].rearrange("p a d -> p (a d)")

            def lo(k, slot):
                xh_a.wait(dve, i, k)
                dve.tensor_tensor(xT[:, 1], pa[:, 2 * slot:2 * slot + 2, :], xT[:, 0].bitcast(F32), ALU.subtract).then_inc(xl_a.sem, 1)

            yield 0
            norm_stats(dve, i, xtile, stats, mv, var, var_a)
            yield 1
            rstd_a.wait(dve, i, 0)
            for k in range(NT):
                norm_apply(dve, k, xn[:, k], xtile(k), mv, rstd)
            dve.drain().then_inc(xn_a.sem, 1)
            yield 2
            lo(0, 0)
            yield 6
            ps_a.wait(dve, i, 4)
            for c in range(DC):
                dve.tensor_tensor(vk[:, c, 0:P], pa[:, c, 0:P], blk, ALU.mult)
                dve.tensor_copy(den[:, c:c + 1], pa[:, c, P:P + 1])
            dve.drain()
            for c in range(DC):
                dve.tensor_scalar(vk[:, c, P:P + 4], hm4, den[:, c:c + 1], None, ALU.mult)
            dve.drain().then_inc(vk_a.sem, 1)
            for half in range(2):
                if half == 0:
                    yield 7
                ps_a.wait(dve, i, 5 + half)
                src = pa[:, 2 * (1 - half):2 * (1 - half) + 2, :]
                for kk in range(2):
                    o_src = src[:, kk, 0:DC * (P + 4)].rearrange("p (c n) -> p c n", c=DC)
                    r = rden[:, 8 * kk:8 * kk + 8]
                    dve.tensor_scalar(r.rearrange("p (c h) -> p c h", c=DC), o_src[:, :, P:P + 4], EPS_ATT, None, ALU.add)
                dve.drain()
                dve.reciprocal(rden, rden)
                dve.drain()
                for kk in range(2):
                    for c in range(DC):
                        o_src = src[:, kk, c * (P + 4):c * (P + 4) + P].rearrange("p (h e) -> p h e", e=LD)
                        r = rden[:, 8 * kk + 4 * c:8 * kk + 4 * c + 4]
                        dve.tensor_tensor(o0[:, 2 * half + kk, c * P:(c + 1) * P].rearrange("p (h e) -> p h e", e=LD), o_src,
                                          r.unsqueeze(2).to_broadcast([P, 4, LD]), ALU.mult)
                dve.drain().then_inc(o_a.sem, 1)
            yield 8
            lo(1, 1)
            yield 9
            ps_a.wait(dve, i, 8)
            dve.tensor_tensor(xn[:], pa[:, 0:2, :].rearrange("p b (k d) -> p (b k) d", d=D),
                              bias[:].unsqueeze(1).to_broadcast([P, NT, D]), ALU.add).then_inc(y_a.sem, 1)
            dve.drain()
            norm_stats(dve, i, lambda k: xn[:, k], stats, mv, var, var_a)
            yield 10
            rstd_a.wait(dve, i, 1)
            for k in range(NT):
                norm_apply(dve, k, xn[:, k], xn[:, k], mv, rstd)
            dve.drain()
            xb = X[:, ds(i * NT, NT), :]
            dve.tensor_tensor(xb, xb, xn[:], ALU.add)
            dve.drain()
            norm_stats(dve, i, xtile, stats, mv, var, var_a)
            yield 11
            rstd_a.wait(dve, i, 2)
            for k in range(NT):
                norm_apply(dve, k, xn[:, k], xtile(k), mv, rstd)
            dve.drain().then_inc(xn_a.sem, 1)
            lo(2, 1)
            yield 12
            yield from dve_ffn(dve, i, 12)
            yield 21
            dn_a.wait(dve, i, FC - 1)

            def product(k):
                return pa[:, 2 + k // 2, (k % 2) * D:(k % 2 + 1) * D]

            norm_stats(dve, i, product, stats, mv, var, var_a)
            yield 22
            rstd_a.wait(dve, i, 3)
            for k in range(NT):
                norm_apply(dve, k, xn[:, k], product(k), mv, rstd)
            dve.drain().then_inc(z_a.sem, 1)
            dve.tensor_tensor(xb, xb, xn[:], ALU.add)
            dve.drain()

        def pool_A(pool, i):
            for k, at in enumerate((0, 9, 10)):
                yield at
                rsqrt(pool, i, k, var, rstd[:], var_a, rstd_a)
            yield from pool_ffn(pool, i, 12)
            yield 21
            rsqrt(pool, i, 3, var, rstd[:], var_a, rstd_a)

        def units_of(g):
            for kb in range(NT):
                hh = {0: 1, 1: 1, 2: 2, 3: 4}[kb]
                for h0 in range(0, REP, hh):
                    yield kb, h0, hh
        SEQ = []
        for g in range(G):
            for u, (kb, h0, hh) in enumerate(units_of(g)):
                SEQ.append(("S", g, kb, h0, hh))
                if u == 5 and g > 0:
                    SEQ.append(("T", g - 1))
        SEQ.append(("T", G - 1))
        MAXU = [(g, qb, h0, {0: 4, 1: 2, 2: 1, 3: 1}[qb]) for g in range(G) for qb in range(NT)
                for h0 in range(0, REP, {0: 4, 1: 2, 2: 1, 3: 1}[qb])]

        def pe_B(pe, i):
            yield 1
            xn_b.wait(pe, i)
            for c in range(DC):
                for k in range(NT):
                    mm = pe.transpose(pb[:, c, k * P:(k + 1) * P], xnb[:, k, c * P:(c + 1) * P], ident)
            mm.then_inc(psg_b.sem, 1)
            yield 3
            z_b.wait_prev(pe, i)
            xh_b.wait(pe, i, 0)
            xl_b.wait(pe, i, 0)
            for m in range(DC):
                for c in range(DC):
                    mm = split3(pe, pb[:, 2 + m, :], [w_q[s][:, c, m * P:(m + 1) * P] for s in range(2)],
                                [xTb[:, s, c, :] for s in range(2)], c == 0, c == 1)
            mm.then_inc(psg_b.sem, 1)
            for c in range(DC):
                mm = split3(pe, pb[:, 0, :], [w_kv[s][:, c, :] for s in range(2)], [xTb[:, s, c, :] for s in range(2)], c == 0, c == 1)
            mm.then_inc(psg_b.sem, 1)
            yield 4
            kh_b.wait(pe, i)
            for k in range(NT):
                mm = pe.transpose(pb[:, 1, k * P:(k + 1) * P], kvs[:, k * P:(k + 1) * P], ident)
            mm.then_inc(psg_b.sem, 1)
            yield 5
            q6_b.wait(pe, i, 5)
            k6_b.wait(pe, i, 5)
            v_b.wait(pe, i)
            pc_b.wait(pe, i, 1)
            for n, (g, qb, h0, hh) in enumerate(MAXU):
                if n % 4 == 0:
                    yield 5 + n // 4
                if n >= 2:
                    mx_b.wait(pe, i, n - 2)
                w = (qb + 1) * P
                for x in range(hh):
                    h = g * REP + h0 + x
                    pe.matmul(pb[:, n % 2, x * w:(x + 1) * w], Q6[0:KROWS, h, qb * P:(qb + 1) * P], K6[0:KROWS, g, 0:w],
                              start=True, stop=False, skip_group_check=True)
                    mm = pe.matmul(pb[:, n % 2, x * w + qb * P:(x + 1) * w], identb[:], maskb[:], start=False, stop=True, skip_group_check=True)
                mm.then_inc(psm_b.sem, 1)
            yield 16
            mx_b.wait(pe, i, len(MAXU) - 1)
            pe.transpose(pb[:, 2, 0:P], mxn[:], ident).then_inc(psg_b.sem, 1)
            yield 17
            m6_b.wait(pe, i, 2)

            def front(n):
                u = SEQ[n]
                if n >= 2:
                    bank_b.wait(pe, i, n - 2)
                if u[0] == "S":
                    _, g, kb, h0, hh = u
                    w = S - kb * P
                    pe.matmul(pb[:, n % 2, 0:hh * w], K6[0:KROWS + 3, g, kb * P:(kb + 1) * P],
                              Q6[0:KROWS + 3, g * REP + h0:g * REP + h0 + hh, kb * P:S], start=True, stop=True).then_inc(pss_b.sem, 1)
                else:
                    g = u[1]
                    ot_b.wait(pe, i, g)
                    for k in range(NT):
                        mm = pe.transpose(pb[:, n % 2, k * P:(k + 1) * P], OT[:, g % 2, k * P:(k + 1) * P], ident)
                    mm.then_inc(pst_b.sem, 1)

            s_at = 0
            front(0)
            front(1)
            for n, u in enumerate(SEQ[:-1]):
                if n % 4 == 0:
                    yield 17 + n // 4
                if n + 2 < len(SEQ) - 1:
                    front(n + 2)
                if u[0] == "S":
                    _, g, kb, h0, hh = u
                    w = S - kb * P
                    ex_b.wait(pe, i, s_at)
                    if kb == 0 and h0 == 0 and g >= 2:
                        ot_b.wait(pe, i, g - 2)
                    for x in range(hh):
                        hq = h0 + x
                        mm = pe.matmul(pb[hq * VW:(hq + 1) * VW, 2 + g % 2, kb * P:S], V1[:, kb, g, :], pr[:, s_at % 3, x * w:(x + 1) * w],
                                       start=kb == 0, stop=kb == NT - 1, skip_group_check=True)
                    s_at += 1
                    mm.then_inc(pv_b.sem, 1)
                    if kb == NT - 1:
                        pe.drain().then_inc(pso_b.sem, 1)
            front(len(SEQ) - 1)

        def pe_B_tail(pe, i):
            yield 29
            on_b.wait(pe, i)
            for c in range(DC):
                for k in range(NT):
                    mm = pe.transpose(pb[:, c, k * P:(k + 1) * P], xnb[:, k, c * P:(c + 1) * P], ident)
            mm.then_inc(psg_b.sem, 1)
            yield 30
            xh_b.wait(pe, i, 1)
            xl_b.wait(pe, i, 1)
            ot_b.wait(pe, i, G - 1)
            for k in range(NT):
                for c in range(DC):
                    mm = split3(pe, pb[:, 2 + k // 2, (k % 2) * D:(k % 2 + 1) * D], [xTb[:, s, c, k * P:(k + 1) * P] for s in range(2)],
                                [w_o[s][:, c, :] for s in range(2)], c == 0, c == 1)
            mm.then_inc(psg_b.sem, 1)

        def act_B(act, i):
            yield 1
            psg_b.wait(act, i, 0)
            act.activation(xTb[:, 0], pb[:, 0:2, :], ACT.Copy).then_inc(xh_b.sem, 1)
            yield 3
            psg_b.wait(act, i, 1)
            act.activation(pq[:, 0], pb[:, 2:4, :], ACT.Copy, scale=HD ** -0.5).then_inc(qh_b.sem, 1)
            psg_b.wait(act, i, 2)
            act.activation(pk[:, 0], pb[:, 0, :], ACT.Copy)
            act.activation(kvs[:], pb[:, 0, :], ACT.Copy)
            act.drain().then_inc(kh_b.sem, 1)
            s_at = 0
            for n, u in enumerate(SEQ):
                if n % 4 == 0:
                    yield 17 + n // 4
                if u[0] != "S":
                    continue
                _, g, kb, h0, hh = u
                w = S - kb * P
                bank_b.wait(act, i, n)
                if s_at >= 3:
                    pv_b.wait(act, i, s_at - 3)
                act.activation(pr[:, s_at % 3, 0:hh * w], sbi[:, s_at % 2, 0:hh * w], ACT.Exp).then_inc(ex_b.sem, 1)
                s_at += 1
                if kb == 0 and h0 == 1 and g > 0:
                    copy_OT(act, i, g - 1)
            copy_OT(act, i, G - 1)

        def act_B_tail(act, i):
            yield 29
            psg_b.wait(act, i, 5)
            act.activation(xTb[:, 0], pb[:, 0:2, :], ACT.Copy).then_inc(xh_b.sem, 1)

        def copy_OT(act, i, g):
            pso_b.wait(act, i, g)
            act.activation(OT[:, g % 2], pb[:, 2 + g % 2, :], ACT.Copy).then_inc(ot_b.sem, 1)

        def dve_B(dve, i):
            def xtile(k):
                return X[:, tile_of(i, k), :].rearrange("p a d -> p (a d)")

            yield 0
            norm_stats(dve, i, xtile, statsb, mvb, varb, var_b)
            yield 1
            rstd_b.wait(dve, i, 0)
            for k in range(NT):
                norm_apply(dve, k, xnb[:, k], xtile(k), mvb, rstdb)
            dve.drain().then_inc(xn_b.sem, 1)
            yield 2
            xh_b.wait(dve, i, 0)
            dve.tensor_tensor(xTb[:, 1], pb[:, 0:2, :], xTb[:, 0].bitcast(F32), ALU.subtract).then_inc(xl_b.sem, 1)
            yield 3
            qh_b.wait(dve, i)
            for c in range(DC):
                dve.scalar_tensor_tensor(out=rq[:], in0=pb[:, 2 + c, :], scalar=HD ** -0.5, in1=pq[:, 0, c], op0=ALU.mult, op1=ALU.subtract)
                dve.drain()
                dve.tensor_copy(pq[:, 1, c], rq[:])
                dve.drain()
                dve.tensor_tensor(pq[:, 2, c], rq[:], pq[:, 1, c], ALU.subtract)
                dve.drain()
            dve.drain().then_inc(pc_b.sem, 1)
            kh_b.wait(dve, i)
            dve.tensor_tensor(rq[:], pb[:, 0, :], pk[:, 0], ALU.subtract)
            dve.drain()
            dve.tensor_copy(pk[:, 1], rq[:])
            dve.drain()
            dve.tensor_tensor(pk[:, 2], rq[:], pk[:, 1], ALU.subtract).then_inc(pc_b.sem, 1)
            yield 4
            psg_b.wait(dve, i, 3)
            dve.tensor_copy(V1[:, :, :, 0:HD], pb[:, 1, :].rearrange("p (k z g d) -> p k z g d", k=NT, z=2, g=G)[:, :, 1]).then_inc(v_b.sem, 1)
            for n, (g, qb, h0, hh) in enumerate(MAXU):
                if n % 4 == 0:
                    yield 5 + n // 4
                psm_b.wait(dve, i, n)
                h = g * REP + h0
                dve.tensor_reduce(mxn[:, 0:NT * H].rearrange("p (h k) -> p k h", k=NT)[:, qb, h:h + hh], pb[:, n % 2, 0:hh * (qb + 1) * P].rearrange("p (h w) -> p h w", h=hh), AX, ALU.max,
                                  negate=True).then_inc(mx_b.sem, 1)
            yield 16
            psg_b.wait(dve, i, 4)
            mT = pb[0:NT * H, 2, 0:P]
            dve.tensor_copy(pm[:, 0], mT)
            dve.drain()
            dve.tensor_tensor(pmr, mT, pm[:, 0], ALU.subtract)
            dve.drain()
            dve.tensor_copy(pm[:, 1], pmr)
            dve.drain()
            dve.tensor_tensor(pm[:, 2], pmr, pm[:, 1], ALU.subtract).then_inc(pm_b.sem, 1)
            s_at = 0
            for n, u in enumerate(SEQ):
                if n % 4 == 0:
                    yield 17 + n // 4
                if u[0] == "S":
                    _, g, kb, h0, hh = u
                    w = S - kb * P
                    pss_b.wait(dve, i, s_at)
                    if s_at >= 2:
                        ex_b.wait(dve, i, s_at - 2)
                    for x in range(hh):
                        ins = dve.scalar_tensor_tensor(out=sbi[:, s_at % 2, x * w:(x + 1) * w], in0=dist[:, 0:w], scalar=-SLOPES[g * REP + h0 + x],
                                                       in1=pb[:, n % 2, x * w:(x + 1) * w], op0=ALU.mult, op1=ALU.add)
                    ins.then_inc(bank_b.sem, 1)
                    s_at += 1
                else:
                    g = u[1]
                    pst_b.wait(dve, i, g)
                    src = pb[:, n % 2, :].rearrange("p (k h e) -> p k h e", k=NT, h=REP)
                    dve.reciprocal(rco[:].rearrange("p (k h) -> p k h", k=NT), src[:, :, :, HD])
                    dve.drain()
                    ins = dve.tensor_tensor(xnb[:, :, g * REP * HD:(g + 1) * REP * HD].rearrange("p k (h e) -> p k h e", e=HD), src[:, :, :, 0:HD],
                                            rco[:].rearrange("p (k h) -> p k h", k=NT).unsqueeze(3).to_broadcast([P, NT, REP, HD]), ALU.mult)
                    ins.then_inc(bank_b.sem, 1)
            dve.drain().then_inc(on_b.sem, 1)

        def dve_B_tail(dve, i):
            yield 29
            xh_b.wait(dve, i, 1)
            dve.tensor_tensor(xTb[:, 1], pb[:, 0:2, :], xTb[:, 0].bitcast(F32), ALU.subtract).then_inc(xl_b.sem, 1)
            yield 30
            psg_b.wait(dve, i, 6)

            def product(k):
                return pb[:, 2 + k // 2, (k % 2) * D:(k % 2 + 1) * D]

            norm_stats(dve, i, product, statst, mvt, vart, var_t)
            yield 31
            rstd_t.wait(dve, i)
            for k in range(NT):
                norm_apply(dve, k, zt[:, k], product(k), mvt, rstdt)
            dve.drain().then_inc(z_b.sem, 1)
            xb = X[:, ds(i * NT, NT), :]
            dve.tensor_tensor(xb, xb, zt, ALU.add)
            dve.drain()

        def pool_B(pool, i):
            yield 0
            rsqrt(pool, i, 0, varb, rstdb[:], var_b, rstd_b)

        def pool_B_tail(pool, i):
            yield 30
            rsqrt(pool, i, 0, vart, rstdt[:], var_t, rstd_t)

        QP, KP = [0, 0, 1, 1, 0, 2], [0, 1, 0, 1, 2, 0]

        def sp_B(sp, i):
            yield 3
            pc_b.wait(sp, i, 0)
            sp.dma_start(qd.rearrange("z (c p) n -> p z c n", p=P), pq[:]).then_inc(bo_b.sem, 16)
            bo_b.wait(sp, i, 0)
            for r in range(6):
                sp.dma_start(Q6[r * HD:(r + 1) * HD], qd[QP[r]].rearrange("(h d) n -> d h n", d=HD)).then_inc(q6_b.sem, 16)
            pc_b.wait(sp, i, 1)
            sp.dma_start(kd.rearrange("z p n -> p z n"), pk[0:G * HD]).then_inc(bo_b.sem, 16)
            bo_b.wait(sp, i, 1)
            for r in range(6):
                sp.dma_start(K6[r * HD:(r + 1) * HD], kd[KP[r]].rearrange("(g d) n -> d g n", d=HD)).then_inc(k6_b.sem, 16)
            yield 16
            pm_b.wait(sp, i)
            for r in range(3):
                sp.dma_start(Q6[KROWS + r:KROWS + r + 1].rearrange("p h (k q) -> p (h k) q", k=NT), pm[:, r, :]).then_inc(m6_b.sem, 16)

        def pe_S(pe, i):
            yield 1
            xn_c.wait(pe, i)
            for c in range(DC):
                for k in range(NT):
                    mm = pe.transpose(pa[:, c, k * P:(k + 1) * P], XN[:, i * NT + k, c * P:(c + 1) * P], ident)
            mm.then_inc(t_c.sem, 1)
            yield 3
            xh_c.wait(pe, i)
            xl_c.wait(pe, i)
            if i == 0:
                z_a.wait(pe, B - 1)
                pe.wait_ge(rt_lo, 1)
            else:
                z_s.wait(pe, i - 1)
            for c in range(DC):
                mm = split3(pe, pa[:, 2, :], [rt[:, s, c, :] for s in range(2)], [xT[:, s, c, :] for s in range(2)], c == 0, c == 1)
            mm.then_inc(lg_c.sem, 1)
            yield 4
            lgc_c.wait(pe, i)
            for k in range(NT):
                mm = pe.transpose(pa[:, 3, k * P:(k + 1) * P], lgT[:, k * P:(k + 1) * P], ident)
            mm.then_inc(lgt_c.sem, 1)
            yield 5
            if i == 0:
                pe.wait_ge(s_lo, 3)
            L_c.wait(pe, i)
            yield from pe_ffn(pe, B + i, 5)

        def act_S(act, i):
            yield 1
            t_c.wait(act, i)
            act.activation(xT[:, 0], pa[:, 0:2, :], ACT.Copy).then_inc(xh_c.sem, 1)
            yield 3
            lg_c.wait(act, i)
            act.activation(lgT, pa[:, 2, :], ACT.Copy).then_inc(lgc_c.sem, 1)
            yield 5
            yield from act_ffn(act, B + i, 5)
            yield 14
            dn_a.wait(act, B + i, FC - 1)
            act.activation(SH[:, i * NT:(i + 1) * NT, :], pa[:, 2:4, :].rearrange("p b (k d) -> p (b k) d", d=D), ACT.Copy).then_inc(z_s.sem, 1)

        def dve_S(dve, i):
            yield 0
            if i == 0:
                dve.memset(XN[:, :, D + 2:ROW], 0.0)
            norm_stats(dve, i, lambda k: X[:, i * NT + k, :], c_stats, c_mv, c_var, var_c)
            yield 1
            rstd_c.wait(dve, i)
            for k in range(NT):
                norm_apply(dve, k, XN[:, i * NT + k, 0:D], X[:, i * NT + k, :], c_mv, c_rstd)
            dve.drain().then_inc(xn_c.sem, 1)
            yield 2
            xh_c.wait(dve, i)
            dve.tensor_tensor(xT[:, 1], pa[:, 0:2, :], xT[:, 0].bitcast(F32), ALU.subtract).then_inc(xl_c.sem, 1)
            yield 4
            lgt_c.wait(dve, i)
            dve.tensor_copy(L[:, i * NT:(i + 1) * NT, :], pa[:, 3, :].rearrange("p (k e) -> p k e", k=NT)[:, :, 0:E]).then_inc(L_c.sem, 1)
            yield 5
            yield from dve_ffn(dve, B + i, 5)

        def pool_S(pool, i):
            yield 0
            rsqrt(pool, i, 0, c_var, c_rstd[:], var_c, rstd_c)
            yield from pool_ffn(pool, B + i, 5)

        def act_W(act):
            for n in range(3):
                yield n
                act.wait_ge(s_in[n], 16)
                act.activation(SHARED[n][0], SHARED_RAW[n], ACT.Copy).then_inc(s_hi, 1)

        def dve_W(dve):
            for n in range(3):
                yield n
                dve.wait_ge(s_hi, n + 1)
                dve.tensor_tensor(SHARED[n][1], SHARED_RAW[n], SHARED[n][0].bitcast(F32), ALU.subtract).then_inc(s_lo, 1)

        def pool_scatter(pool):
            for n in range(TILES):
                if n % 2 == 0:
                    yield n // 2
                for k in range(2):
                    pool.indirect_dma_start(xs, bass.IndirectOffsetOnAxis(ap=idx[:, k, n:n + 1], axis=0), XN[:, n, :], None).then_inc(ysc[k].sem, 16)

        def over_experts(a):
            return a.unsqueeze(2).to_broadcast([P, TILES, E])

        def over_tiles(a):
            return a.unsqueeze(1).to_broadcast([P, TILES, E])

        def dve_route(dve):
            def choose(logits, best, equal, key, kbest, mask):
                dve.tensor_reduce(best[:], logits[:], AX, ALU.max)
                dve.drain()
                dve.tensor_tensor(equal[:], logits[:], over_experts(best[:]), ALU.is_equal)
                dve.drain()
                dve.tensor_tensor(key[:], equal[:], over_tiles(ehigh), ALU.mult)
                dve.drain()
                dve.tensor_reduce(kbest[:], key[:], AX, ALU.max)
                dve.drain()
                dve.tensor_tensor(mask[:], key[:], over_experts(kbest[:]), ALU.is_equal)
                dve.drain()

            dve.memset(ones[:], 1.0)
            M1, M2, both = R[2], R[6], R[7]
            choose(L, r16[0], R[0], R[1], r16[1], M1)
            dve.scalar_tensor_tensor(out=R[3][:], in0=M1[:], scalar=-3.0e38, in1=L[:], op0=ALU.mult, op1=ALU.add)
            dve.drain()
            choose(R[3], r16[2], R[4], R[5], r16[3], M2)
            dve.tensor_tensor(r16[4][:], r16[2][:], r16[0][:], ALU.subtract)
            dve.tensor_tensor(both[:], M1[:], M2[:], ALU.add)
            dve.tensor_scalar(XN[:, :, D + 1], r16[1][:], -1.0, float(E), ALU.mult, ALU.add)
            dve.tensor_copy(XN[:, :, D], tok2)
            dve.drain().then_inc(chosen, 1)
            dve.wait_ge(counted, 1)
            total, inc = R[8], R[10]
            dve.tensor_copy(total[:], pb[:, 3, 0:TILES * E].rearrange("p (t e) -> p t e", e=E))
            dve.drain()
            src = total
            for n, dst in enumerate((R[9], R[10], R[11], R[10])):
                w = 1 << n
                dve.tensor_tensor(dst[:, w:], src[:, w:], src[:, :TILES - w], ALU.add)
                dve.tensor_copy(dst[:, 0:w], src[:, 0:w])
                dve.drain()
                src = dst
            dve.tensor_scalar(r8[0][:], inc[:, TILES - 1, :], float(P - 1), None, ALU.add)
            dve.drain()
            dve.tensor_copy(i8[0][:], r8[0][:])
            dve.drain()
            dve.tensor_scalar(i8[1][:], i8[0][:], 7, None, ALU.logical_shift_right)
            dve.drain()
            dve.tensor_copy(r8[1][:], i8[1][:])
            dve.drain()
            src = r8[1]
            for n, dst in enumerate((r8[2], r8[3], r8[4])):
                w = 1 << n
                dve.tensor_tensor(dst[:, w:], src[:, w:], src[:, :E - w], ALU.add)
                dve.tensor_copy(dst[:, 0:w], src[:, 0:w])
                dve.drain()
                src = dst
            end = r8[4]
            dve.tensor_tensor(r8[5][:], end[:], r8[1][:], ALU.subtract)
            dve.tensor_tensor(R[12][:], inc[:], total[:], ALU.subtract)
            dve.tensor_tensor(teC[:], tile_no.unsqueeze(2).to_broadcast([P, MT, E]), end[:].unsqueeze(1).to_broadcast([P, MT, E]), ALU.is_ge)
            dve.drain()
            dve.tensor_reduce(teF[0][:], teC[:], AX, ALU.add)
            dve.tensor_scalar(r8[6][:], r8[5][:], float(P), None, ALU.mult)
            dve.tensor_tensor(R[13][:], R[12][:], pb[:, 2, 0:TILES * E].rearrange("p (t e) -> p t e", e=E), ALU.add)
            dve.drain()
            dve.tensor_scalar(teF[1][:], teF[0][:], float(E - 1), None, ALU.min)
            dve.tensor_tensor(R[11][:], R[13][:], over_tiles(r8[6][:]), ALU.add)
            dve.drain()
            dve.tensor_copy(teI[:], teF[1][:])
            for k, m in enumerate((M1, M2)):
                dve.tensor_tensor(R[k][:], R[11][:], m[:], ALU.mult)
            dve.drain()
            for k in range(2):
                dve.tensor_reduce(r16[4 * k][:] if k == 0 else r16[3][:], R[k][:], AX, ALU.add)
            dve.drain()
            dve.tensor_copy(idx[:, 0, :], r16[0][:])
            dve.tensor_copy(idx[:, 1, :], r16[3][:])
            dve.drain().then_inc(slots, 1)
            dve.wait_ge(exped, 1)
            dve.tensor_scalar(r16[6][:], r16[5][:], 1.0, None, ALU.add)
            dve.drain()
            dve.reciprocal(r16[7][:], r16[6][:])
            dve.drain()
            dve.tensor_tensor(r16[8][:], r16[5][:], r16[7][:], ALU.mult)
            dve.drain()

        def before(n, k=1):
            for _ in range(k):
                n = (n[0], 0) if n[1] else (n[0] - 1, 1)
            return n

        def after(n):
            return (n[0] + 1, 0) if n[1] else (n[0], 1)

        def expert_of(pe, n):
            return pe.value_load(teI[0:1, ds(2 * n[0] + n[1], 1)], min_val=0, max_val=E - 1)

        def pe_slot_rows(pe, n, bank_new=False):
            m, x = n
            xt_in[x].wait(pe, m)
            if not bank_new:
                y_d.wait(pe, m - 2, x)
            for c in range(DC):
                mm = pe.transpose(pb[:, x, c * P:(c + 1) * P], xt[:, x, c * P:(c + 1) * P], ident)
            mm.then_inc(tx_d.sem, 1)

        def pe_step(pe, n, up, down, rows=False):
            m, x = n
            m1, x1 = before(n)

            def w1(u):
                for c in range(DC):
                    mm = pe.matmul(pa[:, 2 * x + u, :], xtT[:, x, c, :], ew1[:, ds(te, 1), c, u * INTER:(u + 1) * INTER].rearrange("p a n -> p (a n)"),
                                   start=c == 0, stop=c == 1)
                mm.then_inc(w1_d.sem, 1)

            if up:
                te = expert_of(pe, n)
                xT_d.wait(pe, m, x)
                h_d.wait(pe, m - 1, x)
                w1(0)
            if down:
                te1 = expert_of(pe, (m1, x1))
                h_d.wait(pe, m1, x1)
                hT_d.wait(pe, m1 - 1, x1)
                for q in range(INTER // P):
                    mm = pe.transpose(pb[:, 2 + x1, q * P:(q + 1) * P], e_h[:, x1, q * P:(q + 1) * P], ident)
                mm.then_inc(th_d.sem, 1)
            if up:
                w1(1)
            if down:
                hT_d.wait(pe, m1, x1)
                if rows:
                    xT_d.wait(pe, *after(n))
                for q in range(INTER // P):
                    mm = pe.matmul(pb[:, x1, D:2 * D], e_hT[:, x1, q, :], ew2[:, ds(te1, 1), q, :].rearrange("p a n -> p (a n)"), start=q == 0, stop=q == INTER // P - 1)
                mm.then_inc(w2_d.sem, 1)

        def pe_experts(pe, n, first=False, last=False):
            if first:
                pe_slot_rows(pe, n, True)
            if not last:
                pe_slot_rows(pe, after(n), first)
            pe_step(pe, n, True, not first, not last)
            if last:
                pe_step(pe, after(n), False, True)

        def act_experts(act, n, first=False, last=False):
            def rows(n):
                m, x = n
                tx_d.wait(act, m, x)
                w1_d.wait(act, m - 1, 2 * x + 1)
                act.activation(xtT[:, x], pb[:, x, 0:D].rearrange("p (c n) -> p c n", c=DC), ACT.Copy).then_inc(xT_d.sem, 1)

            def result(n):
                m, x = n
                w2_d.wait(act, m, x)
                ysc[x].wait(act, m - 1)
                act.activation(e_y[:, x], pb[:, x, D:2 * D], ACT.Copy).then_inc(y_d.sem, 1)

            if first:
                rows(n)
            if not last:
                rows(after(n))
            m, x = n
            w1_d.wait(act, m, 2 * x)
            act.activation(e_s[:, x], pa[:, 2 * x, :], ACT.Silu).then_inc(s_d.sem, 1)
            if not first:
                result(before(n))
            if last:
                result(n)

        def dve_experts(dve, n, first=False, last=False):
            def number(n):
                m, x = n
                xt_in[x].wait(dve, m)
                dve.tensor_scalar(e_number[:, x:x + 1], xt[:, x, D + 1:D + 2], teF[1][:, ds(2 * m + x, 1)], xt[:, x, D:D + 1],
                                  ALU.not_equal, ALU.add).then_inc(number_d.sem, 1)

            def hidden_T(n):
                m, x = n
                th_d.wait(dve, m, x)
                dve.tensor_copy(e_hT[:, x], pb[:, 2 + x, :].rearrange("p (q n) -> p q n", n=P)).then_inc(hT_d.sem, 1)

            def row(n):
                m, x = n
                dve.drain()
                ysc[x].wait(dve, m - 1)
                dve.tensor_copy(e_row[:, x:x + 1], e_number[:, x:x + 1]).then_inc(row_d.sem, 1)
                dve.drain()

            m, x = n
            if first:
                number(n)
            else:
                row(before(n))
            if not last:
                number(after(n))
            if not first:
                hidden_T(before(n))
            w1_d.wait(dve, m, 2 * x + 1)
            s_d.wait(dve, m, x)
            dve.tensor_tensor(e_h[:, x], e_s[:, x], pa[:, 2 * x + 1, :], ALU.mult).then_inc(h_d.sem, 1)
            if last:
                row(n)
                hidden_T(n)

        def pool_experts(pool, n, first=False, last=False):
            def scatter(n):
                m, x = n
                row_d.wait(pool, m, x)
                y_d.wait(pool, m, x)
                pool.sem_inc(turns, 1)
                pool.indirect_dma_start(ys, bass.IndirectOffsetOnAxis(ap=e_row[:, x:x + 1], axis=0), e_y[:, x, :], None).then_inc(ysc[x].sem, 16)

            if not first:
                scatter(before(n))
            if last:
                scatter(n)

        def sp_experts(sp, n):
            m, x = n
            tx_d.wait(sp, m - 1, x)
            number_d.wait(sp, m - 1, x)
            sp.dma_start(xt[:, x, :], xs[ds((2 * m + x) * P, P), :]).then_inc(xt_in[x].sem, 16)

        def all_slot_tiles(engine, steps):
            steps(engine, (0, 0), first=True)
            with engine.Fori(0, MT // 2 - 1) as m:
                steps(engine, (m, 1))
                steps(engine, (m + 1, 0))
            steps(engine, (MT // 2 - 1, 1), last=True)

        def dve_result(dve, p):
            for x in range(2):
                yb_in[x].wait(dve, p)
                base = 2 * NT * p + x * NT
                def w(r, k):
                    return r[:, ds(base + k, 1)]
                for k in range(NT):
                    dve.scalar_tensor_tensor(out=zc[:, x, k], in0=yb[:, x, k, 0], scalar=w(r16[7], k), in1=SH[:, ds(base + k, 1), :].rearrange("p a d -> p (a d)"),
                                             op0=ALU.mult, op1=ALU.add)
                dve.drain()
                for k in range(NT):
                    dve.scalar_tensor_tensor(out=zc[:, x, k], in0=yb[:, x, k, 1], scalar=w(r16[8], k), in1=zc[:, x, k], op0=ALU.mult, op1=ALU.add)
                dve.drain().then_inc(y_used.sem, 1)
                norm_stats(dve, p, lambda k: zc[:, x, k], c_stats, c_mv, c_var, var_e)
                rstd_e.wait(dve, p, x)
                for k in range(NT):
                    norm_apply(dve, k, zc[:, x, k], zc[:, x, k], c_mv, c_rstd)
                dve.drain()
                xb = X[:, ds(base, NT), :]
                dve.tensor_tensor(xb, xb, zc[:, x], ALU.add).then_inc(out_e.sem, 1)
                dve.drain()

        def sp_result(sp, p):
            for x in range(2):
                y_used.wait_prev(sp, p, x)
                sp.dma_start(yb[:, x], ys[ds((2 * p + x) * 2 * S, 2 * S), :].rearrange("(t p k) d -> p t k d", p=P, k=2)).then_inc(yb_in[x].sem, 16)

        out_sem = sem("out_written")
        block = ctx.enter_context(nc.Block())

        def done(eng, flag):
            eng.drain().then_inc(flag, 1)

        SHARED = [[w_up[:, s, u].rearrange("p c n -> p (c n)") for s in range(2)] for u in range(2)] + \
                 [[w_dn[:, s].rearrange("p c n -> p (c n)") for s in range(2)]]
        SHARED_RAW = [up_raw[:, 1, u].rearrange("p c n -> p (c n)") for u in range(2)] + [dn_raw[:, 1].rearrange("p c n -> p (c n)")]

        @block.sync
        def _(sp):
            sp.dma_start(const[:], t["const"]).then_inc(c_in, 16)
            sp.dma_start(table[:], t["table"]).then_inc(t_in, 16)
            sp.dma_start(rt_raw[:, 1].rearrange("p c n -> p (c n)"), t["router"]).then_inc(r_in, 16)
            for n, (r, w) in enumerate(RAW):
                if n == 3:
                    sp.wait_ge(split_lo, 1)
                if n == 4:
                    sp.wait_ge(split_lo, 2)
                sp.dma_start(r[:, 0:w], t[f"raw{n}"]).then_inc(raw_in[n], 16)
            for e in (bo_b, q6_b, k6_b, m6_b):
                e.open(sp)
            sp.wait_ge(pad_set, 1)
            for x in range(2):
                sp.dma_start(xs.rearrange("(t x p) r -> x p t r", x=2, p=P)[x], pad_row[:, x].unsqueeze(1).to_broadcast([P, MT // 2, ROW])).then_inc(pad_out, 16)
            with sp.Fori(0, B - 1) as i:
                in_order(ALONE_B, b=sp_B(sp, i))
            dn_a.wait(sp, B - 1, FC - 1)
            for n in range(3):
                sp.dma_start(SHARED_RAW[n], t[f"shared{n}"]).then_inc(s_in[n], 16)
            in_order(ALONE_B, b=sp_B(sp, B - 1))
            for n in range(4):
                sp.wait_ge(b_done[n], 1)
            sp.dma_start(ew1[:].rearrange("p e c n -> p (e c n)"), t["expert1"]).then_inc(ew_in[0], 16)
            for n in range(4):
                sp.wait_ge(s_done[n], 1)
            sp.dma_start(ew2[:].rearrange("p e c n -> p (e c n)"), t["expert2"]).then_inc(ew_in[1], 16)
            for e in xt_in + yb_in:
                e.open(sp)
            for k in range(2):
                sp.wait_ge(ysc[k].sem, 16 * TILES)
            with sp.Fori(0, MT // 2) as m:
                for x in range(2):
                    sp_experts(sp, (m, x))
            for x in range(2):
                ysc[x].wait(sp, MT // 2 - 1)
            with sp.Fori(0, B // 2) as p:
                sp_result(sp, p)

        @block.scalar
        def _(act):
            act.dma_start(X[:], t["x"].rearrange("(t p) d -> p t d", p=P)).then_inc(x_in, 16)
            act.dma_start(bias[:], t["b_proj"].unsqueeze(0).to_broadcast([P, D])).then_inc(b_in, 16)
            for n in range(4):
                act.wait_ge(raw_in[n], 16)
                act.activation(HI_LO[n][0], RAW[n][0][:, 0:RAW[n][1]], ACT.Copy).then_inc(split_hi, 1)
            act.wait_ge(r_in, 16)
            act.activation(rt[:, 0], rt_raw[:, 1], ACT.Copy).then_inc(rt_hi, 1)
            for q in range(2):
                act.wait_ge(hadd, q + 1)
                act.activation(w_dn[:, 0, 4 * q:4 * q + 4].rearrange("p a d -> p (a d)"), pa[:, 2 * q:2 * q + 2, :], ACT.Copy, scale=1 / 32).then_inc(hadh, 1)
            for e in (xh_a, q_a, kv_a, th_a, hh_a, xh_b, qh_b, kh_b, ex_b, ot_b, xh_c, lgc_c, z_s, xT_d, s_d, y_d):
                e.open(act)
            in_order(ALONE_A, a=act_A(act, 0))
            act.wait_ge(pad_out, 32)
            in_order(FIRST, a=act_A(act, 1), b=act_B(act, 0))
            with act.Fori(1, B - 1) as i:
                in_order(TOGETHER, c=act_B_tail(act, i - 1), a=act_A(act, i + 1), b=act_B(act, i))
            third_S, last_S = Steps(act_S(act, B - 2)), Steps(act_S(act, B - 1))
            in_order(LAST, c=act_B_tail(act, B - 2), b=act_B(act, B - 1), s=act_S(act, 0), t=act_S(act, 1), u=third_S, w=act_W(act))
            in_order(TAIL, c=act_B_tail(act, B - 1), u=third_S, s=last_S)
            done(act, b_done[1])
            act.wait_ge(chosen, 1)
            act.activation(r16[5][:], r16[4][:], ACT.Exp).then_inc(exped, 1)
            in_order(S_FFN, s=last_S)
            done(act, s_done[1])
            all_slot_tiles(act, act_experts)
            with act.Fori(0, B) as i:
                act.wait_ge(out_e.sem, i + 3)
                act.dma_start(out[ds(i * S, S), :].rearrange("(t p) d -> p t d", p=P), X[:, ds(i * NT, NT), :]).then_inc(out_sem, 16)
            act.wait_ge(out_sem, 16 * B)

        @block.vector
        def _(dve):
            dve.memset(mhalf[:], -0.5)
            dve.memset(vsb[:, :, :, P:P + 1], 1.0)
            dve.memset(pad_row, 0.0)
            dve.drain().then_inc(setup, 1)
            dve.wait_ge(t_in, 16)
            dve.tensor_copy(pad_row[:, :, D], table[:, 64:66]).then_inc(pad_set, 1)
            dve.wait_ge(c_in, 16)
            dve.tensor_copy(identb[:], ident)
            dve.tensor_copy(maskb[:], noncausal)
            dve.drain().then_inc(setup, 1)
            for n in range(4):
                dve.wait_ge(split_hi, n + 1)
                dve.tensor_tensor(HI_LO[n][1], RAW[n][0][:, 0:RAW[n][1]], HI_LO[n][0].bitcast(F32), ALU.subtract).then_inc(split_lo, 1)
            dve.wait_ge(rt_hi, 1)
            dve.tensor_tensor(rt[:, 1], rt_raw[:, 1], rt[:, 0].bitcast(F32), ALU.subtract).then_inc(rt_lo, 1)
            dve.wait_ge(raw_in[4], 16)
            dve.drain()
            src, dst = rawB, rawC
            for st in range(3):
                a = src[:].rearrange("p (x two y) -> p x two y", two=2, y=D << st)
                b = dst[:].rearrange("p (x two y) -> p x two y", two=2, y=D << st)
                dve.tensor_tensor(b[:, :, 0], a[:, :, 0], a[:, :, 1], ALU.add)
                dve.tensor_tensor(b[:, :, 1], a[:, :, 0], a[:, :, 1], ALU.subtract)
                dve.drain()
                src, dst = dst, src
            dve.drain().then_inc(bfly, 1)
            for q in range(2):
                dve.wait_ge(hadh, q + 1)
                dve.scalar_tensor_tensor(out=w_dn[:, 1, 4 * q:4 * q + 4].rearrange("p a d -> p (a d)"), in0=pa[:, 2 * q:2 * q + 2, :].rearrange("p a d -> p (a d)"),
                                         scalar=1 / 32, in1=w_dn[:, 0, 4 * q:4 * q + 4].rearrange("p a d -> p (a d)").bitcast(F32),
                                         op0=ALU.mult, op1=ALU.subtract).then_inc(split_lo, 1)
            dve.drain()
            dve.memset(K6[KROWS:P, :, :], 1.0)
            dve.memset(V1[:], 0.0)
            dve.memset(mxn[:], 0.0)
            dve.drain()
            dve.memset(V1[:, :, :, HD:HD + 1], 1.0)
            dve.drain()
            for e in (var_a, xn_a, xl_a, vk_a, o_a, y_a, h_a, z_a, var_b, var_t, xn_b, xl_b, pc_b, v_b, mx_b, pm_b, bank_b, on_b, z_b, var_c, xn_c, xl_c, L_c, h_d, hT_d, row_d, number_d, var_e, out_e, y_used):
                e.open(dve)
            dve.wait_ge(x_in, 16)
            dve.wait_ge(b_in, 16)
            in_order(ALONE_A, a=dve_A(dve, 0))
            in_order(FIRST, a=dve_A(dve, 1), b=dve_B(dve, 0))
            with dve.Fori(1, B - 1) as i:
                in_order(TOGETHER, c=dve_B_tail(dve, i - 1), a=dve_A(dve, i + 1), b=dve_B(dve, i))
            third_S, last_S = Steps(dve_S(dve, B - 2)), Steps(dve_S(dve, B - 1))
            in_order(LAST, c=dve_B_tail(dve, B - 2), b=dve_B(dve, B - 1), s=dve_S(dve, 0), t=dve_S(dve, 1), u=third_S, w=dve_W(dve))
            in_order(TAIL, c=dve_B_tail(dve, B - 1), u=third_S, s=last_S)
            done(dve, b_done[2])
            dve_route(dve)
            in_order(S_FFN, s=last_S)
            done(dve, s_done[2])
            all_slot_tiles(dve, dve_experts)
            dve.drain()
            with dve.Fori(0, B // 2) as p:
                dve_result(dve, p)

        @block.gpsimd
        def _(pool):
            pool.wait_ge(setup, 1)
            for e in (rstd_a, hl_a, rstd_b, rstd_t, rstd_c, rstd_e):
                e.open(pool)
            in_order(ALONE_A, a=pool_A(pool, 0))
            in_order(FIRST, a=pool_A(pool, 1), b=pool_B(pool, 0))
            with pool.Fori(1, B - 1) as i:
                in_order(TOGETHER, c=pool_B_tail(pool, i - 1), a=pool_A(pool, i + 1), b=pool_B(pool, i))
            third_S, last_S = Steps(pool_S(pool, B - 2)), Steps(pool_S(pool, B - 1))
            in_order(LAST, c=pool_B_tail(pool, B - 2), b=pool_B(pool, B - 1), s=pool_S(pool, 0), t=pool_S(pool, 1), u=third_S)
            in_order(TAIL, c=pool_B_tail(pool, B - 1), u=third_S, s=last_S)
            done(pool, b_done[3])
            pool.wait_ge(pad_out, 32)
            pool.wait_ge(slots, 1)
            in_order(S_FFN, s=last_S, r=pool_scatter(pool))
            done(pool, s_done[3])
            all_slot_tiles(pool, pool_experts)
            with pool.Fori(0, B // 2) as p:
                for x in range(2):
                    rsqrt(pool, p, x, c_var, c_rstd[:], var_e, rstd_e)

        @block.tensor
        def _(pe):
            pe.wait_ge(setup, 2)
            pe.wait_ge(c_in, 16)
            pe.wait_ge(bfly, 1)
            for q in range(4):
                mm = pe.matmul(pa[:, q, :], had, rawC[:, q * 512:(q + 1) * 512], start=True, stop=True)
                if q % 2:
                    mm.then_inc(hadd, 1)
            pe.wait_ge(split_lo, 6)
            for e in (ps_a, ps_f, dn_a, psg_b, psm_b, pss_b, pv_b, pso_b, pst_b, t_c, lg_c, lgt_c, tx_d, w1_d, th_d, w2_d):
                e.open(pe)
            in_order(ALONE_A, a=pe_A(pe, 0))
            in_order(FIRST, a=pe_A(pe, 1), b=pe_B(pe, 0))
            with pe.Fori(1, B - 1) as i:
                in_order(TOGETHER, c=pe_B_tail(pe, i - 1), a=pe_A(pe, i + 1), b=pe_B(pe, i))
            third_S, last_S = Steps(pe_S(pe, B - 2)), Steps(pe_S(pe, B - 1))
            in_order(LAST, c=pe_B_tail(pe, B - 2), b=pe_B(pe, B - 1), s=pe_S(pe, 0), t=pe_S(pe, 1), u=third_S)
            in_order(TAIL, c=pe_B_tail(pe, B - 1), u=third_S, s=last_S)
            done(pe, b_done[0])
            pe.wait_ge(chosen, 1)
            both = R[7][:].rearrange("p t e -> p (t e)")
            pe.matmul(pb[:, 2, 0:TILES * E], upper, both, start=True, stop=True)
            pe.matmul(pb[:, 3, 0:TILES * E], ones[:], both, start=True, stop=True).then_inc(counted, 1)
            in_order(S_FFN, s=last_S)
            done(pe, s_done[0])
            pe.wait_ge(ew_in[0], 16)
            pe.wait_ge(ew_in[1], 16)
            pe.wait_ge(slots, 1)
            all_slot_tiles(pe, pe_experts)


def constants():
    import numpy as np
    c = np.zeros((P, 1156), np.float32)
    i = np.arange(P)
    c[:, 0:128] = np.eye(P)
    had = np.array([[1.0]])
    while had.shape[0] < P:
        had = np.block([[had, had], [had, -had]])
    c[:, 128:256] = had
    c[:, 256:384] = i[:, None] // LD == i[None, :] // LD
    c[:, 384:512] = i[:, None] < i[None, :]
    d = np.arange(512)[None, :] - i[:, None]
    c[:, 512:1024] = np.where(d >= 0, np.sqrt(np.maximum(d, 0).astype(np.float32)), 1e30)
    c[:, 1024:1028] = i[:, None] // LD == np.arange(4)[None, :]
    c[:, 1028:1156] = np.where(i[None, :] > i[:, None], NEG, 0)
    return c


def tables():
    import numpy as np
    c = np.zeros((P, 72), np.float32)
    i = np.arange(P)
    c[:, 0:TILES] = 2 * (np.arange(TILES)[None, :] * P + i[:, None])
    c[:, 16:24] = E - np.arange(E)
    c[:, 24:24 + MT] = np.arange(MT)
    c[:, 64:66] = 2 * (TILES + np.arange(2)[None, :]) * P + 2 * i[:, None]
    return c


def layout(inputs):
    import numpy as np

    def kt(w):
        w = np.asarray(w)
        k, n = w.shape
        return w.reshape(k // P, P, n).transpose(1, 0, 2).reshape(P, -1)

    g = {k: np.asarray(v) for k, v in inputs.items()}
    kv = np.concatenate([g["L1_attn_Wk"].T, g["L1_attn_Wv"].T], 1)
    return {
        "x": g["L0_attn_x"].reshape(B * S, D),
        "b_proj": g["L0_attn_b_proj"],
        "raw0": kt(g["L0_attn_w_qkv"].T),
        "raw1": np.concatenate([kt(g["L0_attn_w_proj"].T), kt(g["L1_attn_Wq"].T), kt(kv), kt(g["L1_attn_Wo"].T)], 1),
        "raw2": kt(g["L0_ffn_W1"].T),
        "raw3": kt(g["L0_ffn_W3"].T),
        "raw4": kt(g["L0_ffn_W2"].T),
        "const": constants(),
        "table": tables(),
        "router": kt(np.pad(g["L1_ffn_router_w"], ((0, 0), (0, P - E)))),
        "shared0": kt(g["L1_ffn_w_gate"]),
        "shared1": kt(g["L1_ffn_w_up"]),
        "shared2": kt(g["L1_ffn_w_down"]),
        "expert1": np.concatenate([kt(w) for w in g["L1_ffn_w1"]], 1),
        "expert2": np.concatenate([kt(w) for w in g["L1_ffn_w2"]], 1),
    }


def kernel(**inputs):
    import numpy as np
    import concourse.bacc as bacc
    from concourse.bass_utils import run_bass_kernel_spmd

    nc = bacc.Bacc("TRN2", target_bir_lowering=False, num_devices=1)
    arrays = {f"in_{k}": np.ascontiguousarray(v) for k, v in layout(inputs).items()}
    t = {k[3:]: nc.dram_tensor(k, v.shape, mybir.dt.from_np(v.dtype), kind="ExternalInput").ap() for k, v in arrays.items()}
    out = nc.dram_tensor("out", (B * S, D), F32, kind="ExternalOutput").ap()
    build(nc, t, out)
    r = run_bass_kernel_spmd(nc, [arrays], core_ids=[0])
    return r.results[0]["out"].reshape(B, S, D)
```

```python
from contextlib import ExitStack

import concourse.bass as bass
from concourse import mybir

F32 = mybir.dt.float32
F32R = mybir.dt.float32r
BF16 = mybir.dt.bfloat16
I32 = mybir.dt.int32
ALU = mybir.AluOpType
ACT = mybir.ActivationFunctionType
AX = mybir.AxisListType.X
ds = bass.ds

P = 128
B, S, D = 4, 512, 256
NT = S // P
TILES = B * NT
DC = D // P
FF = 1024
FC = FF // P
LD = 32
H, G, HD = 16, 4, 16
REP = H // G
VW = 32
KROWS = 6 * HD
E, INTER = 8, 512
MT = 39
ROW = 260
NEG = -1.0e30
EPS_LN = 1e-5
EPS_ATT = 1e-15
SLOPES = [2.0 ** (-0.5 * (h + 1)) for h in range(H)]


class Edge:

    def __init__(self, sem, per, by=1, ahead=None):
        self.sem, self.per, self.by, self.ahead = sem, per, by, per if ahead is None else ahead

    def open(self, engine):
        engine.sem_inc(self.sem, self.ahead * self.by)

    def wait(self, engine, i, k=0):
        engine.wait_ge(self.sem, (i * self.per + self.ahead + k + 1) * self.by)

    def wait_prev(self, engine, i, k=0):
        engine.wait_ge(self.sem, (i * self.per + self.ahead - self.per + k + 1) * self.by)


class Steps:

    def __init__(self, program):
        self.program, self.ahead = program, next(program)

    def through(self, step):
        while self.ahead is not None and self.ahead <= step:
            self.ahead = next(self.program, None)


def orders():
    start = """h0 a0 a1 a1.5 a2 a2.5 h1 a3 h2 a4 a5 a6 a6.5 a7 a7.5 h3 a8 a8.5 h4 h5 a9 a9.5 a10 a11 h6 a11.5 a12 a12.5 a13 a13.5 h7
               a14 a14.5 a15 a15.5 a16 a16.5 a17 a17.5 a18 a18.5 a19 a19.5 a20 a20.5 a21 a22"""
    both = """c29 c29.5 b0 c30 a0 c30.5 b1 b1.5 a1 a1.5 c31 b2 a2 a2.5 b3 b3.5 a3 a4 a5 b4 b4.5 a6 a6.5 a7 a7.5 a8 a8.5 a9 a9.5 b5
              a10 b6 a11 a11.5 b7 a12 a12.5 b8 a13 a13.5 b9 b10 a14 a14.5 b11 b12 b13 a15 a15.5 b14 b15 a16 a16.5 b16 a17 a17.5 a18
              a18.5 b17 a19 a19.5 a20 b18 b19 b20 a20.5 b21 a21 b22 b23 a22 b24 b25 b26 b27 b28"""
    last = """c29 c29.5 b0 s0 c30 c30.5 b1 b1.5 s1 s1.5 c31 b2 s2 b3 b3.5 w0 s3 s4 s4.5 w1 w2 b4 b4.5 s5 s5.5 s6 s6.5 s7 s7.5 b5 s8
              s8.5 b6 s9 s9.5 b7 s10 s10.5 b8 b9 s11 s11.5 s12 s12.5 s13 b10 s13.5 s14 t0 t1 b11 t1.5 b12 t2 b13 t3 b14 t4 t4.5 t5
              t5.5 b15 t6 t6.5 b16 t7 t7.5 t8 t8.5 b17 t9 t9.5 b18 t10 t10.5 b19 t11 b20 t11.5 t12 t12.5 t13 b21 t13.5 t14 u0 b22 u1
              u1.5 b23 u2 u3 u4 u4.5 b24 u5 u5.5 u6 b25 b26 u6.5 u7 u7.5 u8 u8.5 b27 u9 u9.5 b28"""
    tail = """c29 c29.5 u10 u10.5 c30 c30.5 u11 u11.5 c31 u12 u12.5 u13 s0 u13.5 s1 u14 s1.5 s2 s3 s4 s4.5"""
    ffn = """g0 g1 g2 g3 s5 s5.5 r0 r1 s6 s6.5 s7 s7.5 s8 s8.5 r2 r3 s9 s9.5 s10 r4 s10.5 r5 s11 s11.5 r6 s12 s12.5 r7 s14"""

    def steps(plan, streams):
        return [(step[0], float(step[1:])) for step in plan.split() if step[0] in streams]

    return steps(start, "ah"), steps(both, "ab"), steps(both, "abc"), steps(last, "bcstuw"), steps(tail, "csu"), steps(ffn, "gsr")


def build(nc, t, out):
    ctx = ExitStack()
    with ctx:
        def sem(name):
            return ctx.enter_context(nc.semaphore(name))

        def edge(name, per, by=1, ahead=None):
            return Edge(sem(name), per, by, ahead)

        def sb(name, shape, dt, where=ctx):
            return where.enter_context(nc.sbuf_tensor(name, shape, dt))

        pa = ctx.enter_context(nc.psum_tensor("pa", [P, 4, 512], F32))
        pb = ctx.enter_context(nc.psum_tensor("pb", [P, 4, 512], F32))

        const = sb("const", [P, 1156], F32)
        ident = const[:, 0:128]
        had = const[:, 128:256]
        blk = const[:, 256:384]
        upper = const[:, 384:512]
        dist = const[:, 512:1024]
        hm4 = const[:, 1024:1028]
        noncausal = const[:, 1028:1156]
        table = sb("table", [P, 72], F32)
        tok2 = table[:, 0:TILES]
        ehigh = table[:, 16:24]
        tile_no = table[:, 24:24 + MT]
        identb = sb("identb", [P, P], BF16)
        maskb = sb("maskb", [P, P], BF16)
        mhalf = sb("mhalf", [P, NT], F32)
        X = sb("X", [P, TILES, D], F32)
        in_place = ExitStack()
        rt_raw = sb("rt_raw", [P, 2, DC, P], F32, in_place)
        in_place.close()
        rt = sb("rt", [P, 2, DC, P], F32R)
        L = sb("L", [P, TILES, E], F32)

        in_place = ExitStack()
        up_raw = sb("up_raw", [P, 2, 2, DC, FF], F32, in_place)
        dn_raw = sb("dn_raw", [P, 2, FC, D], F32, in_place)
        in_place.close()
        ffn = ExitStack()
        w_up = sb("w_up", [P, 2, 2, DC, FF], F32R, ffn)
        w_dn = sb("w_dn", [P, 2, FC, D], F32R, ffn)
        xT = sb("xT", [P, 2, DC, S], F32R, ffn)
        hT = sb("hT", [P, 2, 2, S], F32R, ffn)
        hf = sb("hf", [P, 2, S], F32, ffn)
        th = sb("th", [P, 2, S // 2], F32, ffn)
        lgT = th[:].rearrange("p a b -> p (a b)")
        ffn.close()
        moe = ExitStack()
        ew2 = sb("ew2", [P, E, INTER // P, D], F32, moe)
        xt = sb("xt", [P, 2, ROW], F32, moe)
        xtT = sb("xtT", [P, 2, DC, P], F32, moe)
        e_s = sb("e_s", [P, 2, INTER], F32, moe)
        e_h = sb("e_h", [P, 2, INTER], F32, moe)
        e_hT = sb("e_hT", [P, 2, INTER // P, P], F32, moe)
        e_y = sb("e_y", [P, 2, D], F32, moe)
        e_number = sb("e_number", [P, 2], F32, moe)
        e_pick = sb("e_pick", [P, 2, 3], F32, moe)
        e_weight = sb("e_weight", [P, 2], F32, moe)
        e_row = sb("e_row", [P, 2], I32, moe)
        moe.close()
        ffn_room = sb("ffn_room", [P, 17920], F32)
        small = sb("small", [P, 168], F32)

        def norm_buffers(at):
            return (small[:, at:at + 24].rearrange("p (t s) -> p t s", t=NT), small[:, at + 24:at + 32].rearrange("p (t s) -> p t s", t=NT),
                    small[:, at + 32:at + 36])
        stats, mv, var = norm_buffers(0)
        statsb, mvb, varb = norm_buffers(36)
        statst, mvt, vart = norm_buffers(72)
        c_stats, c_mv, c_var = norm_buffers(108)
        rden = small[:, 144:160]
        den = small[:, 160:164]
        rstd = sb("rstd", [P, NT], F32)
        rstdb = sb("rstdb", [P, NT], F32)
        rstdt = sb("rstdt", [P, NT], F32)
        c_rstd = sb("c_rstd", [P, NT], F32)

        mix = ExitStack()
        w_mix = sb("w_mix", [P, 2, 1792], F32R, mix)
        mix.close()
        ones = sb("ones", [P, P], F32)
        R = [sb(f"R{n}", [P, TILES, E], F32) for n in range(14)]
        r16 = [sb(f"r16_{n}", [P, TILES], F32) for n in range(11)]
        r8 = [sb(f"r8_{n}", [P, E], F32) for n in range(8)]
        i8 = [sb(f"i8_{n}", [P, E], I32) for n in range(2)]
        idx = sb("idx", [P, 2, TILES], I32)
        teI = sb("teI", [P, MT], I32)
        teF = [sb(f"teF{n}", [P, MT], F32) for n in range(2)]
        teC = sb("teC", [P, MT, E], F32)
        mix_rest = sb("mix_rest", [P, 2 * 1792 - P - 14 * TILES * E - 13 * TILES - 10 * E - MT * (E + 3)], F32)

        def wmix(s, at, n):
            return w_mix[:, s, at:at + DC * n].rearrange("p (c n) -> p c n", c=DC)
        w_proj = [wmix(s, 0, D) for s in range(2)]
        w_q = [wmix(s, 512, D) for s in range(2)]
        w_kv = [wmix(s, 1024, P) for s in range(2)]
        w_o = [wmix(s, 1280, D) for s in range(2)]

        lin = ExitStack()
        bias = sb("bias", [P, D], F32, lin)
        w_qkv = sb("w_qkv", [P, 2, DC, 3 * D], F32R, lin)
        xn = sb("xn", [P, NT, D], F32, lin)
        qT = sb("qT", [P, DC, S], F32, lin)
        ksb = sb("ksb", [P, NT, D], F32, lin)
        vsb = sb("vsb", [P, NT, DC, P + 1], F32, lin)
        vk = sb("vk", [P, DC, P + 4], F32, lin)
        o0 = xn
        lin.close()
        XN = sb("XN", [P, TILES, ROW], F32)
        SH = sb("SH", [P, TILES, D], F32)

        raw = ExitStack()
        staged = [sb(f"staged{n}", [P, w], F32, raw) for n, w in enumerate((1536, 1792, 2048, 2048, 2048))]
        spare = sb("spare", [P, 2048], F32, raw)
        raw.close()
        att = ExitStack()
        Q6 = sb("Q6", [P, H, S], BF16, att)
        K6 = sb("K6", [P, G, S], BF16, att)
        V1 = sb("V1", [P, NT, G, VW], F32, att)
        pq = sb("pq", [P, 3, DC, S], BF16, att)
        pk = sb("pk", [P, 3, S], BF16, att)
        kvs = sb("kvs", [P, S], F32, att)
        sbi = sb("sbi", [P, 2, S], F32, att)
        pr = sb("pr", [P, 3, S], F32, att)
        mxn = sb("mxn", [P, P], F32, att)
        pm = sb("pm", [NT * H, 3, P], BF16, att)
        xnb = sb("xnb", [P, NT, D], F32, att)
        xTb = sb("xTb", [P, 2, DC, S], F32R, att)
        rq = sb("rq", [P, S], F32, att)
        pmr = rq[0:NT * H, 0:P]
        OT = sb("OT", [P, 2, S], F32, att)
        zt = OT[:].rearrange("p g (k d) -> p (g k) d", d=D)
        pad_row = OT[:].rearrange("p g n -> p (g n)")[:, 0:2 * ROW].rearrange("p (x r) -> p x r", x=2)
        rco = sb("rco", [P, NT * REP], F32, att)
        att.close()
        end = ExitStack()
        yb = sb("yb", [P, B, NT, 2, D], F32, end)
        zc = sb("zc", [P, B, NT, D], F32, end)
        e_small = sb("e_small", [P, B, 36], F32, end)
        e_norm = [[e_small[:, x, 0:24].rearrange("p (t s) -> p t s", t=NT), e_small[:, x, 24:32].rearrange("p (t s) -> p t s", t=NT), e_small[:, x, 32:36]]
                  for x in range(B)]
        e_rstd = sb("e_rstd", [P, B, NT], F32, end)
        e_shift = sb("e_shift", [P, B, NT], F32, end)
        end.close()
        ew1 = sb("ew1", [P, E, DC, 2 * INTER], F32)

        qd = nc.dram_tensor("q_pieces", (3, D, S), BF16, kind="Internal").ap()
        kd = nc.dram_tensor("k_pieces", (3, G * HD, S), BF16, kind="Internal").ap()
        xs = nc.dram_tensor("x_slots", (MT * P, ROW), F32, kind="Internal").ap()
        ys = nc.dram_tensor("y_rows", (2 * (TILES + 2) * P, D), F32, kind="Internal").ap()

        c_in = sem("const_loaded")
        b_in = sem("bias_loaded")
        x_in = [sem(f"x_loaded{n}") for n in range(2)]
        raw_in = [sem(f"raw_loaded{n}") for n in range(5)]
        split_hi = sem("weight_hi_written")
        split_lo = sem("weight_lo_written")
        setup = sem("setup_by_vector")
        bfly = sem("butterflies_done")
        hadd = sem("hadamard_product_done")
        hadh = sem("hadamard_hi_written")

        var_a, rstd_a = edge("variance_a", 4), edge("rstd_a", 4)
        xn_a, ps_a = edge("normed_a", 2), edge("psum_a_full", 10)
        ps_f = edge("ffn_up_full", 16)
        xh_a, xl_a = edge("xT_hi_a", 3), edge("xT_lo_a", 3)
        q_a, kv_a, vk_a, o_a, y_a = edge("q_written", 1), edge("kv_written", 2), edge("vk_written", 1), edge("o_written", 2), edge("proj_added", 1)
        th_a, h_a, hh_a, hl_a, dn_a, z_a = edge("tanh_written", 16), edge("h_written", 16), edge("h_hi_written", 8), edge("h_lo_written", 8), edge("h_used", 8), edge("ffn_copied", 1)

        var_b, rstd_b = edge("variance_b", 1), edge("rstd_b", 1)
        var_t, rstd_t = edge("variance_t", 1), edge("rstd_t", 1)
        xn_b, psg_b = edge("normed_b", 1), edge("psum_b_full", 7)
        xh_b, xl_b = edge("xT_hi_b", 2), edge("xT_lo_b", 2)
        qh_b, kh_b, pc_b = edge("q_hi_written", 1), edge("k_hi_written", 1), edge("pieces_written", 2)
        v_b = edge("v_written", 1)
        bo_b = edge("pieces_in_dram", 2, 16)
        q6_b, k6_b = edge("q_packed", 6, 16), edge("k_packed", 6, 16)
        psm_b, mx_b = edge("max_scores_full", 44), edge("max_taken", 44)
        pm_b, m6_b = edge("max_pieces_written", 1), edge("max_packed", 3, 16)
        pss_b, bank_b = edge("scores_full", 44), edge("score_bank_read", 48)
        ex_b, pv_b, pso_b = edge("exp_written", 44), edge("probs_used", 44), edge("heads_summed", 4)
        ot_b, pst_b, on_b = edge("OT_written", 4), edge("OT_transposed", 4), edge("attention_written", 1)
        z_b = edge("attention_added", 1)
        var_c, rstd_c, xn_c = edge("variance_c", 1), edge("rstd_c", 1), edge("normed_c", 1)
        t_c, xh_c, xl_c = edge("xn_c_transposed", 1), edge("XT_hi", 1), edge("XT_lo", 1)
        lg_c, lgc_c, lgt_c, L_c = edge("logits_full", 1), edge("logits_copied", 1), edge("logits_transposed", 1), edge("logits_written", 1)
        t_in, pad_set, pad_out, r_in, rt_hi, rt_lo = (sem(n) for n in ("table_loaded", "pad_row_set", "pads_written", "router_loaded", "router_hi", "router_lo"))
        s_in = [sem(f"shared_weight_loaded{n}") for n in range(3)]
        s_hi, s_lo = sem("shared_hi_written"), sem("shared_lo_written")
        chosen, exped, counted, slots = (sem(n) for n in ("experts_chosen", "gap_exponentiated", "counts_full", "slots_written"))
        z_s = edge("shared_output_written", 1)
        hl_v = edge("h_lo_written_by_vector", 8, ahead=0)
        b_done = [sem(f"stream_b_done_{n}") for n in ("pe", "act", "dve", "pool")]
        ew_in = [sem("expert_w1_loaded"), sem("expert_w2_loaded")]
        xt_in = [edge(f"slot_rows_loaded{x}", 1, 16) for x in range(2)]
        tx_d, xT_d, w1_d, s_d, h_d = edge("slot_rows_transposed", 2), edge("xtT_written", 2), edge("expert_up_full", 4), edge("expert_silu_written", 2), edge("expert_h_written", 2)
        th_d, hT_d, w2_d, y_d, row_d = edge("expert_h_transposed", 2), edge("expert_hT_written", 2), edge("expert_down_full", 2), edge("expert_y_written", 2), edge("row_numbers_written", 2)
        number_d, turns = edge("number_written", 2), sem("scatters_begun")
        ysc = [edge(f"rows_scattered{x}", 1, 16, ahead=TILES) for x in range(2)]
        yb_in = [sem(f"y_rows_loaded{i}") for i in range(B)]
        y_sum, shifts, normed, result = sem("y_rows_added"), sem("shifts_written"), sem("sum_normed"), sem("result_ready")
        out_sem = sem("out_written")
        var_e, rstd_e = edge("variance_e", 1), edge("rstd_e", 1)

        HI_LO = [
            [w_qkv[:, s].rearrange("p c n -> p (c n)") for s in range(2)],
            [w_mix[:, s] for s in range(2)],
            [w_up[:, s, 0].rearrange("p c n -> p (c n)") for s in range(2)],
            [w_up[:, s, 1].rearrange("p c n -> p (c n)") for s in range(2)],
            [w_dn[:, s].rearrange("p c n -> p (c n)") for s in range(2)],
        ]

        def tile_of(i, k):
            return ds(i * NT + k, 1)

        PASSES = [(0, 0), (0, 1), (1, 0)]

        def norm_stats(dve, i, src, st, m, v, e_var):
            for k in range(NT):
                dve.bn_stats(st[:, k, :], src(k))
            dve.drain()
            for k in range(NT):
                dve.bn_aggr(m[:, k, :], st[:, k, :])
            dve.drain()
            dve.tensor_scalar(v, m[:, :, 1], EPS_LN, None, ALU.add).then_inc(e_var.sem, 1)

        def norm_apply(dve, k, dst, src, m, r):
            return dve.tensor_scalar(dst, src, m[:, k, 0:1], r[:, k:k + 1], ALU.subtract, ALU.mult)

        def rsqrt(pool, i, k, v, r, e_var, e_rstd):
            e_var.wait(pool, i, k)
            pool.tensor_tensor(r, v, mhalf[:, :], ALU.pow).then_inc(e_rstd.sem, 1)

        def split3(pe, dst, lhs, rhs, first=True, last=True):
            for n, (a, b) in enumerate(PASSES):
                mm = pe.matmul(dst, lhs[a], rhs[b], start=first and n == 0, stop=last and n == 2,
                               skip_group_check=True)
            return mm

        def is_use(i, n):
            return isinstance(i, int) and i == n

        def in_order(order, **streams):
            streams = {name: stream if isinstance(stream, Steps) else Steps(stream) for name, stream in streams.items()}
            for name, step in order:
                if name in streams:
                    streams[name].through(step)

        ALONE_B = [("b", n) for n in range(32)]
        START, FIRST, TOGETHER, LAST, TAIL, S_FFN = orders()

        def pe_ffn(pe, f, at):
            def down(j):
                if is_use(f, 0) and j == 0:
                    pe.wait_ge(split_lo, 6)
                if is_use(f, LAST_FFN):
                    hl_v.wait(pe, 0, j)
                else:
                    hl_a.wait(pe, f, j)
                for k in range(NT):
                    mm = split3(pe, pa[:, 2 + k // 2, (k % 2) * D:(k % 2 + 1) * D], [hT[:, s, j % 2, k * P:(k + 1) * P] for s in range(2)],
                                [w_dn[:, s, j, :] for s in range(2)], j == 0 and k % 2 == 0, j == FC - 1)
                mm.then_inc(dn_a.sem, 1)
                return mm

            for j in range(FC):
                if j >= 1:
                    yield at + j
                for half in range(2):
                    if j >= 1:
                        h_a.wait(pe, f, 2 * (j - 1) + half)
                    for u in range(2):
                        for c in range(DC):
                            mm = split3(pe, pa[:, half, u * D:(u + 1) * D], [w_up[:, s, u, c, j * P:(j + 1) * P] for s in range(2)],
                                        [xT[:, s, c, half * D:(half + 1) * D] for s in range(2)], c == 0, c == 1)
                    mm.then_inc(ps_f.sem, 1)
                if j >= 2:
                    down(j - 2)
            yield at + FC
            down(FC - 2)
            yield at + FC + 0.5
            down(FC - 1)

        def act_ffn(act, f, at):
            def h_hi(j):
                h_a.wait(act, f, 2 * j + 1)
                if j >= 2:
                    dn_a.wait(act, f, j - 2)
                act.activation(hT[:, 0, j % 2], hf[:, j % 2], ACT.Copy).then_inc(hh_a.sem, 1)

            for j in range(FC):
                if j >= 1:
                    yield at + j
                if j >= 1:
                    h_hi(j - 1)
                for half in range(2):
                    ps_f.wait(act, f, 2 * j + half)
                    act.activation(th[:, half], pa[:, half, 0:D], ACT.Tanh, scale=0.5).then_inc(th_a.sem, 1)
            yield at + FC
            h_hi(FC - 1)

        LAST_FFN = 2 * B - 1

        def dve_ffn(dve, f, at):
            def h_lo(j):
                hh_a.wait(dve, f, j)
                dve.tensor_tensor(hT[:, 1, j % 2], hf[:, j % 2], hT[:, 0, j % 2].bitcast(F32), ALU.subtract).then_inc(hl_v.sem, 1)

            for j in range(FC):
                yield at + j + 0.5
                if is_use(f, LAST_FFN) and j >= 1:
                    h_lo(j - 1)
                for half in range(2):
                    th_a.wait(dve, f, 2 * j + half)
                    dve.scalar_tensor_tensor(out=th[:, half], in0=th[:, half], scalar=1.0, in1=pa[:, half, 0:D], op0=ALU.add, op1=ALU.mult)
                    dve.drain()
                    if j >= 2 and half == 0 and not is_use(f, LAST_FFN):
                        hl_a.wait(dve, f, j - 2)
                    dve.scalar_tensor_tensor(out=hf[:, j % 2, half * D:(half + 1) * D], in0=th[:, half], scalar=0.5, in1=pa[:, half, D:2 * D],
                                             op0=ALU.mult, op1=ALU.mult).then_inc(h_a.sem, 1)
            if is_use(f, LAST_FFN):
                yield at + FC
                h_lo(FC - 1)

        def pool_ffn(pool, f, at):
            if is_use(f, LAST_FFN):
                return
            for j in range(FC):
                yield at + 1 + j
                hh_a.wait(pool, f, j)
                pool.tensor_tensor(hT[:, 1, j % 2], hf[:, j % 2], hT[:, 0, j % 2].bitcast(F32), ALU.subtract).then_inc(hl_a.sem, 1)

        def pe_A(pe, i):
            def xs_(c):
                return [xT[:, s, c, :] for s in range(2)]

            def transposes(src, n):
                for c in range(DC):
                    for k in range(NT):
                        mm = pe.transpose(pa[:, 2 * (n % 2) + c, k * P:(k + 1) * P], src[:, k, c * P:(c + 1) * P], ident)
                mm.then_inc(ps_a.sem, 1)

            def weights(n):
                if is_use(i, 0):
                    pe.wait_ge(split_lo, n + 1)

            yield 1.5
            xn_a.wait(pe, i, 0)
            transposes(xn, 0)
            yield 3
            weights(0)
            xh_a.wait(pe, i, 0)
            xl_a.wait(pe, i, 0)
            z_a.wait_prev(pe, i)
            for m in range(DC):
                for c in range(DC):
                    mm = split3(pe, pa[:, 2 + m, :], [w_qkv[:, s, c, m * P:(m + 1) * P] for s in range(2)], xs_(c), c == 0, c == 1)
            mm.then_inc(ps_a.sem, 1)
            for half in range(2):
                yield 4 + half
                if half == 1:
                    q_a.wait(pe, i)
                for kk in range(2):
                    k = 2 * half + kk
                    for c in range(DC):
                        mm = split3(pe, pa[:, 2 * half + kk, :], [xT[:, s, c, k * P:(k + 1) * P] for s in range(2)],
                                    [w_qkv[:, s, c, D:3 * D] for s in range(2)], c == 0, c == 1)
                mm.then_inc(ps_a.sem, 1)
            yield 6
            kv_a.wait(pe, i, 1)
            for c in range(DC):
                for k in range(NT):
                    mm = pe.matmul(pa[:, c, 0:P + 1], ksb[:, k, c * P:(c + 1) * P], vsb[:, k, c, :], start=k == 0, stop=k == NT - 1)
            mm.then_inc(ps_a.sem, 1)
            yield 7
            vk_a.wait(pe, i)
            for half in range(2):
                for kk in range(2):
                    k = 2 * half + kk
                    for c in range(DC):
                        mm = pe.matmul(pa[:, 2 * (1 - half) + kk, c * (P + 4):(c + 1) * (P + 4)], qT[:, c, k * P:(k + 1) * P], vk[:, c, :],
                                       start=True, stop=True, skip_group_check=True)
                mm.then_inc(ps_a.sem, 1)
            yield 8
            o_a.wait(pe, i, 1)
            transposes(o0, 1)
            yield 9
            weights(1)
            xh_a.wait(pe, i, 1)
            xl_a.wait(pe, i, 1)
            for k in range(NT):
                for c in range(DC):
                    mm = split3(pe, pa[:, k // 2, (k % 2) * D:(k % 2 + 1) * D], [xT[:, s, c, k * P:(k + 1) * P] for s in range(2)],
                                [w_proj[s][:, c, :] for s in range(2)], c == 0, c == 1)
            mm.then_inc(ps_a.sem, 1)
            yield 11.5
            xn_a.wait(pe, i, 1)
            transposes(xn, 1)
            yield 12
            weights(3)
            xh_a.wait(pe, i, 2)
            xl_a.wait(pe, i, 2)
            yield from pe_ffn(pe, i, 12)

        def act_A(act, i):
            def hi(k, n, slot):
                ps_a.wait(act, i, n)
                act.activation(xT[:, 0], pa[:, 2 * slot:2 * slot + 2, :], ACT.Copy).then_inc(xh_a.sem, 1)

            yield 1.5
            hi(0, 0, 0)
            yield 3
            ps_a.wait(act, i, 1)
            act.activation(qT[:], pa[:, 2:4, :], ACT.Relu).then_inc(q_a.sem, 1)
            for half in range(2):
                yield 4 + half
                ps_a.wait(act, i, 2 + half)
                src = pa[:, 2 * half:2 * half + 2, :]
                act.activation(ksb[:, 2 * half:2 * half + 2, :], src[:, :, 0:D], ACT.Relu)
                for kk in range(2):
                    v = act.activation(vsb[:, 2 * half + kk, :, 0:P], src[:, kk, D:2 * D].rearrange("p (c n) -> p c n", c=DC), ACT.Copy)
                act.drain().then_inc(kv_a.sem, 1)
            yield 8
            hi(1, 7, 1)
            yield 11.5
            hi(2, 9, 1)

            yield 12
            yield from act_ffn(act, i, 12)

        def dve_A(dve, i):
            def xtile(k):
                return X[:, tile_of(i, k), :].rearrange("p a d -> p (a d)")

            def lo(k, slot):
                xh_a.wait(dve, i, k)
                dve.tensor_tensor(xT[:, 1], pa[:, 2 * slot:2 * slot + 2, :], xT[:, 0].bitcast(F32), ALU.subtract).then_inc(xl_a.sem, 1)

            yield 0
            if is_use(i, 0):
                dve.wait_ge(x_in[0], 16)
            norm_stats(dve, i, xtile, stats, mv, var, var_a)
            yield 1
            rstd_a.wait(dve, i, 0)
            for k in range(NT):
                norm_apply(dve, k, xn[:, k], xtile(k), mv, rstd)
            dve.drain().then_inc(xn_a.sem, 1)
            yield 2.5
            lo(0, 0)
            yield 6.5
            ps_a.wait(dve, i, 4)
            for c in range(DC):
                dve.tensor_tensor(vk[:, c, 0:P], pa[:, c, 0:P], blk, ALU.mult)
                dve.tensor_copy(den[:, c:c + 1], pa[:, c, P:P + 1])
            dve.drain()
            for c in range(DC):
                dve.tensor_scalar(vk[:, c, P:P + 4], hm4, den[:, c:c + 1], None, ALU.mult)
            dve.drain().then_inc(vk_a.sem, 1)
            for half in range(2):
                if half == 0:
                    yield 7.5
                ps_a.wait(dve, i, 5 + half)
                src = pa[:, 2 * (1 - half):2 * (1 - half) + 2, :]
                for kk in range(2):
                    o_src = src[:, kk, 0:DC * (P + 4)].rearrange("p (c n) -> p c n", c=DC)
                    r = rden[:, 8 * kk:8 * kk + 8]
                    dve.tensor_scalar(r.rearrange("p (c h) -> p c h", c=DC), o_src[:, :, P:P + 4], EPS_ATT, None, ALU.add)
                dve.drain()
                dve.reciprocal(rden, rden)
                dve.drain()
                for kk in range(2):
                    for c in range(DC):
                        o_src = src[:, kk, c * (P + 4):c * (P + 4) + P].rearrange("p (h e) -> p h e", e=LD)
                        r = rden[:, 8 * kk + 4 * c:8 * kk + 4 * c + 4]
                        dve.tensor_tensor(o0[:, 2 * half + kk, c * P:(c + 1) * P].rearrange("p (h e) -> p h e", e=LD), o_src,
                                          r.unsqueeze(2).to_broadcast([P, 4, LD]), ALU.mult)
                dve.drain().then_inc(o_a.sem, 1)
            yield 8.5
            lo(1, 1)
            yield 9.5
            if is_use(i, 0):
                dve.wait_ge(b_in, 16)
            ps_a.wait(dve, i, 8)
            dve.tensor_tensor(xn[:], pa[:, 0:2, :].rearrange("p b (k d) -> p (b k) d", d=D),
                              bias[:].unsqueeze(1).to_broadcast([P, NT, D]), ALU.add).then_inc(y_a.sem, 1)
            dve.drain()
            norm_stats(dve, i, lambda k: xn[:, k], stats, mv, var, var_a)
            yield 10
            rstd_a.wait(dve, i, 1)
            for k in range(NT):
                norm_apply(dve, k, xn[:, k], xn[:, k], mv, rstd)
            dve.drain()
            xb = X[:, ds(i * NT, NT), :]
            dve.tensor_tensor(xb, xb, xn[:], ALU.add)
            dve.drain()
            norm_stats(dve, i, xtile, stats, mv, var, var_a)
            yield 11
            rstd_a.wait(dve, i, 2)
            for k in range(NT):
                norm_apply(dve, k, xn[:, k], xtile(k), mv, rstd)
            dve.drain().then_inc(xn_a.sem, 1)
            lo(2, 1)
            yield 12
            yield from dve_ffn(dve, i, 12)
            yield 21
            dn_a.wait(dve, i, FC - 1)

            def product(k):
                return pa[:, 2 + k // 2, (k % 2) * D:(k % 2 + 1) * D]

            norm_stats(dve, i, product, stats, mv, var, var_a)
            yield 22
            rstd_a.wait(dve, i, 3)
            for k in range(NT):
                norm_apply(dve, k, xn[:, k], product(k), mv, rstd)
            dve.drain().then_inc(z_a.sem, 1)
            dve.tensor_tensor(xb, xb, xn[:], ALU.add)
            dve.drain()

        def pool_A(pool, i):
            for k, at in enumerate((0, 9, 10)):
                yield at
                rsqrt(pool, i, k, var, rstd[:], var_a, rstd_a)
            yield from pool_ffn(pool, i, 12)
            yield 21
            rsqrt(pool, i, 3, var, rstd[:], var_a, rstd_a)

        def units_of(g):
            for kb in range(NT):
                hh = {0: 1, 1: 1, 2: 2, 3: 4}[kb]
                for h0 in range(0, REP, hh):
                    yield kb, h0, hh
        SEQ = []
        for g in range(G):
            for u, (kb, h0, hh) in enumerate(units_of(g)):
                SEQ.append(("S", g, kb, h0, hh))
                if u == 9 and g > 0:
                    SEQ.append(("T", g - 1))
        SEQ.append(("T", G - 1))
        MAXU = [(g, qb, h0, {0: 4, 1: 2, 2: 1, 3: 1}[qb]) for g in range(G) for qb in range(NT)
                for h0 in range(0, REP, {0: 4, 1: 2, 2: 1, 3: 1}[qb])]

        def pe_B(pe, i):
            yield 1.5
            xn_b.wait(pe, i)
            for c in range(DC):
                for k in range(NT):
                    mm = pe.transpose(pb[:, c, k * P:(k + 1) * P], xnb[:, k, c * P:(c + 1) * P], ident)
            mm.then_inc(psg_b.sem, 1)
            yield 3
            z_b.wait_prev(pe, i)
            xh_b.wait(pe, i, 0)
            xl_b.wait(pe, i, 0)
            for m in range(DC):
                for c in range(DC):
                    mm = split3(pe, pb[:, 2 + m, :], [w_q[s][:, c, m * P:(m + 1) * P] for s in range(2)],
                                [xTb[:, s, c, :] for s in range(2)], c == 0, c == 1)
            mm.then_inc(psg_b.sem, 1)
            for c in range(DC):
                mm = split3(pe, pb[:, 0, :], [w_kv[s][:, c, :] for s in range(2)], [xTb[:, s, c, :] for s in range(2)], c == 0, c == 1)
            mm.then_inc(psg_b.sem, 1)
            yield 4
            kh_b.wait(pe, i)
            for k in range(NT):
                mm = pe.transpose(pb[:, 1, k * P:(k + 1) * P], kvs[:, k * P:(k + 1) * P], ident)
            mm.then_inc(psg_b.sem, 1)
            yield 5
            q6_b.wait(pe, i, 5)
            k6_b.wait(pe, i, 5)
            v_b.wait(pe, i)
            pc_b.wait(pe, i, 1)
            for n, (g, qb, h0, hh) in enumerate(MAXU):
                if n % 4 == 0:
                    yield 5 + n // 4
                if n >= 4:
                    mx_b.wait(pe, i, n - 4)
                w = (qb + 1) * P
                for x in range(hh):
                    h = g * REP + h0 + x
                    pe.matmul(pb[:, n % 4, x * w:(x + 1) * w], Q6[0:KROWS, h, qb * P:(qb + 1) * P], K6[0:KROWS, g, 0:w],
                              start=True, stop=False, skip_group_check=True)
                    mm = pe.matmul(pb[:, n % 4, x * w + qb * P:(x + 1) * w], identb[:], maskb[:], start=False, stop=True, skip_group_check=True)
                mm.then_inc(psm_b.sem, 1)
            yield 16
            mx_b.wait(pe, i, len(MAXU) - 1)
            pe.transpose(pb[:, 2, 0:P], mxn[:], ident).then_inc(psg_b.sem, 1)
            yield 17
            m6_b.wait(pe, i, 2)

            def front(n):
                u = SEQ[n]
                if n >= 3:
                    bank_b.wait(pe, i, n - 3)
                if u[0] == "S":
                    _, g, kb, h0, hh = u
                    w = S - kb * P
                    pe.matmul(pb[:, n % 3, 0:hh * w], K6[0:KROWS + 3, g, kb * P:(kb + 1) * P],
                              Q6[0:KROWS + 3, g * REP + h0:g * REP + h0 + hh, kb * P:S], start=True, stop=True).then_inc(pss_b.sem, 1)
                else:
                    g = u[1]
                    ot_b.wait(pe, i, g)
                    for k in range(NT):
                        mm = pe.transpose(pb[:, n % 3, k * P:(k + 1) * P], OT[:, g % 2, k * P:(k + 1) * P], ident)
                    mm.then_inc(pst_b.sem, 1)

            s_at = 0
            front(0)
            front(1)
            front(2)
            for n, u in enumerate(SEQ[:-1]):
                if n % 4 == 0:
                    yield 17 + n // 4
                if n + 3 < len(SEQ) - 1:
                    front(n + 3)
                if u[0] == "S":
                    _, g, kb, h0, hh = u
                    w = S - kb * P
                    ex_b.wait(pe, i, s_at)
                    if kb == 0 and h0 == 0 and g >= 1:
                        ot_b.wait(pe, i, g - 1)
                    for x in range(hh):
                        hq = h0 + x
                        mm = pe.matmul(pb[hq * VW:(hq + 1) * VW, 3, kb * P:S], V1[:, kb, g, :], pr[:, s_at % 3, x * w:(x + 1) * w],
                                       start=kb == 0, stop=kb == NT - 1, skip_group_check=True)
                    s_at += 1
                    mm.then_inc(pv_b.sem, 1)
                    if kb == NT - 1:
                        pe.drain().then_inc(pso_b.sem, 1)
            front(len(SEQ) - 1)

        def pe_B_tail(pe, i):
            yield 29
            on_b.wait(pe, i)
            for c in range(DC):
                for k in range(NT):
                    mm = pe.transpose(pb[:, c, k * P:(k + 1) * P], xnb[:, k, c * P:(c + 1) * P], ident)
            mm.then_inc(psg_b.sem, 1)
            yield 30
            xh_b.wait(pe, i, 1)
            xl_b.wait(pe, i, 1)
            ot_b.wait(pe, i, G - 1)
            for k in range(NT):
                for c in range(DC):
                    mm = split3(pe, pb[:, 2 + k // 2, (k % 2) * D:(k % 2 + 1) * D], [xTb[:, s, c, k * P:(k + 1) * P] for s in range(2)],
                                [w_o[s][:, c, :] for s in range(2)], c == 0, c == 1)
            mm.then_inc(psg_b.sem, 1)

        def act_B(act, i):
            yield 1.5
            psg_b.wait(act, i, 0)
            act.activation(xTb[:, 0], pb[:, 0:2, :], ACT.Copy).then_inc(xh_b.sem, 1)
            yield 3
            psg_b.wait(act, i, 1)
            act.activation(pq[:, 0], pb[:, 2:4, :], ACT.Copy, scale=HD ** -0.5).then_inc(qh_b.sem, 1)
            psg_b.wait(act, i, 2)
            act.activation(pk[:, 0], pb[:, 0, :], ACT.Copy)
            act.activation(kvs[:], pb[:, 0, :], ACT.Copy)
            act.drain().then_inc(kh_b.sem, 1)
            s_at = 0
            for n, u in enumerate(SEQ):
                if n % 4 == 0:
                    yield 17 + n // 4
                if u[0] != "S":
                    continue
                _, g, kb, h0, hh = u
                w = S - kb * P
                bank_b.wait(act, i, n)
                if s_at >= 3:
                    pv_b.wait(act, i, s_at - 3)
                act.activation(pr[:, s_at % 3, 0:hh * w], sbi[:, s_at % 2, 0:hh * w], ACT.Exp).then_inc(ex_b.sem, 1)
                s_at += 1
                if kb == 0 and h0 == 0 and g > 0:
                    copy_OT(act, i, g - 1)
            copy_OT(act, i, G - 1)

        def act_B_tail(act, i):
            yield 29
            psg_b.wait(act, i, 5)
            act.activation(xTb[:, 0], pb[:, 0:2, :], ACT.Copy).then_inc(xh_b.sem, 1)

        def copy_OT(act, i, g):
            pso_b.wait(act, i, g)
            act.activation(OT[:, g % 2], pb[:, 3, :], ACT.Copy).then_inc(ot_b.sem, 1)

        def dve_B(dve, i):
            def xtile(k):
                return X[:, tile_of(i, k), :].rearrange("p a d -> p (a d)")

            yield 0
            norm_stats(dve, i, xtile, statsb, mvb, varb, var_b)
            yield 1
            rstd_b.wait(dve, i, 0)
            for k in range(NT):
                norm_apply(dve, k, xnb[:, k], xtile(k), mvb, rstdb)
            dve.drain().then_inc(xn_b.sem, 1)
            yield 2
            xh_b.wait(dve, i, 0)
            dve.tensor_tensor(xTb[:, 1], pb[:, 0:2, :], xTb[:, 0].bitcast(F32), ALU.subtract).then_inc(xl_b.sem, 1)
            yield 3.5
            qh_b.wait(dve, i)
            for c in range(DC):
                dve.scalar_tensor_tensor(out=rq[:], in0=pb[:, 2 + c, :], scalar=HD ** -0.5, in1=pq[:, 0, c], op0=ALU.mult, op1=ALU.subtract)
                dve.drain()
                dve.tensor_copy(pq[:, 1, c], rq[:])
                dve.drain()
                dve.tensor_tensor(pq[:, 2, c], rq[:], pq[:, 1, c], ALU.subtract)
                dve.drain()
            dve.drain().then_inc(pc_b.sem, 1)
            kh_b.wait(dve, i)
            dve.tensor_tensor(rq[:], pb[:, 0, :], pk[:, 0], ALU.subtract)
            dve.drain()
            dve.tensor_copy(pk[:, 1], rq[:])
            dve.drain()
            dve.tensor_tensor(pk[:, 2], rq[:], pk[:, 1], ALU.subtract).then_inc(pc_b.sem, 1)
            yield 4.5
            psg_b.wait(dve, i, 3)
            dve.tensor_copy(V1[:, :, :, 0:HD], pb[:, 1, :].rearrange("p (k z g d) -> p k z g d", k=NT, z=2, g=G)[:, :, 1]).then_inc(v_b.sem, 1)
            for n, (g, qb, h0, hh) in enumerate(MAXU):
                if n % 4 == 0:
                    yield 5 + n // 4
                psm_b.wait(dve, i, n)
                h = g * REP + h0
                dve.tensor_reduce(mxn[:, 0:NT * H].rearrange("p (h k) -> p k h", k=NT)[:, qb, h:h + hh], pb[:, n % 4, 0:hh * (qb + 1) * P].rearrange("p (h w) -> p h w", h=hh), AX, ALU.max,
                                  negate=True).then_inc(mx_b.sem, 1)
            yield 16
            psg_b.wait(dve, i, 4)
            mT = pb[0:NT * H, 2, 0:P]
            dve.tensor_copy(pm[:, 0], mT)
            dve.drain()
            dve.tensor_tensor(pmr, mT, pm[:, 0], ALU.subtract)
            dve.drain()
            dve.tensor_copy(pm[:, 1], pmr)
            dve.drain()
            dve.tensor_tensor(pm[:, 2], pmr, pm[:, 1], ALU.subtract).then_inc(pm_b.sem, 1)
            s_at = 0
            for n, u in enumerate(SEQ):
                if n % 4 == 0:
                    yield 17 + n // 4
                if u[0] == "S":
                    _, g, kb, h0, hh = u
                    w = S - kb * P
                    pss_b.wait(dve, i, s_at)
                    if s_at >= 2:
                        ex_b.wait(dve, i, s_at - 2)
                    for x in range(hh):
                        ins = dve.scalar_tensor_tensor(out=sbi[:, s_at % 2, x * w:(x + 1) * w], in0=dist[:, 0:w], scalar=-SLOPES[g * REP + h0 + x],
                                                       in1=pb[:, n % 3, x * w:(x + 1) * w], op0=ALU.mult, op1=ALU.add)
                    ins.then_inc(bank_b.sem, 1)
                    s_at += 1
                else:
                    g = u[1]
                    pst_b.wait(dve, i, g)
                    src = pb[:, n % 3, :].rearrange("p (k h e) -> p k h e", k=NT, h=REP)
                    dve.reciprocal(rco[:].rearrange("p (k h) -> p k h", k=NT), src[:, :, :, HD])
                    dve.drain()
                    ins = dve.tensor_tensor(xnb[:, :, g * REP * HD:(g + 1) * REP * HD].rearrange("p k (h e) -> p k h e", e=HD), src[:, :, :, 0:HD],
                                            rco[:].rearrange("p (k h) -> p k h", k=NT).unsqueeze(3).to_broadcast([P, NT, REP, HD]), ALU.mult)
                    ins.then_inc(bank_b.sem, 1)
            dve.drain().then_inc(on_b.sem, 1)

        def dve_B_tail(dve, i):
            yield 29.5
            xh_b.wait(dve, i, 1)
            dve.tensor_tensor(xTb[:, 1], pb[:, 0:2, :], xTb[:, 0].bitcast(F32), ALU.subtract).then_inc(xl_b.sem, 1)
            yield 30.5
            psg_b.wait(dve, i, 6)

            def product(k):
                return pb[:, 2 + k // 2, (k % 2) * D:(k % 2 + 1) * D]

            norm_stats(dve, i, product, statst, mvt, vart, var_t)
            yield 31
            rstd_t.wait(dve, i)
            for k in range(NT):
                norm_apply(dve, k, zt[:, k], product(k), mvt, rstdt)
            dve.drain().then_inc(z_b.sem, 1)
            xb = X[:, ds(i * NT, NT), :]
            dve.tensor_tensor(xb, xb, zt, ALU.add)
            dve.drain()

        def pool_B(pool, i):
            yield 0
            rsqrt(pool, i, 0, varb, rstdb[:], var_b, rstd_b)

        def pool_B_tail(pool, i):
            yield 30
            rsqrt(pool, i, 0, vart, rstdt[:], var_t, rstd_t)

        QP, KP = [0, 0, 1, 1, 0, 2], [0, 1, 0, 1, 2, 0]

        def sp_B(sp, i):
            yield 3.5
            pc_b.wait(sp, i, 0)
            sp.dma_start(qd.rearrange("z (c p) n -> p z c n", p=P), pq[:]).then_inc(bo_b.sem, 16)
            bo_b.wait(sp, i, 0)
            for r in range(6):
                sp.dma_start(Q6[r * HD:(r + 1) * HD], qd[QP[r]].rearrange("(h d) n -> d h n", d=HD)).then_inc(q6_b.sem, 16)
            pc_b.wait(sp, i, 1)
            sp.dma_start(kd.rearrange("z p n -> p z n"), pk[0:G * HD]).then_inc(bo_b.sem, 16)
            bo_b.wait(sp, i, 1)
            for r in range(6):
                sp.dma_start(K6[r * HD:(r + 1) * HD], kd[KP[r]].rearrange("(g d) n -> d g n", d=HD)).then_inc(k6_b.sem, 16)
            yield 16
            pm_b.wait(sp, i)
            for r in range(3):
                sp.dma_start(Q6[KROWS + r:KROWS + r + 1].rearrange("p h (k q) -> p (h k) q", k=NT), pm[:, r, :]).then_inc(m6_b.sem, 16)

        def pe_S(pe, i):
            yield 1.5
            xn_c.wait(pe, i)
            for c in range(DC):
                for k in range(NT):
                    mm = pe.transpose(pa[:, c, k * P:(k + 1) * P], XN[:, i * NT + k, c * P:(c + 1) * P], ident)
            mm.then_inc(t_c.sem, 1)
            yield 3
            xh_c.wait(pe, i)
            xl_c.wait(pe, i)
            if i == 0:
                z_a.wait(pe, B - 1)
                pe.wait_ge(rt_lo, 1)
            else:
                z_s.wait(pe, i - 1)
            for c in range(DC):
                mm = split3(pe, pa[:, 2, :], [rt[:, s, c, :] for s in range(2)], [xT[:, s, c, :] for s in range(2)], c == 0, c == 1)
            mm.then_inc(lg_c.sem, 1)
            yield 4
            lgc_c.wait(pe, i)
            for k in range(NT):
                mm = pe.transpose(pa[:, 3, k * P:(k + 1) * P], lgT[:, k * P:(k + 1) * P], ident)
            mm.then_inc(lgt_c.sem, 1)
            yield 5
            if i == 0:
                pe.wait_ge(s_lo, 3)
            L_c.wait(pe, i)
            yield from pe_ffn(pe, B + i, 5)

        def act_S(act, i):
            yield 1.5
            t_c.wait(act, i)
            act.activation(xT[:, 0], pa[:, 0:2, :], ACT.Copy).then_inc(xh_c.sem, 1)
            yield 3
            lg_c.wait(act, i)
            act.activation(lgT, pa[:, 2, :], ACT.Copy).then_inc(lgc_c.sem, 1)
            yield 5
            yield from act_ffn(act, B + i, 5)
            yield 14
            dn_a.wait(act, B + i, FC - 1)
            act.activation(SH[:, i * NT:(i + 1) * NT, :], pa[:, 2:4, :].rearrange("p b (k d) -> p (b k) d", d=D), ACT.Copy).then_inc(z_s.sem, 1)

        def dve_S(dve, i):
            yield 0
            norm_stats(dve, i, lambda k: X[:, i * NT + k, :], c_stats, c_mv, c_var, var_c)
            yield 1
            rstd_c.wait(dve, i)
            for k in range(NT):
                norm_apply(dve, k, XN[:, i * NT + k, 0:D], X[:, i * NT + k, :], c_mv, c_rstd)
            dve.drain().then_inc(xn_c.sem, 1)
            yield 2
            xh_c.wait(dve, i)
            dve.tensor_tensor(xT[:, 1], pa[:, 0:2, :], xT[:, 0].bitcast(F32), ALU.subtract).then_inc(xl_c.sem, 1)
            yield 4.5
            lgt_c.wait(dve, i)
            dve.tensor_copy(L[:, i * NT:(i + 1) * NT, :], pa[:, 3, :].rearrange("p (k e) -> p k e", k=NT)[:, :, 0:E]).then_inc(L_c.sem, 1)
            yield 5
            yield from dve_ffn(dve, B + i, 5)

        def pool_S(pool, i):
            yield 0
            rsqrt(pool, i, 0, c_var, c_rstd[:], var_c, rstd_c)
            yield from pool_ffn(pool, B + i, 5)

        def act_W(act):
            for n in range(3):
                yield n
                act.wait_ge(s_in[n], 16)
                act.activation(SHARED[n][0], SHARED_RAW[n], ACT.Copy).then_inc(s_hi, 1)

        def dve_W(dve):
            for n in range(3):
                yield n
                dve.wait_ge(s_hi, n + 1)
                dve.tensor_tensor(SHARED[n][1], SHARED_RAW[n], SHARED[n][0].bitcast(F32), ALU.subtract).then_inc(s_lo, 1)

        def act_route(act):
            yield 0
            act.wait_ge(chosen, 1)
            act.activation(r16[5][:], r16[4][:], ACT.Exp).then_inc(exped, 1)

        def pe_route(pe):
            yield 0
            pe.wait_ge(chosen, 1)
            both = R[7][:].rearrange("p t e -> p (t e)")
            pe.matmul(pb[:, 2, 0:TILES * E], upper, both, start=True, stop=True)
            pe.matmul(pb[:, 3, 0:TILES * E], ones[:], both, start=True, stop=True).then_inc(counted, 1)

        def pool_scatter(pool):
            for n in range(TILES):
                if n % 2 == 0:
                    yield n // 2
                for k in range(2):
                    pool.indirect_dma_start(xs, bass.IndirectOffsetOnAxis(ap=idx[:, k, n:n + 1], axis=0), XN[:, n, :], None).then_inc(ysc[k].sem, 16)

        def over_experts(a):
            return a.unsqueeze(2).to_broadcast([P, TILES, E])

        def over_tiles(a):
            return a.unsqueeze(1).to_broadcast([P, TILES, E])

        def dve_route(dve):
            def choose(logits, best, equal, key, kbest, mask):
                dve.tensor_reduce(best[:], logits[:], AX, ALU.max)
                dve.drain()
                dve.tensor_tensor(equal[:], logits[:], over_experts(best[:]), ALU.is_equal)
                dve.drain()
                dve.tensor_tensor(key[:], equal[:], over_tiles(ehigh), ALU.mult)
                dve.drain()
                dve.tensor_reduce(kbest[:], key[:], AX, ALU.max)
                dve.drain()
                dve.tensor_tensor(mask[:], key[:], over_experts(kbest[:]), ALU.is_equal)
                dve.drain()

            yield 0
            dve.memset(ones[:], 1.0)
            M1, M2, both = R[2], R[6], R[7]
            choose(L, r16[0], R[0], R[1], r16[1], M1)
            dve.scalar_tensor_tensor(out=R[3][:], in0=M1[:], scalar=-3.0e38, in1=L[:], op0=ALU.mult, op1=ALU.add)
            dve.drain()
            choose(R[3], r16[2], R[4], R[5], r16[3], M2)
            dve.tensor_tensor(r16[4][:], r16[2][:], r16[0][:], ALU.subtract)
            dve.tensor_tensor(both[:], M1[:], M2[:], ALU.add)
            dve.tensor_scalar(XN[:, :, D + 1], r16[1][:], -1.0, float(E), ALU.mult, ALU.add)
            dve.tensor_copy(XN[:, :, D], tok2)
            dve.drain().then_inc(chosen, 1)
            dve.wait_ge(exped, 1)
            dve.tensor_scalar(r16[6][:], r16[5][:], 1.0, None, ALU.add)
            dve.drain()
            dve.reciprocal(r16[7][:], r16[6][:])
            dve.drain()
            dve.tensor_copy(XN[:, :, D + 2], r16[7][:])
            dve.tensor_tensor(XN[:, :, D + 3], r16[5][:], r16[7][:], ALU.mult)
            yield 1
            dve.wait_ge(counted, 1)
            total, inc = R[8], R[10]
            dve.tensor_copy(total[:], pb[:, 3, 0:TILES * E].rearrange("p (t e) -> p t e", e=E))
            dve.drain()
            src = total
            for n, dst in enumerate((R[9], R[10], R[11], R[10])):
                w = 1 << n
                dve.tensor_tensor(dst[:, w:], src[:, w:], src[:, :TILES - w], ALU.add)
                dve.tensor_copy(dst[:, 0:w], src[:, 0:w])
                dve.drain()
                src = dst
            yield 2
            dve.tensor_scalar(r8[0][:], inc[:, TILES - 1, :], float(P - 1), None, ALU.add)
            dve.drain()
            dve.tensor_copy(i8[0][:], r8[0][:])
            dve.drain()
            dve.tensor_scalar(i8[1][:], i8[0][:], 7, None, ALU.logical_shift_right)
            dve.drain()
            dve.tensor_copy(r8[1][:], i8[1][:])
            dve.drain()
            src = r8[1]
            for n, dst in enumerate((r8[2], r8[3], r8[4])):
                w = 1 << n
                dve.tensor_tensor(dst[:, w:], src[:, w:], src[:, :E - w], ALU.add)
                dve.tensor_copy(dst[:, 0:w], src[:, 0:w])
                dve.drain()
                src = dst
            end = r8[4]
            dve.tensor_tensor(r8[5][:], end[:], r8[1][:], ALU.subtract)
            dve.tensor_tensor(R[12][:], inc[:], total[:], ALU.subtract)
            dve.tensor_tensor(teC[:], tile_no.unsqueeze(2).to_broadcast([P, MT, E]), end[:].unsqueeze(1).to_broadcast([P, MT, E]), ALU.is_ge)
            dve.drain()
            yield 3
            dve.tensor_reduce(teF[0][:], teC[:], AX, ALU.add)
            dve.tensor_scalar(r8[6][:], r8[5][:], float(P), None, ALU.mult)
            dve.tensor_tensor(R[13][:], R[12][:], pb[:, 2, 0:TILES * E].rearrange("p (t e) -> p t e", e=E), ALU.add)
            dve.drain()
            dve.tensor_scalar(teF[1][:], teF[0][:], float(E - 1), None, ALU.min)
            dve.tensor_tensor(R[11][:], R[13][:], over_tiles(r8[6][:]), ALU.add)
            dve.drain()
            dve.tensor_copy(teI[:], teF[1][:])
            for k, m in enumerate((M1, M2)):
                dve.tensor_tensor(R[k][:], R[11][:], m[:], ALU.mult)
            dve.drain()
            for k in range(2):
                dve.tensor_reduce(r16[4 * k][:] if k == 0 else r16[3][:], R[k][:], AX, ALU.add)
            dve.drain()
            dve.tensor_copy(idx[:, 0, :], r16[0][:])
            dve.tensor_copy(idx[:, 1, :], r16[3][:])
            dve.drain().then_inc(slots, 1)
        def before(n, k=1):
            for _ in range(k):
                n = (n[0], 0) if n[1] else (n[0] - 1, 1)
            return n

        def after(n):
            return (n[0] + 1, 0) if n[1] else (n[0], 1)

        def expert_of(pe, n):
            return pe.value_load(teI[0:1, ds(2 * n[0] + n[1], 1)], min_val=0, max_val=E - 1)

        def pe_slot_rows(pe, n, bank_new=False):
            m, x = n
            xt_in[x].wait(pe, m)
            if not bank_new:
                y_d.wait(pe, m - 2, x)
            for c in range(DC):
                mm = pe.transpose(pb[:, x, c * P:(c + 1) * P], xt[:, x, c * P:(c + 1) * P], ident)
            mm.then_inc(tx_d.sem, 1)

        def pe_step(pe, n, up, down, rows=False, w2_new=False):
            m, x = n
            m1, x1 = before(n)

            def w1(u):
                for c in range(DC):
                    mm = pe.matmul(pa[:, 2 * x + u, :], xtT[:, x, c, :], ew1[:, ds(te, 1), c, u * INTER:(u + 1) * INTER].rearrange("p a n -> p (a n)"),
                                   start=c == 0, stop=c == 1)
                mm.then_inc(w1_d.sem, 1)

            if up:
                te = expert_of(pe, n)
                xT_d.wait(pe, m, x)
                h_d.wait(pe, m - 1, x)
                w1(0)
            if down:
                te1 = expert_of(pe, (m1, x1))
                h_d.wait(pe, m1, x1)
                hT_d.wait(pe, m1 - 1, x1)
                for q in range(INTER // P):
                    mm = pe.transpose(pb[:, 2 + x1, q * P:(q + 1) * P], e_h[:, x1, q * P:(q + 1) * P], ident)
                mm.then_inc(th_d.sem, 1)
            if up:
                w1(1)
            if down:
                hT_d.wait(pe, m1, x1)
                if rows:
                    xT_d.wait(pe, *after(n))
                if w2_new:
                    pe.wait_ge(ew_in[1], 16)
                for q in range(INTER // P):
                    mm = pe.matmul(pb[:, x1, D:2 * D], e_hT[:, x1, q, :], ew2[:, ds(te1, 1), q, :].rearrange("p a n -> p (a n)"), start=q == 0, stop=q == INTER // P - 1)
                mm.then_inc(w2_d.sem, 1)

        def pe_experts(pe, n, first=False, last=False, second=False):
            if first:
                pe_slot_rows(pe, n, True)
            if not last:
                pe_slot_rows(pe, after(n), first)
            pe_step(pe, n, True, not first, not last, second)
            if last:
                pe_step(pe, after(n), False, True)

        def act_experts(act, n, first=False, last=False, second=False):
            def rows(n):
                m, x = n
                tx_d.wait(act, m, x)
                w1_d.wait(act, m - 1, 2 * x + 1)
                act.activation(xtT[:, x], pb[:, x, 0:D].rearrange("p (c n) -> p c n", c=DC), ACT.Copy).then_inc(xT_d.sem, 1)

            def result(n):
                m, x = n
                w2_d.wait(act, m, x)
                ysc[x].wait(act, m - 1)
                row_d.wait(act, m, x)
                act.activation(e_y[:, x], pb[:, x, D:2 * D], ACT.Copy, scale=e_weight[:, x:x + 1]).then_inc(y_d.sem, 1)

            if first:
                rows(n)
            if not last:
                rows(after(n))
            m, x = n
            w1_d.wait(act, m, 2 * x)
            act.activation(e_s[:, x], pa[:, 2 * x, :], ACT.Silu).then_inc(s_d.sem, 1)
            if not first:
                result(before(n))
            if last:
                result(n)

        def dve_experts(dve, n, first=False, last=False, second=False):
            def number(n):
                m, x = n
                xt_in[x].wait(dve, m)
                second, first_w, weight = (e_pick[:, x, c:c + 1] for c in range(3))
                te = teF[1][:, ds(2 * m + x, 1)]
                dve.tensor_scalar(second, xt[:, x, D + 1:D + 2], te, None, ALU.not_equal)
                dve.tensor_scalar(e_number[:, x:x + 1], xt[:, x, D + 1:D + 2], te, xt[:, x, D:D + 1], ALU.not_equal, ALU.add)
                dve.tensor_scalar(first_w, xt[:, x, D + 1:D + 2], te, xt[:, x, D + 2:D + 3], ALU.is_equal, ALU.mult)
                dve.drain()
                dve.tensor_scalar(weight, xt[:, x, D + 3:D + 4], second, first_w, ALU.mult, ALU.add).then_inc(number_d.sem, 1)

            def hidden_T(n):
                m, x = n
                th_d.wait(dve, m, x)
                dve.tensor_copy(e_hT[:, x], pb[:, 2 + x, :].rearrange("p (q n) -> p q n", n=P)).then_inc(hT_d.sem, 1)

            def row(n):
                m, x = n
                dve.drain()
                ysc[x].wait(dve, m - 1)
                y_d.wait(dve, m - 1, x)
                dve.tensor_copy(e_weight[:, x:x + 1], e_pick[:, x, 2:3])
                dve.tensor_copy(e_row[:, x:x + 1], e_number[:, x:x + 1])
                dve.drain().then_inc(row_d.sem, 1)
                dve.drain()

            m, x = n
            if first:
                number(n)
            else:
                row(before(n))
            if not last:
                number(after(n))
            if not first:
                hidden_T(before(n))
            w1_d.wait(dve, m, 2 * x + 1)
            s_d.wait(dve, m, x)
            dve.tensor_tensor(e_h[:, x], e_s[:, x], pa[:, 2 * x + 1, :], ALU.mult).then_inc(h_d.sem, 1)
            if last:
                row(n)
                hidden_T(n)

        def pool_experts(pool, n, first=False, last=False, second=False):
            def scatter(n):
                m, x = n
                row_d.wait(pool, m, x)
                y_d.wait(pool, m, x)
                pool.sem_inc(turns, 1)
                pool.indirect_dma_start(ys, bass.IndirectOffsetOnAxis(ap=e_row[:, x:x + 1], axis=0), e_y[:, x, :], None).then_inc(ysc[x].sem, 16)

            if not first:
                scatter(before(n))
            if last:
                scatter(n)

        def sp_experts(sp, n):
            m, x = n
            tx_d.wait(sp, m - 1, x)
            number_d.wait(sp, m - 1, x)
            sp.dma_start(xt[:, x, :], xs[ds((2 * m + x) * P, P), :]).then_inc(xt_in[x].sem, 16)

        def all_slot_tiles(engine, steps):
            steps(engine, (0, 0), first=True)
            steps(engine, (0, 1), second=True)
            steps(engine, (1, 0))
            with engine.Fori(1, (MT - 2) // 2) as m:
                steps(engine, (m, 1))
                steps(engine, (m + 1, 0))
            steps(engine, ((MT - 2) // 2, 1))
            steps(engine, (MT // 2, 0), last=True)

        def pool_result(pool):
            for i in range(B + 1):
                if i < B:
                    pool.wait_ge(yb_in[i], 16)
                    pool.tensor_tensor(zc[:, i], yb[:, i, :, 0], yb[:, i, :, 1], ALU.add).then_inc(y_sum, 1)
                if i >= 1:
                    rsqrt(pool, i - 1, 0, e_norm[i - 1][2], e_rstd[:, i - 1], var_e, rstd_e)

        def dve_result(dve):
            for i in range(B + 2):
                if i < B:
                    z = zc[:, i]
                    dve.wait_ge(y_sum, i + 1)
                    dve.tensor_tensor(z, z, SH[:, i * NT:(i + 1) * NT, :], ALU.add)
                    dve.drain()
                    norm_stats(dve, i, lambda k: zc[:, i, k], *e_norm[i], var_e)
                if 1 <= i <= B:
                    rstd_e.wait(dve, i - 1)
                    dve.scalar_tensor_tensor(out=e_shift[:, i - 1], in0=e_norm[i - 1][1][:, :, 0], scalar=-1.0, in1=e_rstd[:, i - 1],
                                             op0=ALU.mult, op1=ALU.mult).then_inc(shifts, 1)
                if i >= 2:
                    dve.wait_ge(normed, i - 1)
                    xb = X[:, (i - 2) * NT:(i - 1) * NT, :]
                    dve.tensor_tensor(xb, xb, zc[:, i - 2], ALU.add).then_inc(result, 1)

        def act_result(act):
            for i in range(B + 1):
                if i < B:
                    act.wait_ge(shifts, i + 1)
                    for k in range(NT):
                        act.activation(zc[:, i, k], zc[:, i, k], ACT.Identity, bias=e_shift[:, i, k:k + 1], scale=e_rstd[:, i, k:k + 1])
                    act.drain().then_inc(normed, 1)
                if i >= 1:
                    b = i - 1
                    act.wait_ge(result, b + 1)
                    act.dma_start(out[b * S:(b + 1) * S, :].rearrange("(t p) d -> p t d", p=P), X[:, b * NT:(b + 1) * NT, :]).then_inc(out_sem, 16)

        block = ctx.enter_context(nc.Block())

        def done(eng, flag):
            eng.drain().then_inc(flag, 1)

        SHARED = [[w_up[:, s, u].rearrange("p c n -> p (c n)") for s in range(2)] for u in range(2)] + \
                 [[w_dn[:, s].rearrange("p c n -> p (c n)") for s in range(2)]]
        SHARED_RAW = [up_raw[:, 1, u].rearrange("p c n -> p (c n)") for u in range(2)] + [dn_raw[:, 1].rearrange("p c n -> p (c n)")]

        x_tiles = t["x"].rearrange("(t p) d -> p t d", p=P)

        def act_start(act):
            for n in range(4):
                yield n
                act.wait_ge(raw_in[n], 16)
                act.activation(HI_LO[n][0], staged[n][:], ACT.Copy).then_inc(split_hi, 1)
            yield 6
            for q in range(2):
                act.wait_ge(hadd, q + 1)
                act.activation(w_dn[:, 0, 4 * q:4 * q + 4].rearrange("p a d -> p (a d)"), pb[:, 2 * q:2 * q + 2, :], ACT.Copy, scale=1 / 32).then_inc(hadh, 1)
            yield 7
            act.wait_ge(r_in, 16)
            act.activation(rt[:, 0], rt_raw[:, 1], ACT.Copy).then_inc(rt_hi, 1)

        def dve_start(dve):
            for n in range(4):
                yield n
                dve.wait_ge(split_hi, n + 1)
                dve.tensor_tensor(HI_LO[n][1], staged[n][:], HI_LO[n][0].bitcast(F32), ALU.subtract).then_inc(split_lo, 1)
            for st in range(3):
                yield 4 + st // 2
                if st == 0:
                    dve.wait_ge(raw_in[4], 16)
                src, dst = (spare, staged[4]) if st == 1 else (staged[4], spare)
                a = src[:].rearrange("p (x two y) -> p x two y", two=2, y=D << st)
                b = dst[:].rearrange("p (x two y) -> p x two y", two=2, y=D << st)
                dve.tensor_tensor(b[:, :, 0], a[:, :, 0], a[:, :, 1], ALU.add)
                dve.tensor_tensor(b[:, :, 1], a[:, :, 0], a[:, :, 1], ALU.subtract)
                dve.drain()
            dve.drain().then_inc(bfly, 1)
            yield 6
            for q in range(2):
                dve.wait_ge(hadh, q + 1)
                dve.scalar_tensor_tensor(out=w_dn[:, 1, 4 * q:4 * q + 4].rearrange("p a d -> p (a d)"), in0=pb[:, 2 * q:2 * q + 2, :].rearrange("p a d -> p (a d)"),
                                         scalar=1 / 32, in1=w_dn[:, 0, 4 * q:4 * q + 4].rearrange("p a d -> p (a d)").bitcast(F32),
                                         op0=ALU.mult, op1=ALU.subtract).then_inc(split_lo, 1)
            yield 7
            dve.wait_ge(rt_hi, 1)
            dve.tensor_tensor(rt[:, 1], rt_raw[:, 1], rt[:, 0].bitcast(F32), ALU.subtract).then_inc(rt_lo, 1)
            dve.wait_ge(t_in, 16)
            dve.tensor_copy(pad_row[:, :, D], table[:, 64:66]).then_inc(pad_set, 1)
            dve.drain()
            dve.memset(K6[KROWS:P, :, :], 1.0)
            dve.memset(V1[:], 0.0)
            dve.memset(mxn[:], 0.0)
            dve.drain()
            dve.memset(V1[:, :, :, HD:HD + 1], 1.0)
            dve.drain()

        def pe_start(pe):
            yield 6
            pe.wait_ge(bfly, 1)
            for q in range(4):
                mm = pe.matmul(pb[:, q, :], had, spare[:, q * 512:(q + 1) * 512], start=True, stop=True)
                if q % 2:
                    mm.then_inc(hadd, 1)

        @block.sync
        def _(sp):
            sp.dma_start(const[:], t["const"]).then_inc(c_in, 16)
            for n, r in enumerate(staged):
                sp.dma_start(r[:], t[f"raw{n}"]).then_inc(raw_in[n], 16)
            for e in (bo_b, q6_b, k6_b, m6_b):
                e.open(sp)
            sp.dma_start(table[:], t["table"]).then_inc(t_in, 16)
            sp.dma_start(rt_raw[:, 1].rearrange("p c n -> p (c n)"), t["router"]).then_inc(r_in, 16)
            sp.dma_start(X[:, NT:TILES], x_tiles[:, NT:TILES]).then_inc(x_in[1], 16)
            sp.wait_ge(pad_set, 1)
            for x in range(2):
                sp.dma_start(xs.rearrange("(t p) r -> p t r", p=P)[:, x::2], pad_row[:, x].unsqueeze(1).to_broadcast([P, (MT + 1 - x) // 2, ROW])).then_inc(pad_out, 16)
            with sp.Fori(0, B - 1) as i:
                in_order(ALONE_B, b=sp_B(sp, i))
            dn_a.wait(sp, B - 1, FC - 1)
            for n in range(3):
                sp.dma_start(SHARED_RAW[n], t[f"shared{n}"]).then_inc(s_in[n], 16)
            in_order(ALONE_B, b=sp_B(sp, B - 1))
            for n in range(4):
                sp.wait_ge(b_done[n], 1)
            sp.dma_start(ew1[:].rearrange("p e c n -> p (e c n)"), t["expert1"]).then_inc(ew_in[0], 16)
            for e in xt_in:
                e.open(sp)
            dn_a.wait(sp, 2 * B - 1, FC - 1)
            for k in range(2):
                sp.wait_ge(ysc[k].sem, 16 * TILES)
            for x in range(2):
                sp_experts(sp, (0, x))
            sp.dma_start(ew2[:].rearrange("p e c n -> p (e c n)"), t["expert2"]).then_inc(ew_in[1], 16)
            with sp.Fori(1, MT // 2) as m:
                for x in range(2):
                    sp_experts(sp, (m, x))
            sp_experts(sp, (MT // 2, 0))
            for x in range(2):
                ysc[x].wait(sp, (MT - 1 - x) // 2)
            for i in range(B):
                sp.dma_start(yb[:, i], ys[i * 2 * S:(i + 1) * 2 * S, :].rearrange("(t p k) d -> p t k d", p=P, k=2)).then_inc(yb_in[i], 16)

        @block.scalar
        def _(act):
            act.dma_start(X[:, 0:NT], x_tiles[:, 0:NT]).then_inc(x_in[0], 16)
            act.dma_start(bias[:], t["b_proj"].unsqueeze(0).to_broadcast([P, D])).then_inc(b_in, 16)
            for e in (xh_a, q_a, kv_a, th_a, hh_a, xh_b, qh_b, kh_b, ex_b, ot_b, xh_c, lgc_c, z_s, xT_d, s_d, y_d):
                e.open(act)
            in_order(START, a=act_A(act, 0), h=act_start(act))
            act.wait_ge(pad_out, 32)
            in_order(FIRST, a=act_A(act, 1), b=act_B(act, 0))
            with act.Fori(1, B - 1) as i:
                in_order(TOGETHER, c=act_B_tail(act, i - 1), a=act_A(act, i + 1), b=act_B(act, i))
            third_S, last_S = Steps(act_S(act, B - 2)), Steps(act_S(act, B - 1))
            in_order(LAST, c=act_B_tail(act, B - 2), b=act_B(act, B - 1), s=act_S(act, 0), t=act_S(act, 1), u=third_S, w=act_W(act))
            in_order(TAIL, c=act_B_tail(act, B - 1), u=third_S, s=last_S)
            done(act, b_done[1])
            in_order(S_FFN, s=last_S, g=act_route(act))
            all_slot_tiles(act, act_experts)
            act_result(act)
            act.wait_ge(out_sem, 16 * B)

        @block.vector
        def _(dve):
            dve.memset(mhalf[:], -0.5)
            dve.memset(vsb[:, :, :, P:P + 1], 1.0)
            dve.memset(pad_row, 0.0)
            dve.drain().then_inc(setup, 1)
            dve.wait_ge(c_in, 16)
            dve.tensor_copy(identb[:], ident)
            dve.tensor_copy(maskb[:], noncausal)
            dve.drain().then_inc(setup, 1)
            for e in (var_a, xn_a, xl_a, vk_a, o_a, y_a, h_a, z_a, var_b, var_t, xn_b, xl_b, pc_b, v_b, mx_b, pm_b, bank_b, on_b, z_b, var_c, xn_c, xl_c, L_c, h_d, hT_d, row_d, number_d, var_e):
                e.open(dve)
            in_order(START, a=dve_A(dve, 0), h=dve_start(dve))
            dve.wait_ge(x_in[1], 16)
            in_order(FIRST, a=dve_A(dve, 1), b=dve_B(dve, 0))
            with dve.Fori(1, B - 1) as i:
                in_order(TOGETHER, c=dve_B_tail(dve, i - 1), a=dve_A(dve, i + 1), b=dve_B(dve, i))
            third_S, last_S = Steps(dve_S(dve, B - 2)), Steps(dve_S(dve, B - 1))
            in_order(LAST, c=dve_B_tail(dve, B - 2), b=dve_B(dve, B - 1), s=dve_S(dve, 0), t=dve_S(dve, 1), u=third_S, w=dve_W(dve))
            in_order(TAIL, c=dve_B_tail(dve, B - 1), u=third_S, s=last_S)
            done(dve, b_done[2])
            in_order(S_FFN, s=last_S, g=dve_route(dve))
            all_slot_tiles(dve, dve_experts)
            dve_result(dve)

        @block.gpsimd
        def _(pool):
            pool.wait_ge(setup, 1)
            for e in (rstd_a, hl_a, rstd_b, rstd_t, rstd_c, rstd_e):
                e.open(pool)
            in_order(START, a=pool_A(pool, 0))
            in_order(FIRST, a=pool_A(pool, 1), b=pool_B(pool, 0))
            with pool.Fori(1, B - 1) as i:
                in_order(TOGETHER, c=pool_B_tail(pool, i - 1), a=pool_A(pool, i + 1), b=pool_B(pool, i))
            third_S, last_S = Steps(pool_S(pool, B - 2)), Steps(pool_S(pool, B - 1))
            in_order(LAST, c=pool_B_tail(pool, B - 2), b=pool_B(pool, B - 1), s=pool_S(pool, 0), t=pool_S(pool, 1), u=third_S)
            in_order(TAIL, c=pool_B_tail(pool, B - 1), u=third_S, s=last_S)
            done(pool, b_done[3])
            pool.wait_ge(pad_out, 32)
            pool.wait_ge(slots, 1)
            in_order(S_FFN, s=last_S, r=pool_scatter(pool))
            all_slot_tiles(pool, pool_experts)
            pool_result(pool)

        @block.tensor
        def _(pe):
            pe.wait_ge(setup, 2)
            pe.wait_ge(c_in, 16)
            for e in (ps_a, ps_f, dn_a, psg_b, psm_b, pss_b, pv_b, pso_b, pst_b, t_c, lg_c, lgt_c, tx_d, w1_d, th_d, w2_d):
                e.open(pe)
            in_order(START, a=pe_A(pe, 0), h=pe_start(pe))
            in_order(FIRST, a=pe_A(pe, 1), b=pe_B(pe, 0))
            with pe.Fori(1, B - 1) as i:
                in_order(TOGETHER, c=pe_B_tail(pe, i - 1), a=pe_A(pe, i + 1), b=pe_B(pe, i))
            third_S, last_S = Steps(pe_S(pe, B - 2)), Steps(pe_S(pe, B - 1))
            in_order(LAST, c=pe_B_tail(pe, B - 2), b=pe_B(pe, B - 1), s=pe_S(pe, 0), t=pe_S(pe, 1), u=third_S)
            in_order(TAIL, c=pe_B_tail(pe, B - 1), u=third_S, s=last_S)
            done(pe, b_done[0])
            in_order(S_FFN, s=last_S, g=pe_route(pe))
            pe.wait_ge(ew_in[0], 16)
            pe.wait_ge(slots, 1)
            all_slot_tiles(pe, pe_experts)


def constants():
    import numpy as np
    c = np.zeros((P, 1156), np.float32)
    i = np.arange(P)
    c[:, 0:128] = np.eye(P)
    had = np.array([[1.0]])
    while had.shape[0] < P:
        had = np.block([[had, had], [had, -had]])
    c[:, 128:256] = had
    c[:, 256:384] = i[:, None] // LD == i[None, :] // LD
    c[:, 384:512] = i[:, None] < i[None, :]
    d = np.arange(512)[None, :] - i[:, None]
    c[:, 512:1024] = np.where(d >= 0, np.sqrt(np.maximum(d, 0).astype(np.float32)), 1e30)
    c[:, 1024:1028] = i[:, None] // LD == np.arange(4)[None, :]
    c[:, 1028:1156] = np.where(i[None, :] > i[:, None], NEG, 0)
    return c


def tables():
    import numpy as np
    c = np.zeros((P, 72), np.float32)
    i = np.arange(P)
    c[:, 0:TILES] = 2 * (np.arange(TILES)[None, :] * P + i[:, None])
    c[:, 16:24] = E - np.arange(E)
    c[:, 24:24 + MT] = np.arange(MT)
    c[:, 64:66] = 2 * (TILES + np.arange(2)[None, :]) * P + 2 * i[:, None]
    return c


def layout(inputs):
    import numpy as np

    def kt(w):
        w = np.asarray(w)
        k, n = w.shape
        return w.reshape(k // P, P, n).transpose(1, 0, 2).reshape(P, -1)

    g = {k: np.asarray(v) for k, v in inputs.items()}
    kv = np.concatenate([g["L1_attn_Wk"].T, g["L1_attn_Wv"].T], 1)
    return {
        "x": g["L0_attn_x"].reshape(B * S, D),
        "b_proj": g["L0_attn_b_proj"],
        "raw0": kt(g["L0_attn_w_qkv"].T),
        "raw1": np.concatenate([kt(g["L0_attn_w_proj"].T), kt(g["L1_attn_Wq"].T), kt(kv), kt(g["L1_attn_Wo"].T)], 1),
        "raw2": kt(g["L0_ffn_W1"].T),
        "raw3": kt(g["L0_ffn_W3"].T),
        "raw4": kt(g["L0_ffn_W2"].T),
        "const": constants(),
        "table": tables(),
        "router": kt(np.pad(g["L1_ffn_router_w"], ((0, 0), (0, P - E)))),
        "shared0": kt(g["L1_ffn_w_gate"]),
        "shared1": kt(g["L1_ffn_w_up"]),
        "shared2": kt(g["L1_ffn_w_down"]),
        "expert1": np.concatenate([kt(w) for w in g["L1_ffn_w1"]], 1),
        "expert2": np.concatenate([kt(w) for w in g["L1_ffn_w2"]], 1),
    }


def kernel(**inputs):
    import numpy as np
    import concourse.bacc as bacc
    from concourse.bass_utils import run_bass_kernel_spmd

    nc = bacc.Bacc("TRN2", target_bir_lowering=False, num_devices=1)
    arrays = {f"in_{k}": np.ascontiguousarray(v) for k, v in layout(inputs).items()}
    t = {k[3:]: nc.dram_tensor(k, v.shape, mybir.dt.from_np(v.dtype), kind="ExternalInput").ap() for k, v in arrays.items()}
    out = nc.dram_tensor("out", (B * S, D), F32, kind="ExternalOutput").ap()
    build(nc, t, out)
    r = run_bass_kernel_spmd(nc, [arrays], core_ids=[0])
    return r.results[0]["out"].reshape(B, S, D)
```
